# Optimizing a Trainium2 kernel written in Bass

```python
import numpy as np
import jax
import jax.numpy as jnp

def _softmax(x, axis=-1):
    return jax.nn.softmax(x, axis=axis)

def _gelu(x):
    return jax.nn.gelu(x, approximate=True)

def _silu(x):
    return jax.nn.silu(x)

def _sigmoid(x):
    return jax.nn.sigmoid(x)

def _layernorm(x, axis=-1, eps=1e-05):
    m = jnp.mean(x, axis=axis, keepdims=True)
    v = jnp.var(x, axis=axis, keepdims=True)
    return (x - m) / jnp.sqrt(v + eps)

def _scatter_add(tgt, idx, src, axis=0):
    return tgt.at[idx].add(src)

def _segment_sum(src, seg, n):
    return jax.ops.segment_sum(src, seg, n)
kernel_name = 'mk_conv_seq_d2_conv_nhwc256_r4_d6868b'

def setup_inputs(seed: int=0):
    np.random.seed(seed)
    _w = jnp.asarray

    def _rec_inputs():
        import jax
        import jax.numpy as jnp
        _gk = jax.random.key(seed)
        x = -0.0003929 + 0.9999 * jax.random.normal(jax.random.fold_in(_gk, 1), (1, 64, 64, 64), jnp.float32)
        return x
    x = _rec_inputs()

    def _L0_conv_setup():
        import jax, jax.numpy as jnp
        import numpy as np
        DIM, IDIM, HEADS = (64, 16, 4)
        B, I, J = (1, 64, 64)
        EPS = 1e-05

        def _sinu(seq, rot):
            inv = 1.0 / 10000.0 ** (np.arange(0, rot, 2, dtype=np.float64) / rot)
            f = np.arange(seq, dtype=np.float64)[:, None] * inv[None, :]
            f = np.repeat(f, 2, axis=-1)
            return (jnp.asarray(np.sin(f)[None], dtype=jnp.float32), jnp.asarray(np.cos(f)[None], dtype=jnp.float32))

        def _ln(x, g, b):
            mu = jnp.mean(x, axis=-1, keepdims=True)
            var = jnp.mean((x - mu) ** 2, axis=-1, keepdims=True)
            return (x - mu) / jnp.sqrt(var + EPS) * g + b

        def _rotate_every_two(x):
            x1, x2 = (x[..., ::2], x[..., 1::2])
            return jnp.stack((-x2, x1), axis=-1).reshape(x.shape)

        def _rope(x, sin, cos):
            sin, cos = (sin[:, None], cos[:, None])
            rd = sin.shape[-1]
            xr, xp = (x[..., :rd], x[..., rd:])
            xr = xr * cos + _rotate_every_two(xr) * sin
            return jnp.concatenate((xr, xp), axis=-1)

        def _attn(a, sin, cos, ga, ba, gb, bb, Wq, Wkv, Wo, bo):
            an = _ln(a, ga, ba)
            bn = _ln(a, gb, bb)
            q = an @ Wq
            k, v = jnp.split(bn @ Wkv, 2, axis=-1)
            Bn, N = (a.shape[0], a.shape[1])

            def heads(t):
                return t.reshape(Bn, N, HEADS, IDIM).transpose(0, 2, 1, 3)
            q, k, v = (heads(q), heads(k), heads(v))
            q = _rope(q, sin, cos)
            k = _rope(k, sin, cos)
            dots = jnp.einsum('bhid,bhjd->bhij', q, k)
            attn = jax.nn.softmax(dots, axis=-1)
            out = jnp.einsum('bhij,bhjd->bhid', attn, v)
            out = out.transpose(0, 2, 3, 1).reshape(Bn, N, IDIM * HEADS)
            return jax.nn.elu(out @ Wo + bo)
        key = jax.random.key(seed)
        ks = jax.random.split(key, 8)
        w = DIM ** (-0.5)
        sin_i, cos_i = _sinu(J, IDIM)
        sin_j, cos_j = _sinu(I, IDIM)
        return {'x': jax.random.normal(ks[0], (B, I, J, DIM), jnp.float32), 'sin_i': sin_i, 'cos_i': cos_i, 'sin_j': sin_j, 'cos_j': cos_j, 'gia': jnp.ones((DIM,), jnp.float32), 'bia': jnp.zeros((DIM,), jnp.float32), 'gib': jnp.ones((DIM,), jnp.float32), 'bib': jnp.zeros((DIM,), jnp.float32), 'Wq_i': jax.random.normal(ks[1], (DIM, IDIM * HEADS), jnp.float32) * w, 'Wkv_i': jax.random.normal(ks[2], (DIM, 2 * IDIM * HEADS), jnp.float32) * w, 'Wo_i': jax.random.normal(ks[3], (IDIM * HEADS, DIM), jnp.float32) * w, 'bo_i': jnp.zeros((DIM,), jnp.float32), 'gja': jnp.ones((DIM,), jnp.float32), 'bja': jnp.zeros((DIM,), jnp.float32), 'gjb': jnp.ones((DIM,), jnp.float32), 'bjb': jnp.zeros((DIM,), jnp.float32), 'Wq_j': jax.random.normal(ks[4], (DIM, IDIM * HEADS), jnp.float32) * w, 'Wkv_j': jax.random.normal(ks[5], (DIM, 2 * IDIM * HEADS), jnp.float32) * w, 'Wo_j': jax.random.normal(ks[6], (IDIM * HEADS, DIM), jnp.float32) * w, 'bo_j': jnp.zeros((DIM,), jnp.float32)}
    _L0_conv_all = _L0_conv_setup()
    _L0_conv_in = {k: v for k, v in _L0_conv_all.items() if k in ('sin_i', 'cos_i', 'sin_j', 'cos_j', 'gia', 'bia', 'gib', 'bib', 'Wq_i', 'Wkv_i', 'Wo_i', 'bo_i', 'gja', 'bja', 'gjb', 'bjb', 'Wq_j', 'Wkv_j', 'Wo_j', 'bo_j')}
    del _L0_conv_all

    def _L1_conv_setup():
        import jax, jax.numpy as jnp
        import numpy as np
        EMB = 64
        D_INNER = 128
        HEADDIM = 16
        NHEADS = D_INNER // HEADDIM
        DSTATE = 32
        DCONV = 4
        CONV_DIM = D_INNER + 2 * DSTATE
        D_IN_PROJ = 2 * D_INNER + 2 * DSTATE + NHEADS
        LN_EPS = 1e-05

        def _layernorm(x, w, b):
            m = jnp.mean(x, axis=-1, keepdims=True)
            v = jnp.mean((x - m) ** 2, axis=-1, keepdims=True)
            return (x - m) * jax.lax.rsqrt(v + LN_EPS) * w + b

        def _wn_linear(x, g, v, b):
            w = g[:, None] * v / jnp.linalg.norm(v, axis=1, keepdims=True)
            return x @ w.T + b

        def _ssm_scan(x, dt, A, Bm, Cm):
            dA = jnp.exp(dt * A)
            dtx = dt[..., None] * x
            bsz = x.shape[0]

            def step(h, inp):
                dA_t, dtx_t, B_t, C_t = inp
                h = h * dA_t[:, :, None, None] + dtx_t[..., None] * B_t[:, None, None, :]
                y = jnp.einsum('bhpn,bn->bhp', h, C_t)
                return (h, y)
            h0 = jnp.zeros((bsz, NHEADS, HEADDIM, DSTATE), x.dtype)
            xs = (jnp.swapaxes(dA, 0, 1), jnp.swapaxes(dtx, 0, 1), jnp.swapaxes(Bm, 0, 1), jnp.swapaxes(Cm, 0, 1))
            _, ys = jax.lax.scan(step, h0, xs)
            return jnp.swapaxes(ys, 0, 1)

        def _mamba2(u, in_proj_w, conv_w, conv_b, dt_bias, A_log, D_param, ssm_norm_w, out_proj_w):
            B, L, _ = u.shape
            zxbcdt = u @ in_proj_w.T
            z_gate = zxbcdt[..., :D_INNER]
            xBC = zxbcdt[..., D_INNER:D_INNER + CONV_DIM]
            dt = zxbcdt[..., D_INNER + CONV_DIM:]
            xp = jnp.pad(xBC, ((0, 0), (DCONV - 1, 0), (0, 0)))
            xc = jax.lax.conv_general_dilated(jnp.swapaxes(xp, 1, 2), conv_w[:, None, :], (1,), 'VALID', feature_group_count=CONV_DIM, dimension_numbers=('NCH', 'OIH', 'NCH'))
            xc = jax.nn.silu(jnp.swapaxes(xc, 1, 2) + conv_b)
            x = xc[..., :D_INNER].reshape(B, L, NHEADS, HEADDIM)
            Bm = xc[..., D_INNER:D_INNER + DSTATE]
            Cm = xc[..., D_INNER + DSTATE:]
            dt = jax.nn.softplus(dt + dt_bias)
            A = -jnp.exp(A_log)
            y = _ssm_scan(x, dt, A, Bm, Cm) + D_param[None, None, :, None] * x
            y = y.reshape(B, L, D_INNER)
            yg = y * jax.nn.silu(z_gate)
            yn = yg * jax.lax.rsqrt(jnp.mean(yg ** 2, axis=-1, keepdims=True) + LN_EPS) * ssm_norm_w
            return yn @ out_proj_w.T
        key = jax.random.key(seed)
        ks = jax.random.split(key, 12)
        B, NU, NA = (1, 16, 128)

        def rn(k, shape, scale):
            return jax.random.normal(k, shape, dtype=jnp.float32) * scale
        z = rn(ks[0], (B, NU, NA, EMB), 1.0)
        in_proj_w = rn(ks[1], (D_IN_PROJ, EMB), EMB ** (-0.5))
        conv_w = rn(ks[2], (CONV_DIM, DCONV), DCONV ** (-0.5))
        conv_b = rn(ks[3], (CONV_DIM,), 0.02)
        dt_bias = jnp.log(jnp.expm1(jax.random.uniform(ks[4], (NHEADS,), minval=0.001, maxval=0.1)))
        A_log = jnp.log(jax.random.uniform(ks[5], (NHEADS,), minval=1.0, maxval=16.0))
        D_param = jnp.ones((NHEADS,), dtype=jnp.float32)
        ssm_norm_w = jnp.ones((D_INNER,), dtype=jnp.float32)
        out_proj_w = rn(ks[6], (EMB, D_INNER), D_INNER ** (-0.5))
        ff_v = rn(ks[7], (EMB, EMB), EMB ** (-0.5))
        ff_g = jnp.linalg.norm(ff_v, axis=1)
        ff_b = jnp.zeros((EMB,), dtype=jnp.float32)
        fc1_v = rn(ks[8], (EMB, EMB), EMB ** (-0.5))
        fc1_g = jnp.linalg.norm(fc1_v, axis=1)
        fc1_b = jnp.zeros((EMB,), dtype=jnp.float32)
        fc2_v = rn(ks[9], (EMB, EMB), EMB ** (-0.5))
        fc2_g = jnp.linalg.norm(fc2_v, axis=1)
        fc2_b = jnp.zeros((EMB,), dtype=jnp.float32)
        return {'z': z, 'ln1_w': jnp.ones((EMB,), dtype=jnp.float32), 'ln1_b': jnp.zeros((EMB,), dtype=jnp.float32), 'in_proj_w': in_proj_w, 'conv_w': conv_w, 'conv_b': conv_b, 'dt_bias': dt_bias, 'A_log': A_log, 'D_param': D_param, 'ssm_norm_w': ssm_norm_w, 'out_proj_w': out_proj_w, 'ff_g': ff_g, 'ff_v': ff_v, 'ff_b': ff_b, 'ln2_w': jnp.ones((EMB,), dtype=jnp.float32), 'ln2_b': jnp.zeros((EMB,), dtype=jnp.float32), 'fc1_g': fc1_g, 'fc1_v': fc1_v, 'fc1_b': fc1_b, 'fc2_g': fc2_g, 'fc2_v': fc2_v, 'fc2_b': fc2_b}
    _L1_conv_all = _L1_conv_setup()
    _L1_conv_in = {k: v for k, v in _L1_conv_all.items() if k in ('ln1_w', 'ln1_b', 'in_proj_w', 'conv_w', 'conv_b', 'dt_bias', 'A_log', 'D_param', 'ssm_norm_w', 'out_proj_w', 'ff_g', 'ff_v', 'ff_b', 'ln2_w', 'ln2_b', 'fc1_g', 'fc1_v', 'fc1_b', 'fc2_g', 'fc2_v', 'fc2_b')}
    del _L1_conv_all
    return {'x': x, 'L0_conv_sin_i': _L0_conv_in['sin_i'], 'L0_conv_cos_i': _L0_conv_in['cos_i'], 'L0_conv_sin_j': _L0_conv_in['sin_j'], 'L0_conv_cos_j': _L0_conv_in['cos_j'], 'L0_conv_gia': _L0_conv_in['gia'], 'L0_conv_bia': _L0_conv_in['bia'], 'L0_conv_gib': _L0_conv_in['gib'], 'L0_conv_bib': _L0_conv_in['bib'], 'L0_conv_Wq_i': _L0_conv_in['Wq_i'], 'L0_conv_Wkv_i': _L0_conv_in['Wkv_i'], 'L0_conv_Wo_i': _L0_conv_in['Wo_i'], 'L0_conv_bo_i': _L0_conv_in['bo_i'], 'L0_conv_gja': _L0_conv_in['gja'], 'L0_conv_bja': _L0_conv_in['bja'], 'L0_conv_gjb': _L0_conv_in['gjb'], 'L0_conv_bjb': _L0_conv_in['bjb'], 'L0_conv_Wq_j': _L0_conv_in['Wq_j'], 'L0_conv_Wkv_j': _L0_conv_in['Wkv_j'], 'L0_conv_Wo_j': _L0_conv_in['Wo_j'], 'L0_conv_bo_j': _L0_conv_in['bo_j'], 'L1_conv_ln1_w': _L1_conv_in['ln1_w'], 'L1_conv_ln1_b': _L1_conv_in['ln1_b'], 'L1_conv_in_proj_w': _L1_conv_in['in_proj_w'], 'L1_conv_conv_w': _L1_conv_in['conv_w'], 'L1_conv_conv_b': _L1_conv_in['conv_b'], 'L1_conv_dt_bias': _L1_conv_in['dt_bias'], 'L1_conv_A_log': _L1_conv_in['A_log'], 'L1_conv_D_param': _L1_conv_in['D_param'], 'L1_conv_ssm_norm_w': _L1_conv_in['ssm_norm_w'], 'L1_conv_out_proj_w': _L1_conv_in['out_proj_w'], 'L1_conv_ff_g': _L1_conv_in['ff_g'], 'L1_conv_ff_v': _L1_conv_in['ff_v'], 'L1_conv_ff_b': _L1_conv_in['ff_b'], 'L1_conv_ln2_w': _L1_conv_in['ln2_w'], 'L1_conv_ln2_b': _L1_conv_in['ln2_b'], 'L1_conv_fc1_g': _L1_conv_in['fc1_g'], 'L1_conv_fc1_v': _L1_conv_in['fc1_v'], 'L1_conv_fc1_b': _L1_conv_in['fc1_b'], 'L1_conv_fc2_g': _L1_conv_in['fc2_g'], 'L1_conv_fc2_v': _L1_conv_in['fc2_v'], 'L1_conv_fc2_b': _L1_conv_in['fc2_b']}

def reference(x, L0_conv_sin_i, L0_conv_cos_i, L0_conv_sin_j, L0_conv_cos_j, L0_conv_gia, L0_conv_bia, L0_conv_gib, L0_conv_bib, L0_conv_Wq_i, L0_conv_Wkv_i, L0_conv_Wo_i, L0_conv_bo_i, L0_conv_gja, L0_conv_bja, L0_conv_gjb, L0_conv_bjb, L0_conv_Wq_j, L0_conv_Wkv_j, L0_conv_Wo_j, L0_conv_bo_j, L1_conv_ln1_w, L1_conv_ln1_b, L1_conv_in_proj_w, L1_conv_conv_w, L1_conv_conv_b, L1_conv_dt_bias, L1_conv_A_log, L1_conv_D_param, L1_conv_ssm_norm_w, L1_conv_out_proj_w, L1_conv_ff_g, L1_conv_ff_v, L1_conv_ff_b, L1_conv_ln2_w, L1_conv_ln2_b, L1_conv_fc1_g, L1_conv_fc1_v, L1_conv_fc1_b, L1_conv_fc2_g, L1_conv_fc2_v, L1_conv_fc2_b):
    import jax
    import jax.numpy as jnp

    def _L0_conv_ref(x, sin_i, cos_i, sin_j, cos_j, gia, bia, gib, bib, Wq_i, Wkv_i, Wo_i, bo_i, gja, bja, gjb, bjb, Wq_j, Wkv_j, Wo_j, bo_j):
        import jax, jax.numpy as jnp
        import numpy as np
        DIM, IDIM, HEADS = (64, 16, 4)
        B, I, J = (1, 64, 64)
        EPS = 1e-05

        def _sinu(seq, rot):
            inv = 1.0 / 10000.0 ** (np.arange(0, rot, 2, dtype=np.float64) / rot)
            f = np.arange(seq, dtype=np.float64)[:, None] * inv[None, :]
            f = np.repeat(f, 2, axis=-1)
            return (jnp.asarray(np.sin(f)[None], dtype=jnp.float32), jnp.asarray(np.cos(f)[None], dtype=jnp.float32))

        def _ln(x, g, b):
            mu = jnp.mean(x, axis=-1, keepdims=True)
            var = jnp.mean((x - mu) ** 2, axis=-1, keepdims=True)
            return (x - mu) / jnp.sqrt(var + EPS) * g + b

        def _rotate_every_two(x):
            x1, x2 = (x[..., ::2], x[..., 1::2])
            return jnp.stack((-x2, x1), axis=-1).reshape(x.shape)

        def _rope(x, sin, cos):
            sin, cos = (sin[:, None], cos[:, None])
            rd = sin.shape[-1]
            xr, xp = (x[..., :rd], x[..., rd:])
            xr = xr * cos + _rotate_every_two(xr) * sin
            return jnp.concatenate((xr, xp), axis=-1)

        def _attn(a, sin, cos, ga, ba, gb, bb, Wq, Wkv, Wo, bo):
            an = _ln(a, ga, ba)
            bn = _ln(a, gb, bb)
            q = an @ Wq
            k, v = jnp.split(bn @ Wkv, 2, axis=-1)
            Bn, N = (a.shape[0], a.shape[1])

            def heads(t):
                return t.reshape(Bn, N, HEADS, IDIM).transpose(0, 2, 1, 3)
            q, k, v = (heads(q), heads(k), heads(v))
            q = _rope(q, sin, cos)
            k = _rope(k, sin, cos)
            dots = jnp.einsum('bhid,bhjd->bhij', q, k)
            attn = jax.nn.softmax(dots, axis=-1)
            out = jnp.einsum('bhij,bhjd->bhid', attn, v)
            out = out.transpose(0, 2, 3, 1).reshape(Bn, N, IDIM * HEADS)
            return jax.nn.elu(out @ Wo + bo)
        b, i, j, d = x.shape
        xi = x.reshape(b * i, j, d)
        xi = _attn(xi, sin_i, cos_i, gia, bia, gib, bib, Wq_i, Wkv_i, Wo_i, bo_i)
        xi = xi.reshape(b, i, j, d)
        xj = x.transpose(0, 2, 1, 3).reshape(b * j, i, d)
        xj = _attn(xj, sin_j, cos_j, gja, bja, gjb, bjb, Wq_j, Wkv_j, Wo_j, bo_j)
        xj = xj.reshape(b, j, i, d).transpose(0, 2, 1, 3)
        return x + (xi + xj) / 2

    def _L1_conv_ref(z, ln1_w, ln1_b, in_proj_w, conv_w, conv_b, dt_bias, A_log, D_param, ssm_norm_w, out_proj_w, ff_g, ff_v, ff_b, ln2_w, ln2_b, fc1_g, fc1_v, fc1_b, fc2_g, fc2_v, fc2_b):
        import jax, jax.numpy as jnp
        import numpy as np
        EMB = 64
        D_INNER = 128
        HEADDIM = 16
        NHEADS = D_INNER // HEADDIM
        DSTATE = 32
        DCONV = 4
        CONV_DIM = D_INNER + 2 * DSTATE
        D_IN_PROJ = 2 * D_INNER + 2 * DSTATE + NHEADS
        LN_EPS = 1e-05

        def _layernorm(x, w, b):
            m = jnp.mean(x, axis=-1, keepdims=True)
            v = jnp.mean((x - m) ** 2, axis=-1, keepdims=True)
            return (x - m) * jax.lax.rsqrt(v + LN_EPS) * w + b

        def _wn_linear(x, g, v, b):
            w = g[:, None] * v / jnp.linalg.norm(v, axis=1, keepdims=True)
            return x @ w.T + b

        def _ssm_scan(x, dt, A, Bm, Cm):
            dA = jnp.exp(dt * A)
            dtx = dt[..., None] * x
            bsz = x.shape[0]

            def step(h, inp):
                dA_t, dtx_t, B_t, C_t = inp
                h = h * dA_t[:, :, None, None] + dtx_t[..., None] * B_t[:, None, None, :]
                y = jnp.einsum('bhpn,bn->bhp', h, C_t)
                return (h, y)
            h0 = jnp.zeros((bsz, NHEADS, HEADDIM, DSTATE), x.dtype)
            xs = (jnp.swapaxes(dA, 0, 1), jnp.swapaxes(dtx, 0, 1), jnp.swapaxes(Bm, 0, 1), jnp.swapaxes(Cm, 0, 1))
            _, ys = jax.lax.scan(step, h0, xs)
            return jnp.swapaxes(ys, 0, 1)

        def _mamba2(u, in_proj_w, conv_w, conv_b, dt_bias, A_log, D_param, ssm_norm_w, out_proj_w):
            B, L, _ = u.shape
            zxbcdt = u @ in_proj_w.T
            z_gate = zxbcdt[..., :D_INNER]
            xBC = zxbcdt[..., D_INNER:D_INNER + CONV_DIM]
            dt = zxbcdt[..., D_INNER + CONV_DIM:]
            xp = jnp.pad(xBC, ((0, 0), (DCONV - 1, 0), (0, 0)))
            xc = jax.lax.conv_general_dilated(jnp.swapaxes(xp, 1, 2), conv_w[:, None, :], (1,), 'VALID', feature_group_count=CONV_DIM, dimension_numbers=('NCH', 'OIH', 'NCH'))
            xc = jax.nn.silu(jnp.swapaxes(xc, 1, 2) + conv_b)
            x = xc[..., :D_INNER].reshape(B, L, NHEADS, HEADDIM)
            Bm = xc[..., D_INNER:D_INNER + DSTATE]
            Cm = xc[..., D_INNER + DSTATE:]
            dt = jax.nn.softplus(dt + dt_bias)
            A = -jnp.exp(A_log)
            y = _ssm_scan(x, dt, A, Bm, Cm) + D_param[None, None, :, None] * x
            y = y.reshape(B, L, D_INNER)
            yg = y * jax.nn.silu(z_gate)
            yn = yg * jax.lax.rsqrt(jnp.mean(yg ** 2, axis=-1, keepdims=True) + LN_EPS) * ssm_norm_w
            return yn @ out_proj_w.T
        b, nu, na, e = z.shape
        u = _layernorm(z, ln1_w, ln1_b).reshape(-1, na, e)
        y = _mamba2(u, in_proj_w, conv_w, conv_b, dt_bias, A_log, D_param, ssm_norm_w, out_proj_w)
        y = _wn_linear(y, ff_g, ff_v, ff_b).reshape(b, nu, na, e)
        z = z + y
        h = _layernorm(z, ln2_w, ln2_b)
        h = jax.nn.gelu(_wn_linear(h, fc1_g, fc1_v, fc1_b), approximate=False)
        h = _wn_linear(h, fc2_g, fc2_v, fc2_b)
        return z + h

    def _gn(v, G=32, eps=1e-05):
        B_, H_, W_, C_ = v.shape
        g = v.reshape(B_, H_, W_, G, C_ // G)
        m = jnp.mean(g, axis=(1, 2, 4), keepdims=True)
        s = jnp.var(g, axis=(1, 2, 4), keepdims=True)
        return ((g - m) / jnp.sqrt(s + eps)).reshape(v.shape)

    def _ln_c(v, eps=1e-06):
        m = jnp.mean(v, axis=-1, keepdims=True)
        s = jnp.var(v, axis=-1, keepdims=True)
        return (v - m) / jnp.sqrt(s + eps)

    def _ln_t(v, eps=1e-05):
        m = jnp.mean(v, axis=-1, keepdims=True)
        s = jnp.var(v, axis=-1, keepdims=True)
        return (v - m) / jnp.sqrt(s + eps)

    def _to_tokens(v):
        B_, H_, W_, C_ = v.shape
        return v.reshape(B_, H_ * W_, C_)

    def _from_tokens(t, like):
        return t.reshape(like.shape)
    x = _L0_conv_ref(x, L0_conv_sin_i, L0_conv_cos_i, L0_conv_sin_j, L0_conv_cos_j, L0_conv_gia, L0_conv_bia, L0_conv_gib, L0_conv_bib, L0_conv_Wq_i, L0_conv_Wkv_i, L0_conv_Wo_i, L0_conv_bo_i, L0_conv_gja, L0_conv_bja, L0_conv_gjb, L0_conv_bjb, L0_conv_Wq_j, L0_conv_Wkv_j, L0_conv_Wo_j, L0_conv_bo_j)
    x = _L1_conv_ref(x, L1_conv_ln1_w, L1_conv_ln1_b, L1_conv_in_proj_w, L1_conv_conv_w, L1_conv_conv_b, L1_conv_dt_bias, L1_conv_A_log, L1_conv_D_param, L1_conv_ssm_norm_w, L1_conv_out_proj_w, L1_conv_ff_g, L1_conv_ff_v, L1_conv_ff_b, L1_conv_ln2_w, L1_conv_ln2_b, L1_conv_fc1_g, L1_conv_fc1_v, L1_conv_fc1_b, L1_conv_fc2_g, L1_conv_fc2_v, L1_conv_fc2_b)
    return x

_drawn_inputs = setup_inputs


def setup_inputs(seed=0):
    import zlib

    import numpy as np

    out = dict(_drawn_inputs(seed))
    spreads = {'L0_conv_gia': (1.0, 0.2),
     'L0_conv_bia': (0.0, 0.1),
     'L0_conv_gib': (1.0, 0.2),
     'L0_conv_bib': (0.0, 0.1),
     'L0_conv_bo_i': (0.0, 0.1),
     'L0_conv_gja': (1.0, 0.2),
     'L0_conv_bja': (0.0, 0.1),
     'L0_conv_gjb': (1.0, 0.2),
     'L0_conv_bjb': (0.0, 0.1),
     'L0_conv_bo_j': (0.0, 0.1),
     'L1_conv_ln1_w': (1.0, 0.2),
     'L1_conv_ln1_b': (0.0, 0.1),
     'L1_conv_D_param': (1.0, 0.2),
     'L1_conv_ssm_norm_w': (1.0, 0.2),
     'L1_conv_ff_b': (0.0, 0.1),
     'L1_conv_ln2_w': (1.0, 0.2),
     'L1_conv_ln2_b': (0.0, 0.1),
     'L1_conv_fc1_b': (0.0, 0.1),
     'L1_conv_fc2_b': (0.0, 0.1)}
    factors = {'L1_conv_conv_b': 3.679}
    for name, (base, spread) in spreads.items():
        noise = np.random.default_rng([zlib.crc32(name.encode()), seed]).standard_normal(out[name].shape)
        drawn = base * np.exp(spread * noise) if base else spread * noise
        out[name] = jnp.asarray(drawn.astype(out[name].dtype))
    for name, factor in factors.items():
        out[name] = (out[name] * factor).astype(out[name].dtype)
    return out
```

```python
from contextlib import ExitStack

import numpy as np

import concourse.bass as bass
from concourse import mybir

F32 = mybir.dt.float32
ALU = mybir.AluOpType
ACT = mybir.ActivationFunctionType
AX = mybir.AxisListType.X

P = 128
GRID = 64
DIM = 64
HEADS, HD = 4, 16
SSM_H, SSM_P, STATE = 8, 16, 32
INNER = SSM_H * SSM_P
LN_EPS = 1e-5
TILES = GRID // 2
CT = 8
CHUNKS = TILES // CT
CW = CT * GRID
ATT_CHUNKS = 2 * CHUNKS
PAIRS = ATT_CHUNKS * CT // 2
ATT_STEPS = PAIRS + 6

CONSTS = dict(ident=P, sign=5 * DIM, head_mask=HEADS, v_mask=P, tri=GRID, tri_quarter=GRID,
              later=P, ident2=GRID, mean_bd=P, sp_mask=2)
PARAMS = dict(wqkv_j=5 * DIM, wqkv_i=5 * DIM, wo_j=P, wo_i=P, cos_j=GRID, sin_j=GRID, cos_i=GRID,
              sin_i=GRID, w_xbc=INNER + 2 * STATE, tap_a=INNER + 2 * STATE, tap_b=INNER + 2 * STATE,
              w_dt=SSM_H, w_z=2 * P, w_out=2 * P, norm_w=2 * P, ff_vt=DIM, fc1_vt=P, fc2_vt=P,
              ff_v=DIM, fc1_v=DIM, fc2_v=DIM, conv_bx=INNER, dt_bias=SSM_H, a_log=SSM_H, d_par=SSM_H)
COLS = dict(ga_j=1, ba_j=1, gb_j=1, bb_j=1, ga_i=1, ba_i=1, gb_i=1, bb_i=1, bo_j=1, bo_i=1, ln1_w=1,
            ln1_b=1, ln2_w=1, ln2_b=1, ff_g=1, ff_b=1, fc1_g=1, fc1_b=1, fc2_g=1, fc2_b=1, conv_bbc=1)


def offsets(widths):
    at, out = 0, {}
    for name, w in widths.items():
        out[name] = (at, at + w)
        at += w
    return out, at


def attention_uses():
    steps = {-1: [(k, 0) for k in ("v", "qA", "qB", "kA", "kB", "vt0", "vt1")]}
    for n in range(PAIRS):
        g, slot = divmod(n, 4)
        uses = []
        if g + 1 < ATT_CHUNKS:
            uses += [(k, g + 1) for k in (("v", "qA"), ("qB", "kA"), ("kB", "vt0"), ("vt1",))[slot]]
        if slot == 1 and 2 <= g < 2 + CHUNKS:
            uses.append(("yt", g - 2))
        if slot == 3 and g >= 1:
            uses.append(("wo", g - 1))
        steps[n] = uses
    for n in range(PAIRS, ATT_STEPS):
        steps[n] = [("wo", ATT_CHUNKS - 1)] if n == PAIRS + 3 else []
    return steps


OUT_LAG = 12
SSM_STEPS = TILES - CT + OUT_LAG + 8


def ssm_uses():
    before = [("xt", q) for q in range(CHUNKS)] + [("ut", q) for q in range(CHUNKS)]
    before += [("bc", 0), ("z0", 0), ("z1", 0)] + [("xp", n) for n in range(TILES // 2)]
    steps = {}
    for m in range(SSM_STEPS):
        uses = []
        if m % CT == 2 and m // CT + 1 < CHUNKS:
            uses.append(("bc", m // CT + 1))
        if m % CT == 3 and m // CT + 1 < CHUNKS:
            uses += [("z0", m // CT + 1), ("z1", m // CT + 1)]
        for lag, kinds in {0: ("ms", "op"), 2: ("yo",), 4: ("ht",), 5: ("f1",), 6: ("f2",), 7: ("fo",)}.items():
            c, rest = divmod(m - OUT_LAG - lag, CT)
            if rest == 0 and 0 <= c < CHUNKS:
                uses += [(k, c) for k in kinds]
        steps[m] = uses
    return before, steps


def build(nc, x, consts, params, cols, out):
    co, n_consts = offsets(CONSTS)
    po, n_params = offsets(PARAMS)
    lo, n_cols = offsets(COLS)
    att_steps = attention_uses()
    ssm_before, ssm_steps = ssm_uses()
    order = [u for n in sorted(att_steps) for u in att_steps[n]] + ssm_before \
        + [u for m in range(SSM_STEPS) for u in ssm_steps[m]]
    ring_at = {use: r for r, use in enumerate(order)}

    x_v = x.rearrange("o (u t i) j c -> t i j (o u) c", t=2, i=2)
    out_v = out.rearrange("o (u t i) j c -> t i j (o u) c", t=2, i=2)
    turned = nc.dram_tensor("attention_j_turned", (GRID, GRID, DIM), F32, kind="Internal").ap()
    turned_w = turned.rearrange("i (u t j) c -> t i u (j c)", t=2, j=2)
    turned_r = turned.rearrange("(u t i) j c -> t i j u c", t=2, i=2)

    with ExitStack() as ctx:
        def sb(name, shape, where=ctx):
            return where.enter_context(nc.sbuf_tensor(name, shape, F32))

        def sem(name):
            return ctx.enter_context(nc.semaphore(name))

        bank = [ctx.enter_context(nc.psum_tensor(f"bank{b}", [P, CW], F32)) for b in range(8)]
        RING, SCORE, PT, OZ = bank[0:2], bank[2:4], bank[4:6], bank[6:8]
        DEC, YT, GB = bank[2:4], bank[4:6], bank[6:8]

        c_sb = sb("c_sb", [P, n_consts])
        p_sb = sb("p_sb", [P, n_params])
        l_sb = sb("l_sb", [P, n_cols])

        def cst(name):
            return c_sb[:, co[name][0]:co[name][1]]

        def par(name):
            return p_sb[:, po[name][0]:po[name][1]]

        def col(name, a=0, b=P):
            return l_sb[a:b, lo[name][0]:lo[name][1]]

        eps_col = sb("eps_col", [P, 3])
        x_tok = sb("x_tok", [P, 16, 2 * DIM])
        back = sb("back", [P, 16, 2 * DIM])
        cen = sb("cen", [P, 2, CW])
        sqr = sb("sqr", [P, 2, CW])
        xhat = sb("xhat", [P, 2, CW])
        ln_s = sb("ln_s", [P, 12, 8])
        ln_n = sb("ln_n", [P, 12, 8])
        ln_v = sb("ln_v", [P, 12, 8])
        ln_l = sb("ln_l", [P, 12, 8])
        ln_r = sb("ln_r", [P, 12, 8])
        y_t = sb("y_t", [P, 2, CHUNKS, CW])
        w_sig = [sb(f"w_sig{d}", [P, 5 * DIM]) for d in range(2)]
        w_att = [sb(f"w_att{d}", [P, 5 * DIM]) for d in range(2)]
        w_xdt = sb("w_xdt", [P, INNER + SSM_H])
        w_xb = sb("w_xb", [P, INNER])
        w_bca = sb("w_bca", [P, 2 * STATE])
        w_bcb = sb("w_bcb", [P, 2 * STATE])
        w_ops = sb("w_ops", [P, 2 * P])
        w_ofd = sb("w_ofd", [P, 2, 2, DIM])
        nrm_q = sb("nrm_q", [P, 3, DIM])
        nrm_s = sb("nrm_s", [P, 3])
        nrm_l = sb("nrm_l", [P, 3])
        nrm_r = sb("nrm_r", [P, 3])
        nrm_g = sb("nrm_g", [P, 3])
        a_neg = sb("a_neg", [P, SSM_H])
        a_exp = sb("a_exp", [P, SSM_H])
        d_half = sb("d_half", [P, SSM_H])

        att = ExitStack()
        xn_t = sb("xn_t", [P, TILES, 2, GRID], att)
        rot = sb("rot", [P, 4, CW], att)
        k_rot = sb("k_rot", [P, CW], att)
        q_bd = sb("q_bd", [P, 2, CT, 2, GRID], att)
        k_bd = sb("k_bd", [P, 2, HEADS, CW], att)
        v_dup = sb("v_dup", [P, CT, 2, GRID], att)
        v_bd = sb("v_bd", [P, 2, CT, P], att)
        s_max = sb("s_max", [P, 2, 8], att)
        s_cen = sb("s_cen", [P, 2, 8, GRID], att)
        prob = sb("prob", [P, 2, 4, P], att)
        prob_t = sb("prob_t", [P, 2, 4, P], att)
        z_log = sb("z_log", [P, 2, P], att)
        z_inv = sb("z_inv", [P, 2, P], att)
        o_t = sb("o_t", [P, 2, CT, GRID], att)
        wo_b = sb("wo_b", [P, CW], att)
        wo_n = sb("wo_n", [P, CW], att)
        wo_e = sb("wo_e", [P, CW], att)
        y_tok = sb("y_tok", [P, CHUNKS, CW], att)
        att.close()

        ssm = ExitStack()
        u2 = sb("u2", [P, CHUNKS, CW], ssm)
        ut_a = sb("ut_a", [P, TILES, 2, GRID], ssm)
        ut_b = sb("ut_b", [P, TILES, 2, GRID], ssm)
        xv = sb("xv", [P, TILES, INNER], ssm)
        xth = sb("xth", [P, 2, 4, INNER], ssm)
        dt_all = sb("dt_all", [P, 9, TILES * SSM_H], ssm)
        b_c = sb("b_c", [P, 2, CW], ssm)
        b_s = sb("b_s", [2 * STATE, 2, CW], ssm)
        c_s = sb("c_s", [2 * STATE, 2, CW], ssm)
        z_s = sb("z_s", [P, 2, 2, CT, GRID], ssm)
        a_msk = sb("a_msk", [P, 2, SSM_H, GRID], ssm)
        dec = sb("dec", [P, 2, SSM_H, GRID], ssm)
        mix = sb("mix", [P, 2, SSM_H, GRID], ssm)
        g_m = sb("g_m", [P, 2, 4, GRID], ssm)
        dtx = sb("dtx", [P, 2, 4, SSM_H, 2, SSM_P], ssm)
        d_x = sb("d_x", [P, 2, 4, SSM_H, 2, SSM_P], ssm)
        y_g = sb("y_g", [P, 2, 2, CT, GRID], ssm)
        ssm.close()
        y_sq = y_t[:, 0, 0:2, :].rearrange("p h (t j) -> p h t j", j=GRID)
        y_n, y_o = y_t[:, 0, 2, :], y_t[:, 0, 3, :]
        h_t, f_1, f_2, rms_l = (back[:, 4 * k:4 * k + 4, :].rearrange("p u n -> p (u n)") for k in range(4))
        rms_r, z_th = y_t[:, 1, 0, :], y_t[:, 1, 1:3, :]

        consts_in = sem("consts_in")
        params_in = sem("params_in")
        cols_in = sem("cols_in")
        turned_out = sem("turned_out")
        out_done = sem("out_done")
        eps_set = sem("eps_set")
        q_zeroed = sem("q_zeroed")
        w_signed = sem("w_signed")
        w_scaled = sem("w_scaled")
        bias_row = sem("bias_row")
        w_ready = sem("w_ready")
        taps_ready = sem("taps_ready")
        out_scaled = sem("out_scaled")
        out_folded = sem("out_folded")
        w_out_ready = sem("w_out_ready")
        nrm_sq = sem("nrm_sq")
        nrm_sum = sem("nrm_sum")
        nrm_log = sem("nrm_log")
        nrm_rs = sem("nrm_rs")
        nrm_ready = sem("nrm_ready")
        a_exped = sem("a_exped")
        a_ready = sem("a_ready")
        d_ready = sem("d_ready")
        xn_ones = sem("xn_ones")
        xn_ready = sem("xn_ready")
        ln_sum = sem("ln_sum")
        ln_negmean = sem("ln_negmean")
        ln_centred = sem("ln_centred")
        ln_squared = sem("ln_squared")
        ln_var = sem("ln_var")
        ln_log = sem("ln_log")
        ln_rstd = sem("ln_rstd")
        ln_done = sem("ln_done")
        ln_turned = sem("ln_turned")
        ring_filled = sem("ring_filled")
        rotated = sem("rotated")
        q_ready = sem("q_ready")
        k_added = sem("k_added")
        k_ready = sem("k_ready")
        v_duped = sem("v_duped")
        v_ready = sem("v_ready")
        scored = sem("scored")
        s_maxed = sem("s_maxed")
        s_centred = sem("s_centred")
        exped = sem("exped")
        p_turned = sem("p_turned")
        p_copied = sem("p_copied")
        av_done = sem("av_done")
        z_logged = sem("z_logged")
        z_inverted = sem("z_inverted")
        o_ready = sem("o_ready")
        wo_biased = sem("wo_biased")
        wo_clipped = sem("wo_clipped")
        wo_exped = sem("wo_exped")
        y_ready = sem("y_ready")
        y_turned = sem("y_turned")
        halved = sem("halved")
        x_halved = sem("x_halved")
        u_starts = sem("u_starts")
        x1_ready = sem("x1_ready")
        u2_ready = sem("u2_ready")
        ssm_zeroed = sem("ssm_zeroed")
        xv_ready = sem("xv_ready")
        dtv_ready = sem("dtv_ready")
        dt_chain = sem("dt_chain")
        dt_act = sem("dt_act")
        dt_ready = sem("dt_ready")
        xth_ready = sem("xth_ready")
        xs_ready = sem("xs_ready")
        x_scaled = sem("x_scaled")
        bc_biased = sem("bc_biased")
        bc_tanh = sem("bc_tanh")
        b_ready = sem("b_ready")
        c_ready = sem("c_ready")
        z_tanh = sem("z_tanh")
        z_ready = sem("z_ready")
        a_masked = sem("a_masked")
        decayed = sem("decayed")
        dec_exped = sem("dec_exped")
        g_scored = sem("g_scored")
        g_masked = sem("g_masked")
        mixed = sem("mixed")
        y_summed = sem("y_summed")
        gated = sem("gated")
        y_squared = sem("y_squared")
        rms_logged = sem("rms_logged")
        rms_ready = sem("rms_ready")
        y_normed = sem("y_normed")
        yo_ready = sem("yo_ready")
        z1_ready = sem("z1_ready")
        h_ready = sem("h_ready")
        f1_ready = sem("f1_ready")
        f2_ready = sem("f2_ready")
        o_added = sem("o_added")
        x_in = [sem(f"x_in{q}") for q in range(CHUNKS)]
        back_in = [sem(f"back_in{q}") for q in range(CHUNKS)]
        ut_in = [sem(f"ut_in{q}") for q in range(CHUNKS)]
        block = ctx.enter_context(nc.Block())

        def filled(eng, use):
            r = ring_at[use]
            eng.wait_ge(ring_filled, r + 1)
            return RING[r % 2]

        def drained(eng, use):
            kind, g = use
            signal, count = {
                "v": (v_duped, g + 1), "qA": (rotated, 4 * g + 1), "qB": (rotated, 4 * g + 2),
                "kA": (rotated, 4 * g + 3), "kB": (rotated, 4 * g + 4), "vt0": (v_ready, 2 * g + 1),
                "vt1": (v_ready, 2 * g + 2), "wo": (wo_biased, g + 1), "yt": (y_turned, g + 1),
                "xt": (x1_ready, g + 1), "ut": (u2_ready, g + 1), "bc": (bc_biased, g + 1),
                "z0": (z_ready, 2 * g + 1), "z1": (z_ready, 2 * g + 2), "xp": (dtv_ready, g + 1),
                "ms": (rms_logged, g + 1), "op": (y_normed, g + 1), "yo": (z1_ready, g + 1),
                "ht": (h_ready, g + 1), "f1": (f1_ready, g + 1), "f2": (f2_ready, g + 1),
                "fo": (o_added, g + 1)}[kind]
            eng.wait_ge(signal, count)

        def x_of(layer, q):
            return x_tok[:, 4 * q:4 * q + 4, :].rearrange("p u n -> p (u n)")

        def groups(ap):
            return ap.rearrange("p (a c) -> p a c", c=DIM)

        def xn_cols(d, c, sp):
            if d == 0:
                flat = xn_t[:, :, :, :].rearrange("p t s (k r) -> p (t s) k r", r=2)
                return flat[:, :, CT * c:CT * c + CT, sp].rearrange("p i k -> p k i")
            return xn_t[:, CT * c:CT * c + CT, sp, :]

        def wide(ap, n=CT):
            return ap.unsqueeze(1).broadcast_to([ap.shape[0], n, ap.shape[1]])

        def deep(ap, n):
            return ap.unsqueeze(2).broadcast_to([ap.shape[0], ap.shape[1], n])

        HALVES = [(tau, ip) for tau in range(2) for ip in range(2)]

        def part_of(tile, q, tau, ip):
            return tile[64 * tau:64 * tau + 64, 4 * q:4 * q + 4, DIM * ip:DIM * ip + DIM]

        @block.sync
        def _(sp):
            for q in range(CHUNKS):
                for tau, ip in HALVES:
                    sp.dma_start(part_of(x_tok, q, tau, ip), x_v[tau, ip, :, 4 * q:4 * q + 4]).then_inc(x_in[q], 16)
                if q == 0:
                    sp.dma_start(c_sb[:, :], consts).then_inc(consts_in, 16)
                    sp.dma_start(l_sb[:, :], cols).then_inc(cols_in, 16)
                    sp.dma_start(p_sb[:, :], params).then_inc(params_in, 16)
            for g in range(CHUNKS):
                sp.wait_ge(y_turned, g + 1)
                for tau in range(2):
                    sp.dma_start(turned_w[tau, :, 4 * g:4 * g + 4],
                                 y_tok[64 * tau:64 * tau + 64, g, :].rearrange("p (u n) -> p u n", u=4)).then_inc(turned_out, 16)
            sp.wait_ge(turned_out, 32 * CHUNKS)
            for q in range(CHUNKS):
                for tau, ip in HALVES:
                    sp.dma_start(part_of(back, q, tau, ip), turned_r[tau, ip, :, 4 * q:4 * q + 4]).then_inc(back_in[q], 16)
            sp.wait_ge(u_starts, 3)
            for q in range(CHUNKS):
                sp.wait_ge(u2_ready, q + 1)
                for dst, half, shift in ((ut_a, 0, 0), (ut_a, 1, 1), (ut_b, 0, 2), (ut_b, 1, 3)):
                    for m in range(2):
                        src = u2[64 * m:64 * m + 64, q, :].rearrange("p (t j) -> p t j", j=GRID)
                        sp.dma_start(dst[64 * half:64 * half + 64, CT * q:CT * q + CT, m, shift:GRID],
                                     src[:, :, 0:GRID - shift]).then_inc(ut_in[q], 16)
            for q in range(CHUNKS):
                sp.wait_ge(o_added, q + 1)
                for tau, ip in HALVES:
                    sp.dma_start(out_v[tau, ip, :, 4 * q:4 * q + 4], part_of(x_tok, q, tau, ip)).then_inc(out_done, 16)
            sp.wait_ge(out_done, 64 * CHUNKS)

        @block.tensor
        def _(pe):
            def mm(dst, lhsT, rhs, start=True, stop=True):
                return pe.matmul(dst, lhsT, rhs, start=start, stop=stop, skip_group_check=True)

            pe.wait_ge(consts_in, 16)
            pe.wait_ge(cols_in, 16)
            pe.wait_ge(params_in, 16)
            for d, n in enumerate("ji"):
                pe.wait_ge(w_signed, d + 1)
                mm(RING[d][64:65, 0:128], col(f"ba_{n}"), w_sig[d][:, 0:128])
                mm(RING[d][64:65, 128:320], col(f"bb_{n}"), w_sig[d][:, 128:320]).then_inc(bias_row, 1)
            pe.wait_ge(out_scaled, 1)
            for hh in range(2):
                last = mm(bank[2][:, DIM * hh:DIM * hh + DIM], w_ops[:, P * hh:P * hh + P], par("ff_vt"))
            last.then_inc(out_folded, 1)

            def turn(dst, src, last_sem=None):
                for k in range(4):
                    last = pe.transpose(dst[:, P * k:P * k + P], src[:, P * k:P * k + P], cst("ident"))
                return last

            for q in range(CHUNKS):
                pe.wait_ge(ln_done, q + 1)
                turn(bank[4 + q], xhat[:, q % 2, :]).then_inc(ln_turned, 1)

            def take(use):
                r = ring_at[use]
                if r >= 2:
                    drained(pe, order[r - 2])
                return RING[r % 2]

            Q, RQ, K, V, RK = (slice(DIM * k, DIM * k + DIM) for k in range(5))

            def att_use(use):
                kind, g = use
                dst = take(use)
                d, c = divmod(g, CHUNKS)
                if kind in ("v", "qA", "qB", "kA", "kB"):
                    part = {"v": V, "qA": Q, "qB": RQ, "kA": K, "kB": RK}[kind]
                    for m in range(2):
                        last = mm(dst[64 * m:64 * m + 64, :], w_att[d][:, part], xn_cols(d, c, m))
                elif kind in ("vt0", "vt1"):
                    if kind == "vt0":
                        pe.wait_ge(v_duped, g + 1)
                    half = int(kind[2])
                    last = turn(dst, v_dup[:, 4 * half:4 * half + 4, :, :].rearrange("p t r j -> p (t r j)"))
                elif kind == "wo":
                    pe.wait_ge(o_ready, 4 * g + 4)
                    last = mm(dst[:, :], par("wo_j" if d == 0 else "wo_i"),
                              o_t[:, g % 2, :, :].rearrange("p t j -> p (t j)"))
                elif kind == "yt":
                    pe.wait_ge(y_ready, g + 1)
                    last = turn(dst, y_t[:, 0, g, :])
                last.then_inc(ring_filled, 1)

            pe.wait_ge(w_ready, 2)
            pe.wait_ge(w_out_ready, 1)
            pe.wait_ge(xn_ones, 2)
            pe.wait_ge(xn_ready, 2 * CHUNKS)
            for use in att_steps[-1]:
                att_use(use)
            for n in range(ATT_STEPS):
                for use in att_steps[n]:
                    att_use(use)
                if n < PAIRS:
                    g, slot = divmod(n, 4)
                    if slot == 0:
                        pe.wait_ge(q_ready, 2 * g + 2)
                        pe.wait_ge(k_ready, 4 * g + 4)
                    if n >= 2:
                        pe.wait_ge(s_centred, n - 1)
                    for k in range(2):
                        t = 2 * slot + k
                        last = mm(SCORE[n % 2][:, 256 * k:256 * k + 256],
                                  q_bd[:, g % 2, t, :, :].rearrange("p s i -> p (s i)"),
                                  k_bd[:, g % 2, :, GRID * t:GRID * t + GRID])
                    last.then_inc(scored, 1)
                if 1 <= n <= PAIRS:
                    e = n - 1
                    pe.wait_ge(exped, e + 1)
                    if e >= 2:
                        pe.wait_ge(p_copied, e - 1)
                    turn(PT[e % 2], prob[:, e % 2, :, :].rearrange("p k n -> p (k n)")).then_inc(p_turned, 1)
                if 2 <= n <= PAIRS + 1:
                    e = n - 2
                    g, slot = divmod(e, 4)
                    pe.wait_ge(p_copied, e + 1)
                    if slot == 0:
                        pe.wait_ge(v_ready, 2 * g + 2)
                    if e >= 2:
                        pe.wait_ge(o_ready, e - 1)
                    pts = prob_t[:, e % 2, :, :].rearrange("p (t r) n -> p t r n", t=2)
                    for k in range(2):
                        for m in range(2):
                            for hp in range(2):
                                row = 64 * m + 32 * hp
                                mm(OZ[e % 2][row:row + 32, 64 * k:64 * k + 64],
                                   v_bd[:, g % 2, 2 * slot + k, row:row + 32], pts[:, k, hp, 64 * m:64 * m + 64])
                    for m in range(2):
                        for hp in range(2):
                            row = 64 * m + 32 * hp
                            last = mm(OZ[e % 2][row:row + 32, 128:256], cst("v_mask")[:, 0:32],
                                      pts[:, :, hp, 64 * m:64 * m + 64])
                    last.then_inc(av_done, 1)

            def ssm_use(use):
                kind, c = use
                dst = take(use)
                if kind == "xt":
                    pe.wait_ge(y_ready, CHUNKS + c + 1)
                    last = turn(dst, y_t[:, 1, c, :])
                elif kind == "ut":
                    pe.wait_ge(ln_done, CHUNKS + c + 1)
                    last = turn(dst, xhat[:, c % 2, :])
                elif kind == "bc":
                    pe.wait_ge(ut_in[c], 128)
                    for half, (w, u) in enumerate(((w_bca, ut_a), (w_bcb, ut_b))):
                        for part in range(2):
                            for m in range(2):
                                row = 64 * part + 32 * m
                                last = mm(dst[row:row + 32, :], w[:, STATE * part:STATE * part + STATE],
                                          u[:, CT * c:CT * c + CT, m, :], start=half == 0, stop=half == 1)
                elif kind in ("z0", "z1"):
                    hh = int(kind[1])
                    last = mm(dst[:, :], par("w_z")[:, P * hh:P * hh + P], u2[:, c, :])
                elif kind == "xp":
                    pe.wait_ge(ut_in[2 * c // CT], 128)
                    for k in range(2):
                        t, w = 2 * c + k, INNER + SSM_H
                        mm(dst[:, w * k:w * k + INNER], ut_b[:, t, :, :].rearrange("p s j -> p (s j)"), w_xb[:, :],
                           start=True, stop=False)
                        last = mm(dst[:, w * k:w * k + w], ut_a[:, t, :, :].rearrange("p s j -> p (s j)"), w_xdt[:, :],
                                  start=False, stop=True)
                elif kind == "ms":
                    pe.wait_ge(y_squared, c + 1)
                    for hh in range(2):
                        last = mm(dst[:, :], cst("mean_bd"), y_sq[:, hh, :, :].rearrange("p t j -> p (t j)"),
                                  start=hh == 0, stop=hh == 1)
                elif kind == "op":
                    for hh in range(2):
                        last = mm(dst[:, :], w_ofd[:, hh, :, :].rearrange("p s c -> p (s c)"),
                                  y_g[:, c % 2, hh, :, :].rearrange("p t j -> p (t j)"), start=hh == 0, stop=hh == 1)
                elif kind == "yo":
                    pe.wait_ge(yo_ready, c + 1)
                    last = turn(dst, y_o)
                elif kind == "ht":
                    pe.wait_ge(ln_done, 2 * CHUNKS + c + 1)
                    last = turn(dst, xhat[:, c % 2, :])
                elif kind == "f1":
                    pe.wait_ge(h_ready, c + 1)
                    last = mm(dst[:, :], par("fc1_vt"), h_t)
                elif kind == "f2":
                    pe.wait_ge(f1_ready, c + 1)
                    last = mm(dst[:, :], par("fc2_vt"), f_1)
                elif kind == "fo":
                    pe.wait_ge(f2_ready, c + 1)
                    last = turn(dst, f_2)
                last.then_inc(ring_filled, 1)

            for use in ssm_before:
                if use == ("bc", 0):
                    pe.wait_ge(taps_ready, 5)
                ssm_use(use)
            for m in range(SSM_STEPS):
                for use in ssm_steps[m]:
                    ssm_use(use)
                if m < TILES and m % 4 == 0:
                    k, c = m // 4, m // CT
                    if m % CT == 0:
                        pe.wait_ge(b_ready, c + 1)
                        pe.wait_ge(c_ready, c + 1)
                    if k >= 2:
                        pe.wait_ge(g_masked, k - 1)
                    for t in range(4):
                        at = GRID * ((m + t) % CT)
                        for s in range(2):
                            rows = slice(STATE * s, STATE * s + STATE)
                            last = mm(GB[k % 2][64 * s:64 * s + 64, GRID * t:GRID * t + GRID],
                                      b_s[rows, c % 2, at:at + GRID], c_s[rows, c % 2, at:at + GRID])
                    last.then_inc(g_scored, 1)
                if m < TILES:
                    pe.wait_ge(a_masked, m + 1)
                    if m >= 2:
                        pe.wait_ge(dec_exped, m - 1)
                    mm(DEC[m % 2][:, :], cst("later"), a_msk[:, m % 2, :, :].rearrange("p h t -> p (h t)"))\
                        .then_inc(decayed, 1)
                e = m - 2
                if 0 <= e < TILES:
                    k = e // 4
                    pe.wait_ge(mixed, e + 1)
                    if e % 4 == 0:
                        pe.wait_ge(x_scaled, 4 * k + 4)
                        if k >= 2:
                            pe.wait_ge(gated, k - 1)
                    for hh in range(2):
                        at = P * (e % 4) + GRID * hh
                        for term in range(2):
                            for h4 in range(4):
                                h = 4 * hh + h4
                                xs = (dtx, d_x)[term][:, k % 2, e % 4, h, :, :].rearrange("p s n -> p (s n)")
                                rhs = cst("ident2") if term else mix[:, e % 2, h, :]
                                last = mm(YT[k % 2][32 * h4:32 * h4 + 32, at:at + GRID], xs, rhs,
                                          start=term == 0, stop=term == 1)
                    last.then_inc(y_summed, 1)

        def wait_ln_turned(eng, m):
            if m < CHUNKS:
                eng.wait_ge(ln_turned, m + 1)
            else:
                filled(eng, ("ut" if m < 2 * CHUNKS else "ht", m % CHUNKS))

        def ln_vector_a(v, m):
            src = x_of(m // CHUNKS, m % CHUNKS)
            v.tensor_reduce(ln_s[:, m, :], groups(src), AX, ALU.add).then_inc(ln_sum, 1)
            v.wait_ge(ln_sum, m + 1)
            v.tensor_scalar(ln_n[:, m, :], ln_s[:, m, :], -1.0 / DIM, None, ALU.mult).then_inc(ln_negmean, 1)
            v.wait_ge(ln_negmean, m + 1)
            v.tensor_tensor(groups(cen[:, m % 2, :]), groups(src), deep(ln_n[:, m, :], DIM), ALU.add).then_inc(ln_centred, 1)

        def ln_scalar_a(a, m):
            a.wait_ge(ln_centred, m + 1)
            if m >= 2:
                a.wait_ge(ln_var, m - 1)
            a.activation(sqr[:, m % 2, :], cen[:, m % 2, :], ACT.Square).then_inc(ln_squared, 1)

        def ln_vector_b(v, m):
            v.wait_ge(ln_squared, m + 1)
            v.tensor_reduce(ln_v[:, m, :], groups(sqr[:, m % 2, :]), AX, ALU.add).then_inc(ln_var, 1)

        def ln_scalar_b(a, m):
            a.wait_ge(ln_var, m + 1)
            a.activation(ln_l[:, m, :], ln_v[:, m, :], ACT.Ln, bias=eps_col[:, 0:1], scale=1.0 / DIM).then_inc(ln_log, 1)
            a.wait_ge(ln_log, m + 1)
            a.activation(ln_r[:, m, :], ln_l[:, m, :], ACT.Exp, scale=-0.5).then_inc(ln_rstd, 1)

        def ln_vector_c(v, m):
            v.wait_ge(ln_rstd, m + 1)
            if m >= 2:
                wait_ln_turned(v, m - 2)
            v.tensor_tensor(groups(xhat[:, m % 2, :]), groups(cen[:, m % 2, :]), deep(ln_r[:, m, :], DIM), ALU.mult)\
                .then_inc(ln_done, 1)

        @block.vector
        def _(v):
            v.memset(eps_col[:, 0:1], LN_EPS)
            v.memset(eps_col[:, 1:2], 4 * LN_EPS)
            v.memset(eps_col[:, 2:3], 0.0).then_inc(eps_set, 1)
            v.memset(xn_t[64:128, :, :, :], 0.0).then_inc(xn_ones, 1)
            v.wait_ge(xn_ones, 1)
            v.memset(xn_t[64:65, :, :, :], 1.0).then_inc(xn_ones, 1)
            v.wait_ge(consts_in, 16)
            v.wait_ge(params_in, 16)
            v.wait_ge(cols_in, 16)
            for d, n in enumerate("ji"):
                v.tensor_tensor(w_sig[d][:, :], par(f"wqkv_{n}"), cst("sign"), ALU.mult).then_inc(w_signed, 1)
                v.wait_ge(w_signed, d + 1)
                v.tensor_scalar(w_att[d][:, 0:128], w_sig[d][:, 0:128], col(f"ga_{n}"), None, ALU.mult).then_inc(w_scaled, 1)
                v.tensor_scalar(w_att[d][:, 128:320], w_sig[d][:, 128:320], col(f"gb_{n}"), None, ALU.mult).then_inc(w_scaled, 1)
            v.tensor_tensor(w_ops[:, :], par("w_out"), par("norm_w"), ALU.mult).then_inc(out_scaled, 1)
            for d in range(2):
                v.wait_ge(bias_row, d + 1)
                v.wait_ge(w_scaled, 2 * d + 2)
                v.tensor_copy(w_att[d][64:65, :], RING[d][64:65, 0:320]).then_inc(w_ready, 1)
            for q in range(CHUNKS + 2):
                if q < CHUNKS:
                    v.wait_ge(x_in[q], 64)
                    if q >= 2:
                        pass
                    ln_vector_a(v, q)
                if 1 <= q <= CHUNKS:
                    ln_vector_b(v, q - 1)
                    ln_vector_c(v, q - 1)
            v.wait_ge(out_folded, 1)
            for hh in range(2):
                for s in range(2):
                    last = v.tensor_scalar(w_ofd[:, hh, s, :], bank[2][:, DIM * hh:DIM * hh + DIM],
                                           cst("sp_mask")[:, s:s + 1], None, ALU.mult)
            last.then_inc(w_out_ready, 1)

            for k, n in enumerate(("ff", "fc1", "fc2")):
                v.tensor_tensor(nrm_q[:, k, :], par(f"{n}_v"), par(f"{n}_v"), ALU.mult).then_inc(nrm_sq, 1)
            v.wait_ge(nrm_sq, 3)
            v.tensor_reduce(nrm_s[:, :], nrm_q[:, :, :], AX, ALU.add).then_inc(nrm_sum, 1)
            v.wait_ge(nrm_rs, 1)
            for k, n in enumerate(("ff", "fc1", "fc2")):
                v.tensor_tensor(nrm_g[:, k:k + 1], nrm_r[:, k:k + 1], col(f"{n}_g"), ALU.mult).then_inc(nrm_ready, 1)
            v.wait_ge(a_exped, 1)
            v.tensor_scalar(a_neg[:, :], a_exp[:, :], -1.0, None, ALU.mult).then_inc(a_ready, 1)
            v.tensor_scalar(d_half[:, :], par("d_par"), 0.5, None, ALU.mult).then_inc(d_ready, 1)
            v.tensor_tensor(w_xdt[:, 0:INNER], par("w_xbc")[:, 0:INNER], par("tap_a")[:, 0:INNER], ALU.mult).then_inc(taps_ready, 1)
            v.tensor_copy(w_xdt[:, INNER:INNER + SSM_H], par("w_dt")).then_inc(taps_ready, 1)
            v.tensor_tensor(w_xb[:, :], par("w_xbc")[:, 0:INNER], par("tap_b")[:, 0:INNER], ALU.mult).then_inc(taps_ready, 1)
            v.tensor_tensor(w_bca[:, :], par("w_xbc")[:, INNER:], par("tap_a")[:, INNER:], ALU.mult).then_inc(taps_ready, 1)
            v.tensor_tensor(w_bcb[:, :], par("w_xbc")[:, INNER:], par("tap_b")[:, INNER:], ALU.mult).then_inc(taps_ready, 1)

            def att_use(use):
                kind, g = use
                if kind in ("qA", "qB", "kA", "kB"):
                    slot = ("qA", "qB", "kA", "kB").index(kind)
                    table = ("cos_", "sin_")[slot % 2] + "ji"[g // CHUNKS]
                    src = filled(v, use)
                    if g >= 1:
                        if slot < 2:
                            v.wait_ge(q_ready, 2 * g)
                        else:
                            v.wait_ge(k_added, g)
                    v.tensor_tensor(rot[:, slot, :].rearrange("p (t j) -> p t j", j=GRID),
                                    src[:, :].rearrange("p (t j) -> p t j", j=GRID), wide(par(table)), ALU.mult)\
                        .then_inc(rotated, 1)
                elif kind in ("vt0", "vt1"):
                    half = int(kind[2])
                    src = filled(v, use)
                    if half == 0 and g >= 2:
                        v.wait_ge(av_done, 4 * (g - 2) + 4)
                    v.tensor_tensor(v_bd[:, g % 2, 4 * half:4 * half + 4, :],
                                    src[:, :].rearrange("p (t n) -> p t n", n=P), wide(cst("v_mask"), 4), ALU.mult)\
                        .then_inc(v_ready, 1)

            for use in att_steps[-1]:
                att_use(use)
            for n in range(ATT_STEPS):
                for use in att_steps[n]:
                    att_use(use)
                g = (n - 9) // 4
                if n % 4 == 1 and 0 <= g < ATT_CHUNKS:
                    v.wait_ge(wo_exped, g + 1)
                    v.scalar_tensor_tensor(y_t[:, g // CHUNKS, g % CHUNKS, :], wo_b[:, :], 0.0, wo_e[:, :], ALU.max, ALU.add)\
                        .then_inc(y_ready, 1)
                if n < PAIRS:
                    v.wait_ge(scored, n + 1)
                    sc = SCORE[n % 2][:, :].rearrange("p (h j) -> p h j", j=GRID)
                    v.tensor_reduce(s_max[:, n % 2, :], sc, AX, ALU.max).then_inc(s_maxed, 1)
                    v.wait_ge(s_maxed, n + 1)
                    if n >= 2:
                        v.wait_ge(exped, n - 1)
                    v.tensor_tensor(s_cen[:, n % 2, :, :], sc, deep(s_max[:, n % 2, :], GRID), ALU.subtract)\
                        .then_inc(s_centred, 1)
                e = n - 3
                if 0 <= e < PAIRS:
                    g, slot = divmod(e, 4)
                    v.wait_ge(z_inverted, e + 1)
                    if slot == 0 and g >= 2:
                        filled(v, ("wo", g - 2))
                    v.tensor_tensor(o_t[:, g % 2, 2 * slot:2 * slot + 2, :].rearrange("p t j -> p (t j)"),
                                    OZ[e % 2][:, 0:128], z_inv[:, e % 2, :], ALU.mult).then_inc(o_ready, 1)

            v.wait_ge(y_ready, ATT_CHUNKS)
            v.memset(ut_a[64:128, :, :, 0:1], 0.0).then_inc(u_starts, 1)
            v.memset(ut_b[0:64, :, :, 0:2], 0.0).then_inc(u_starts, 1)
            v.memset(ut_b[64:128, :, :, 0:3], 0.0).then_inc(u_starts, 1)
            for q in range(CHUNKS + 1):
                if q < CHUNKS:
                    src = filled(v, ("xt", q))
                    v.wait_ge(x_halved, q + 1)
                    v.scalar_tensor_tensor(x_of(0, q), src[:, :], 0.5, back[:, 4 * q:4 * q + 4, :].rearrange("p u n -> p (u n)"),
                                           ALU.mult, ALU.add).then_inc(x1_ready, 1)
                    v.wait_ge(x1_ready, q + 1)
                    ln_vector_a(v, CHUNKS + q)
                if q >= 1:
                    ln_vector_b(v, CHUNKS + q - 1)
                    ln_vector_c(v, CHUNKS + q - 1)

            def z_use(use):
                hh, c = int(use[0][1]), use[1]
                src = filled(v, use)
                v.wait_ge(z_tanh, 2 * c + hh + 1)
                if c >= 2:
                    v.wait_ge(gated, 2 * (c - 2) + 2)
                v.scalar_tensor_tensor(z_s[:, c % 2, hh, :, :].rearrange("p t j -> p (t j)"), z_th[:, hh, :], 1.0, src[:, :],
                                       ALU.add, ALU.mult).then_inc(z_ready, 1)

            def bc_silu(c):
                v.wait_ge(bc_tanh, c + 1)
                if c >= 2:
                    v.wait_ge(g_scored, 2 * (c - 2) + 2)
                for dst, rows, ready in ((b_s, slice(0, 64), b_ready), (c_s, slice(64, 128), c_ready)):
                    v.scalar_tensor_tensor(dst[:, c % 2, :], b_c[rows, 1, :], 1.0, b_c[rows, 0, :], ALU.add, ALU.mult)\
                        .then_inc(ready, 1)

            def x_silu(k):
                v.wait_ge(xth_ready, k + 1)
                at = xv[:, 4 * k:4 * k + 4, :].rearrange("p t n -> p (t n)")
                v.scalar_tensor_tensor(at, xth[:, k % 2, :, :].rearrange("p t n -> p (t n)"), 1.0, at, ALU.add, ALU.mult)\
                    .then_inc(xs_ready, 1)

            z_use(("z0", 0))
            z_use(("z1", 0))
            bc_silu(0)
            for n in range(TILES // 2):
                src = filled(v, ("xp", n))[:, 0:2 * (INNER + SSM_H)].rearrange("p (t w) -> p t w", t=2)
                v.tensor_tensor(xv[:, 2 * n:2 * n + 2, :], src[:, :, 0:INNER], wide(par("conv_bx"), 2), ALU.add).then_inc(xv_ready, 1)
                v.tensor_tensor(dt_all[:, 0, 2 * SSM_H * n:2 * SSM_H * (n + 1)].rearrange("p (t h) -> p t h", t=2),
                                src[:, :, INNER:INNER + SSM_H], wide(par("dt_bias"), 2), ALU.add).then_inc(dtv_ready, 1)
                if n % 2 and n >= 3:
                    x_silu(n // 2 - 1)
            x_silu(TILES // 4 - 1)

            D = [dt_all[:, k, :] for k in range(9)]
            v.wait_ge(dtv_ready, TILES // 2)
            v.scalar_tensor_tensor(D[1], D[0], -1.0, D[0], ALU.mult, ALU.max).then_inc(dt_chain, 1)
            v.wait_ge(dt_act, 1)
            v.tensor_scalar(D[3], D[2], 1.0, None, ALU.add).then_inc(dt_chain, 1)
            v.wait_ge(dt_chain, 2)
            v.scalar_tensor_tensor(D[5], D[3], -1.0, D[2], ALU.add, ALU.subtract).then_inc(dt_chain, 1)
            v.reciprocal(D[6], D[3]).then_inc(dt_chain, 1)
            v.wait_ge(dt_chain, 4)
            v.tensor_tensor(D[7], D[5], D[6], ALU.mult).then_inc(dt_chain, 1)
            v.wait_ge(dt_chain, 5)
            v.wait_ge(dt_act, 2)
            v.tensor_tensor(D[8], D[4], D[7], ALU.subtract).then_inc(dt_chain, 1)
            v.wait_ge(dt_chain, 6)
            v.scalar_tensor_tensor(D[1], D[0], 0.0, D[8], ALU.max, ALU.add).then_inc(dt_chain, 1)
            v.wait_ge(dt_chain, 7)
            v.tensor_tensor(D[2].rearrange("p (t h) -> p t h", h=SSM_H), D[1].rearrange("p (t h) -> p t h", h=SSM_H),
                            wide(a_neg[:, :], TILES), ALU.mult).then_inc(dt_ready, 1)
            v.tensor_scalar(D[3], D[1], 0.5, None, ALU.mult).then_inc(dt_ready, 1)

            for m in range(SSM_STEPS):
                for use in ssm_steps[m]:
                    kind, c = use
                    if kind in ("z0", "z1"):
                        z_use(use)
                    elif kind == "op":
                        src = filled(v, use)
                        v.wait_ge(rms_ready, c + 1)
                        v.tensor_tensor(y_n, src[:, :], rms_r, ALU.mult).then_inc(y_normed, 1)
                        v.wait_ge(y_normed, c + 1)
                        v.tensor_scalar(y_o, y_n, nrm_g[:, 0:1], col("ff_b"), ALU.mult, ALU.add).then_inc(yo_ready, 1)
                    elif kind == "yo":
                        src = filled(v, use)
                        v.tensor_tensor(x_of(0, c), x_of(0, c), src[:, :], ALU.add).then_inc(z1_ready, 1)
                        v.wait_ge(z1_ready, c + 1)
                        ln_vector_a(v, 2 * CHUNKS + c)
                    elif kind == "f2":
                        src = filled(v, use)
                        v.tensor_scalar(f_2, src[:, :], nrm_g[:, 2:3], col("fc2_b"), ALU.mult, ALU.add).then_inc(f2_ready, 1)
                    elif kind == "fo":
                        src = filled(v, use)
                        v.tensor_tensor(x_of(0, c), x_of(0, c), src[:, :], ALU.add).then_inc(o_added, 1)
                if m % CT == 3 and m // CT + 1 < CHUNKS:
                    bc_silu(m // CT + 1)
                if m < TILES and m % 4 == 0:
                    k = m // 4
                    v.wait_ge(g_scored, k + 1)
                    if k >= 2:
                        v.wait_ge(mixed, 4 * (k - 2) + 4)
                    v.tensor_tensor(g_m[:, k % 2, :, :], GB[k % 2][:, 0:4 * GRID].rearrange("p (t j) -> p t j", j=GRID),
                                    wide(cst("tri_quarter"), 4), ALU.mult).then_inc(g_masked, 1)
                e = m - 1
                if 0 <= e < TILES:
                    v.wait_ge(dec_exped, e + 1)
                    if e % 4 == 0:
                        v.wait_ge(g_masked, e // 4 + 1)
                    if e >= 2:
                        v.wait_ge(y_summed, e - 1)
                    v.tensor_tensor(mix[:, e % 2, :, :], dec[:, e % 2, :, :], wide(g_m[:, e // 4 % 2, e % 4, :], SSM_H), ALU.mult)\
                        .then_inc(mixed, 1)
                k, rest = divmod(m - 6, 4)
                if rest == 0 and 0 <= k < TILES // 4:
                    c = k // 2
                    v.wait_ge(y_summed, 4 * k + 4)
                    v.wait_ge(z_ready, 2 * c + 2)
                    if c >= 2:
                        filled(v, ("op", c - 2))
                    half = 4 * (k % 2)
                    v.tensor_tensor(y_g[:, c % 2, :, half:half + 4, :], YT[k % 2][:, :].rearrange("p (t h j) -> p h t j", t=4, h=2),
                                    z_s[:, c % 2, :, half:half + 4, :], ALU.mult).then_inc(gated, 1)
                c, rest = divmod(m - OUT_LAG - 3, CT)
                if rest == 0 and 0 <= c < CHUNKS:
                    ln_vector_b(v, 2 * CHUNKS + c)
                    ln_vector_c(v, 2 * CHUNKS + c)

        @block.scalar
        def _(a):
            a.preload_act_table_set("natural_log_exp_and_others")
            a.wait_ge(eps_set, 1)
            for q in range(CHUNKS + 1):
                if q < CHUNKS:
                    ln_scalar_a(a, q)
                if q >= 1:
                    ln_scalar_b(a, q - 1)
                    a.wait_ge(ln_turned, q)
                    for m in range(2):
                        a.activation(xn_t[0:64, CT * (q - 1):CT * q, m, :],
                                     bank[3 + q][64 * m:64 * m + 64, :].rearrange("p (t j) -> p t j", j=GRID),
                                     ACT.Identity).then_inc(xn_ready, 1)
            a.wait_ge(params_in, 16)
            a.activation(a_exp[:, :], par("a_log"), ACT.Exp).then_inc(a_exped, 1)
            a.wait_ge(nrm_sum, 1)
            a.activation(nrm_l[:, :], nrm_s[:, :], ACT.Ln).then_inc(nrm_log, 1)
            a.wait_ge(nrm_log, 1)
            a.activation(nrm_r[:, :], nrm_l[:, :], ACT.Exp, scale=-0.5).then_inc(nrm_rs, 1)
            a.wait_ge(cols_in, 16)

            def att_use(use):
                kind, g = use
                if kind == "v":
                    src = filled(a, use)
                    if g >= 1:
                        filled(a, ("vt1", g - 1))
                    a.activation(v_dup[:, :, :, :], src[:, :].rearrange("p (t j) -> p t j", j=GRID).unsqueeze(2)
                                 .broadcast_to([P, CT, 2, GRID]), ACT.Identity).then_inc(v_duped, 1)
                elif kind == "wo":
                    src = filled(a, use)
                    if g >= 1:
                        a.wait_ge(y_ready, g)
                        a.wait_ge(wo_clipped, g)
                    a.activation(wo_b[:, :], src[:, :], ACT.Identity, bias=col("bo_" + "ji"[g // CHUNKS])).then_inc(wo_biased, 1)
                elif kind == "yt":
                    src = filled(a, use)
                    a.activation(y_tok[:, g, :], src[:, :], ACT.Identity).then_inc(y_turned, 1)

            for use in att_steps[-1]:
                att_use(use)
            for n in range(ATT_STEPS):
                for use in att_steps[n]:
                    att_use(use)
                if n < PAIRS:
                    a.wait_ge(s_centred, n + 1)
                    if n >= 2:
                        a.wait_ge(p_turned, n - 1)
                    a.activation(prob[:, n % 2, :, :].rearrange("p k n -> p (k n)"),
                                 s_cen[:, n % 2, :, :].rearrange("p h j -> p (h j)"), ACT.Exp).then_inc(exped, 1)
                e = n - 1
                if 0 <= e < PAIRS:
                    a.wait_ge(p_turned, e + 1)
                    if e >= 2:
                        a.wait_ge(av_done, e - 1)
                    a.activation(prob_t[:, e % 2, :, :].rearrange("p k n -> p (k n)"), PT[e % 2][:, :], ACT.Identity)\
                        .then_inc(p_copied, 1)
                e = n - 2
                if 0 <= e < PAIRS:
                    a.wait_ge(av_done, e + 1)
                    a.activation(z_log[:, e % 2, :], OZ[e % 2][:, 128:256], ACT.Ln).then_inc(z_logged, 1)
                    a.wait_ge(z_logged, e + 1)
                    if e >= 2:
                        a.wait_ge(o_ready, e - 1)
                    a.activation(z_inv[:, e % 2, :], z_log[:, e % 2, :], ACT.Exp, scale=-1.0).then_inc(z_inverted, 1)
                g = (n - 8) // 4
                if n % 4 == 0 and 0 <= g < ATT_CHUNKS:
                    a.wait_ge(wo_clipped, g + 1)
                    if g >= 1:
                        a.wait_ge(y_ready, g)
                    a.activation(wo_e[:, :], wo_n[:, :], ACT.Exp).then_inc(wo_exped, 1)

            for q in range(CHUNKS + 1):
                if q < CHUNKS:
                    ln_scalar_a(a, CHUNKS + q)
                if q >= 1:
                    ln_scalar_b(a, CHUNKS + q - 1)
                    src = filled(a, ("ut", q - 1))
                    a.wait_ge(y_ready, ATT_CHUNKS)
                    a.activation(u2[:, q - 1, :], src[:, :], ACT.Identity, bias=col("ln1_b"), scale=col("ln1_w")).then_inc(u2_ready, 1)

            def bc_use(c):
                src = filled(a, ("bc", c))
                if c >= 1:
                    a.wait_ge(c_ready, c)
                a.activation(b_c[:, 0, :], src[:, :], ACT.Identity, bias=col("conv_bbc")).then_inc(bc_biased, 1)
                a.wait_ge(bc_biased, c + 1)
                a.activation(b_c[:, 1, :], b_c[:, 0, :], ACT.Tanh, scale=0.5).then_inc(bc_tanh, 1)

            def z_use(use):
                hh, c = int(use[0][1]), use[1]
                src = filled(a, use)
                if c >= 1:
                    a.wait_ge(z_ready, 2 * (c - 1) + hh + 1)
                a.activation(z_th[:, hh, :], src[:, :], ACT.Tanh, scale=0.5).then_inc(z_tanh, 1)

            bc_use(0)
            z_use(("z0", 0))
            z_use(("z1", 0))
            for k in range(TILES // 4):
                a.wait_ge(xv_ready, 2 * k + 2)
                if k >= 2:
                    a.wait_ge(xs_ready, k - 1)
                a.activation(xth[:, k % 2, :, :], xv[:, 4 * k:4 * k + 4, :], ACT.Tanh, scale=0.5).then_inc(xth_ready, 1)
            a.preload_act_table_set("natural_log_exp_and_others")
            a.wait_ge(dt_chain, 1)
            a.activation(dt_all[:, 2, :], dt_all[:, 1, :], ACT.Exp, scale=-1.0).then_inc(dt_act, 1)
            a.wait_ge(dt_chain, 2)
            a.activation(dt_all[:, 4, :], dt_all[:, 3, :], ACT.Ln).then_inc(dt_act, 1)

            for m in range(SSM_STEPS):
                for use in ssm_steps[m]:
                    kind, c = use
                    if kind == "bc":
                        bc_use(c)
                    elif kind in ("z0", "z1"):
                        z_use(use)
                    elif kind == "ms":
                        a.preload_act_table_set("natural_log_exp_and_others")
                        src = filled(a, use)
                        a.activation(rms_l, src[:, :], ACT.Ln, bias=eps_col[:, 1:2]).then_inc(rms_logged, 1)
                        a.wait_ge(rms_logged, c + 1)
                        if c >= 1:
                            a.wait_ge(y_normed, c)
                        a.activation(rms_r, rms_l, ACT.Exp, scale=-0.5).then_inc(rms_ready, 1)
                    elif kind == "ht":
                        src = filled(a, use)
                        a.activation(h_t, src[:, :], ACT.Identity, bias=col("ln2_b"), scale=col("ln2_w")).then_inc(h_ready, 1)
                    elif kind == "f1":
                        src = filled(a, use)
                        a.wait_ge(nrm_ready, 3)
                        a.activation(f_1, src[:, :], ACT.Gelu, bias=col("fc1_b"), scale=nrm_g[:, 1:2]).then_inc(f1_ready, 1)
                    elif kind == "yo":
                        ln_scalar_a(a, 2 * CHUNKS + c)
                if m < TILES:
                    a.wait_ge(decayed, m + 1)
                    if m >= 2:
                        a.wait_ge(mixed, m - 1)
                    a.activation(dec[:, m % 2, :, :].rearrange("p h t -> p (h t)"), DEC[m % 2][:, :], ACT.Exp).then_inc(dec_exped, 1)
                c, rest = divmod(m - OUT_LAG + 1, CT)
                if rest == 0 and 0 <= c < CHUNKS:
                    a.wait_ge(gated, 2 * c + 2)
                    if c >= 1:
                        filled(a, ("ms", c - 1))
                    a.activation(y_sq.rearrange("p h t j -> p (h t j)"),
                                 y_g[:, c % 2, :, :, :].rearrange("p h t j -> p (h t j)"), ACT.Square).then_inc(y_squared, 1)
                c, rest = divmod(m - OUT_LAG - 3, CT)
                if rest == 0 and 0 <= c < CHUNKS:
                    a.preload_act_table_set("natural_log_exp_and_others")
                    ln_scalar_b(a, 2 * CHUNKS + c)

        @block.gpsimd
        def _(gp):
            gp.memset(q_bd[:, :, :, :, :], 0.0).then_inc(q_zeroed, 1)
            gp.wait_ge(q_zeroed, 1)
            gp.wait_ge(consts_in, 16)

            def rotary(g):
                gp.wait_ge(rotated, 4 * g + 2)
                if g >= 2:
                    gp.wait_ge(scored, 4 * (g - 2) + 4)
                for m in range(2):
                    rows = slice(64 * m, 64 * m + 64)
                    if m or g:
                        gp.wait_ge(q_ready, 2 * g + m)
                    gp.tensor_tensor(q_bd[rows, g % 2, :, m, :], rot[rows, 0, :].rearrange("p (t j) -> p t j", j=GRID),
                                     rot[rows, 1, :].rearrange("p (t j) -> p t j", j=GRID), ALU.add).then_inc(q_ready, 1)
                gp.wait_ge(q_ready, 2 * g + 2)
                gp.wait_ge(rotated, 4 * g + 4)
                if g >= 1:
                    gp.wait_ge(k_ready, 4 * g)
                gp.tensor_tensor(k_rot[:, :], rot[:, 2, :], rot[:, 3, :], ALU.add).then_inc(k_added, 1)
                gp.wait_ge(k_added, g + 1)
                for h in range(HEADS):
                    gp.tensor_scalar(k_bd[:, g % 2, h, :], k_rot[:, :], cst("head_mask")[:, h:h + 1], None, ALU.mult)\
                        .then_inc(k_ready, 1)

            def clip(g):
                gp.wait_ge(wo_biased, g + 1)
                if g >= 1:
                    gp.wait_ge(wo_exped, g)
                gp.tensor_scalar(wo_n[:, :], wo_b[:, :], 0.0, None, ALU.min).then_inc(wo_clipped, 1)

            rotary(0)
            rotary(1)
            for g in range(ATT_CHUNKS):
                if g + 2 < ATT_CHUNKS:
                    rotary(g + 2)
                clip(g)
            for q in range(CHUNKS):
                quarter = back[:, 4 * q:4 * q + 4, :].rearrange("p u n -> p (u n)")
                gp.wait_ge(back_in[q], 64)
                gp.tensor_scalar(quarter, quarter, 0.5, -1.0, ALU.mult, ALU.add).then_inc(halved, 1)
                gp.wait_ge(halved, q + 1)
                gp.wait_ge(x_in[q], 64)
                gp.tensor_tensor(quarter, quarter, x_of(0, q), ALU.add).then_inc(x_halved, 1)

            gp.wait_ge(y_ready, ATT_CHUNKS)
            gp.memset(dtx[:, :, :, :, :, :], 0.0).then_inc(ssm_zeroed, 1)
            gp.memset(d_x[:, :, :, :, :, :], 0.0).then_inc(ssm_zeroed, 1)
            gp.wait_ge(ssm_zeroed, 2)
            gp.wait_ge(dt_ready, 2)
            gp.wait_ge(d_ready, 1)

            def scale_x(k, part):
                if part == 0:
                    gp.wait_ge(xs_ready, k + 1)
                    if k >= 2:
                        gp.wait_ge(y_summed, 4 * (k - 2) + 4)
                if k or part:
                    gp.wait_ge(x_scaled, 4 * k + part)
                s, which = part % 2, part // 2
                rows = slice(64 * s, 64 * s + 64)
                xs = xv[rows, 4 * k:4 * k + 4, :].rearrange("p t (h n) -> p t h n", h=SSM_H)
                if which == 0:
                    by = dt_all[rows, 3, 4 * SSM_H * k:4 * SSM_H * (k + 1)].rearrange("p (t h) -> p t h", t=4)\
                        .unsqueeze(3).broadcast_to([64, 4, SSM_H, SSM_P])
                else:
                    by = d_half[rows, :].unsqueeze(1).unsqueeze(3).broadcast_to([64, 4, SSM_H, SSM_P])
                gp.tensor_tensor((dtx, d_x)[which][rows, k % 2, :, :, s, :], xs, by, ALU.mult).then_inc(x_scaled, 1)

            for part in range(4):
                scale_x(0, part)
            for m in range(TILES):
                if m >= 2:
                    gp.wait_ge(decayed, m - 1)
                gp.wait_ge(x_scaled, min(max(m - 2, 0) + 4, TILES))
                gp.tensor_tensor(a_msk[:, m % 2, :, :], deep(dt_all[:, 2, SSM_H * m:SSM_H * (m + 1)], GRID), wide(cst("tri"), SSM_H),
                                 ALU.mult).then_inc(a_masked, 1)
                k, part = divmod(m + 2, 4)
                if 1 <= k < TILES // 4:
                    gp.wait_ge(a_masked, m + 1)
                    scale_x(k, part)


def constants():
    co, width = offsets(CONSTS)
    c = np.zeros((P, width), np.float32)
    row = np.arange(P)
    half, pos = row // 64, row % 64

    def put(name, value):
        c[:, co[name][0]:co[name][1]] = value

    put("ident", np.eye(P))
    n = np.arange(DIM)
    swap = np.where(n % 2 == 0, -1.0, 1.0)
    put("sign", np.concatenate([np.ones(DIM), swap, np.ones(2 * DIM), swap])[None, :])
    put("head_mask", (pos[:, None] // HD) == np.arange(HEADS)[None, :])
    m = np.arange(P)
    put("v_mask", half[:, None] == (m[None, :] // HD % 2))
    t = np.arange(GRID)
    put("tri", pos[:, None] <= t[None, :])
    put("tri_quarter", 0.25 * (pos[:, None] <= t[None, :]))
    put("later", (half[:, None] == half[None, :]) & (pos[:, None] > pos[None, :]))
    put("ident2", pos[:, None] == t[None, :])
    sp = row // SSM_P % 2
    put("mean_bd", (sp[:, None] == half[None, :]) / INNER)
    put("sp_mask", sp[:, None] == np.arange(2)[None, :])
    return c


def stack(*rows):
    a = np.concatenate(rows, axis=0)
    return np.concatenate([a, np.zeros((P - a.shape[0], a.shape[1]), a.dtype)], axis=0)


def two(w):
    z = np.zeros_like(w)
    return np.concatenate([np.concatenate([w, z], 1), np.concatenate([z, w], 1)], 0)


def pack(inp):
    po, n_params = offsets(PARAMS)
    lo, n_cols = offsets(COLS)
    p = np.zeros((P, n_params), np.float32)
    c = np.zeros((P, n_cols), np.float32)
    l0 = lambda n: inp["L0_conv_" + n]
    l1 = lambda n: inp["L1_conv_" + n]

    def put(name, value):
        p[:, po[name][0]:po[name][1]] = value

    def put_col(name, value):
        c[:value.shape[0], lo[name][0]] = value

    pair = np.arange(DIM) ^ 1
    for d in "ji":
        wq, wkv = l0(f"Wq_{d}"), l0(f"Wkv_{d}")
        wk, wv = wkv[:, :DIM], wkv[:, DIM:]
        put(f"wqkv_{d}", stack(np.concatenate([wq, wq[:, pair], wk, wv, wk[:, pair]], 1)))
        wo = l0(f"Wo_{d}").reshape(HD, HEADS, DIM).transpose(1, 0, 2).reshape(DIM, DIM)
        put(f"wo_{d}", two(wo))
        for t in ("cos", "sin"):
            put(f"{t}_{d}", np.tile(l0(f"{t}_{d}")[0].T, (2 * HEADS, 1)))
        for k in ("ga", "ba", "gb", "bb"):
            put_col(f"{k}_{d}", l0(k[0] + d + k[1]))
        put_col(f"bo_{d}", np.tile(l0(f"bo_{d}"), 2))
    w = l1("in_proj_w").T
    xbc = w[:, INNER:2 * INNER + 2 * STATE]
    put("w_xbc", np.concatenate([xbc, xbc], 0))
    taps = l1("conv_w")
    put("tap_a", np.repeat(np.stack([taps[:, 3], taps[:, 2]]), DIM, axis=0))
    put("tap_b", np.repeat(np.stack([taps[:, 1], taps[:, 0]]), DIM, axis=0))
    put("w_dt", stack(w[:, 2 * INNER + 2 * STATE:]))
    wz = w[:, :INNER].reshape(DIM, 2, 4, SSM_P)
    z = np.zeros((2, DIM, 2, 4, 2, SSM_P), np.float32)
    z[0, :, :, :, 0], z[1, :, :, :, 1] = wz, wz
    put("w_z", z.reshape(P, 2 * P))
    spread = lambda a: np.repeat(a.reshape(a.shape[0], 2, 4, 1, SSM_P), 2, axis=3).reshape(a.shape[0], 2 * P)
    put("w_out", stack(spread(l1("out_proj_w"))))
    put("norm_w", np.repeat(spread(l1("ssm_norm_w")[None, :]), P, axis=0))
    put("ff_vt", stack(l1("ff_v").T))
    for n in ("fc1", "fc2"):
        put(f"{n}_vt", two(l1(f"{n}_v").T))
    for n in ("ff", "fc1", "fc2"):
        put(f"{n}_v", np.concatenate([l1(f"{n}_v")] * 2, 0))
        put_col(f"{n}_g", np.tile(l1(f"{n}_g"), 2))
        put_col(f"{n}_b", np.tile(l1(f"{n}_b"), 2))
    put("conv_bx", np.repeat(l1("conv_b")[None, :INNER], P, axis=0))
    put("dt_bias", np.repeat(l1("dt_bias")[None, :], P, axis=0))
    put("a_log", np.repeat(l1("A_log")[None, :], P, axis=0))
    put("d_par", np.repeat(l1("D_param")[None, :], P, axis=0))
    for n in ("ln1_w", "ln1_b", "ln2_w", "ln2_b"):
        put_col(n, np.tile(l1(n), 2))
    bc = l1("conv_b")[INNER:]
    put_col("conv_bbc", np.concatenate([bc[:STATE], bc[:STATE], bc[STATE:], bc[STATE:]]))
    return p, c


def kernel(**inputs):
    import concourse.bacc as bacc
    from concourse.bass_utils import run_bass_kernel_spmd

    inp = {k: np.asarray(v) for k, v in inputs.items()}
    params, cols = pack(inp)
    arrays = {"x": np.ascontiguousarray(inp["x"]), "consts": constants(), "params": params, "cols": cols}
    nc = bacc.Bacc("TRN2", target_bir_lowering=False, num_devices=1)
    aps = {n: nc.dram_tensor(n, a.shape, mybir.dt.from_np(a.dtype), kind="ExternalInput").ap() for n, a in arrays.items()}
    out = nc.dram_tensor("out", (1, GRID, GRID, DIM), F32, kind="ExternalOutput").ap()
    build(nc, out=out, **aps)
    r = run_bass_kernel_spmd(nc, [arrays], core_ids=[0])
    return r.results[0]["out"]
```

```python
from contextlib import ExitStack

import numpy as np

import concourse.bass as bass
from concourse import mybir

F32 = mybir.dt.float32
ALU = mybir.AluOpType
ACT = mybir.ActivationFunctionType
AX = mybir.AxisListType.X

P = 128
GRID = 64
DIM = 64
HEADS, HD = 4, 16
SSM_H, SSM_P, STATE = 8, 16, 32
INNER = SSM_H * SSM_P
LN_EPS = 1e-5
TILES = GRID // 2
CT = 8
CHUNKS = TILES // CT
CW = CT * GRID
ATT_CHUNKS = 2 * CHUNKS
PAIRS = ATT_CHUNKS * CT // 2
ATT_STEPS = 40

CONSTS = dict(ident=P, swap_sign=1, head_mask=HEADS, v_mask=P, tri=GRID, tri_quarter=GRID,
              later=P, ident2=GRID, mean_bd=P, sp_mask=2)
PARAMS = dict(wqkv_j=5 * DIM, wqkv_i=5 * DIM, cos_j=GRID, sin_j=GRID, cos_i=GRID,
              sin_i=GRID, wo_j=P, wo_i=P, w_xbc=INNER + 2 * STATE, tap_a=INNER + 2 * STATE, tap_b=INNER + 2 * STATE,
              w_dt=SSM_H, w_z=2 * P, w_out=2 * P, norm_w=2 * P, ff_vt=DIM, fc1_vt=P, fc2_vt=P,
              ff_v=DIM, fc1_v=DIM, fc2_v=DIM, conv_bx=INNER, dt_bias=SSM_H, a_log=SSM_H, d_par=SSM_H)
COLS = dict(ga_j=1, ba_j=1, gb_j=1, bb_j=1, ga_i=1, ba_i=1, gb_i=1, bb_i=1, bo_j=1, bo_i=1, ln1_w=1,
            ln1_b=1, ln2_w=1, ln2_b=1, ff_g=1, ff_b=1, fc1_g=1, fc1_b=1, fc2_g=1, fc2_b=1, conv_bbc=1)


def offsets(widths):
    at, out = 0, {}
    for name, w in widths.items():
        out[name] = (at, at + w)
        at += w
    return out, at


FOLD_STEP = 6
XT_STEP = (26, 30, 33, 36)
UT_STEP = (29, 33, 36, 39)
XP_STEP = (31, 31, 32, 32, 36, 36, 37, 37)


def attention_uses():
    steps = {-1: [(k, 0) for k in ("kA", "kB", "qA", "qB", "v", "vt0", "vt1")]}
    for n in range(PAIRS):
        g, slot = divmod(n, 4)
        uses = []
        if g + 1 < ATT_CHUNKS:
            uses += [(k, g + 1) for k in (("kA", "kB"), ("qA", "qB"), ("v",), ("vt0", "vt1"))[slot]]
        if slot == 2 and 2 <= g < 2 + CHUNKS:
            uses.append(("yt", g - 2))
        if slot == 3 and g >= 1:
            uses.append(("wo", g - 1))
        if n == FOLD_STEP:
            uses.append(("fold", 0))
        steps[n] = uses
    for n in range(PAIRS, ATT_STEPS):
        steps[n] = []
    for n in range(ATT_STEPS):
        steps[n] += [("ut", q) for q in range(CHUNKS) if UT_STEP[q] == n]
        steps[n] += [("xt", q) for q in range(CHUNKS) if XT_STEP[q] == n]
        steps[n] += [("xp", k) for k, at in enumerate(XP_STEP) if at == n]
    steps[PAIRS + 2].append(("wo", ATT_CHUNKS - 1))
    return steps


PROJ_STEP = (21, 23, 29, 35)
NORM_STEP = (24, 26, 32, 37)
MLP_STEP = (27, 27, 39, 39)
SQUARE_STEP = (19, 21, 28, 34)
SSM_STEPS = 44
SOFTPLUS_STEP = 8
DT_PARTS = ((0, 2 * len(XP_STEP)), (2 * len(XP_STEP), TILES))


def ssm_uses():
    before = [("bc", 0), ("z0", 0), ("z1", 0)]
    steps = {m: [] for m in range(SSM_STEPS)}
    for m in range(TILES // 2 - len(XP_STEP)):
        steps[m].append(("xp", len(XP_STEP) + m))
    for c in range(1, CHUNKS):
        steps[CT * (c - 1) + 2].append(("bc", c))
        steps[CT * (c - 1) + 3] += [("z0", c), ("z1", c)]
    for c in range(CHUNKS):
        steps[PROJ_STEP[c]] += [("ms", c), ("op", c)]
        steps[PROJ_STEP[c] + 1].append(("yo", c))
        steps[NORM_STEP[c]].append(("ht", c))
        steps[MLP_STEP[c]].append(("f1", c))
        steps[MLP_STEP[c] + 1 + c % 2].append(("f2", c))
        steps[MLP_STEP[c] + 2 + c % 2].append(("fo", c))
    return before, steps


def build(nc, x, consts, params, cols, out):
    co, n_consts = offsets(CONSTS)
    po, n_params = offsets(PARAMS)
    lo, n_cols = offsets(COLS)
    att_steps = attention_uses()
    ssm_before, ssm_steps = ssm_uses()
    order = [u for n in sorted(att_steps) for u in att_steps[n]] + ssm_before \
        + [u for m in range(SSM_STEPS) for u in ssm_steps[m]]
    ring_at = {use: r for r, use in enumerate(order)}

    x_v = x.rearrange("o (u t i) j c -> t i j (o u) c", t=2, i=2)
    out_v = out.rearrange("o (u t i) j c -> t i j (o u) c", t=2, i=2)
    turned = nc.dram_tensor("attention_j_turned", (GRID, GRID, DIM), F32, kind="Internal").ap()
    turned_w = turned.rearrange("i (u t j) c -> t i u (j c)", t=2, j=2)
    turned_r = turned.rearrange("(u t i) j c -> t i j u c", t=2, i=2)

    with ExitStack() as ctx:
        def sb(name, shape, where=ctx):
            return where.enter_context(nc.sbuf_tensor(name, shape, F32))

        def sem(name):
            return ctx.enter_context(nc.semaphore(name))

        bank = [ctx.enter_context(nc.psum_tensor(f"bank{b}", [P, CW], F32)) for b in range(8)]
        RING, SCORE, PT, OZ = bank[0:2], bank[2:4], bank[4:6], bank[6:8]
        DEC, YT, GB = bank[2:4], bank[4:6], bank[6:8]

        c_sb = sb("c_sb", [P, n_consts])
        p_sb = sb("p_sb", [P, n_params])
        l_sb = sb("l_sb", [P, n_cols])

        def cst(name):
            return c_sb[:, co[name][0]:co[name][1]]

        def par(name):
            return p_sb[:, po[name][0]:po[name][1]]

        def col(name, a=0, b=P):
            return l_sb[a:b, lo[name][0]:lo[name][1]]

        eps_col = sb("eps_col", [P, 3])
        x_tok = sb("x_tok", [P, 16, 2 * DIM])
        back = sb("back", [P, 16, 2 * DIM])
        cen = sb("cen", [P, 2, CW])
        sqr = sb("sqr", [P, 2, CW])
        xhat = sb("xhat", [P, 2, CW])
        ln_s = sb("ln_s", [P, 12, 8])
        ln_n = sb("ln_n", [P, 12, 8])
        ln_v = sb("ln_v", [P, 12, 8])
        ln_l = sb("ln_l", [P, 12, 8])
        ln_r = sb("ln_r", [P, 12, 8])
        y_t = sb("y_t", [P, 2, CHUNKS, CW])
        sin_s = [sb(f"sin_s{d}", [P, GRID]) for d in range(2)]
        w_att = [sb(f"w_att{d}", [P, 5 * DIM]) for d in range(2)]
        w_xdt = sb("w_xdt", [P, INNER + SSM_H])
        w_xb = sb("w_xb", [P, INNER])
        w_bca = sb("w_bca", [P, 2 * STATE])
        w_bcb = sb("w_bcb", [P, 2 * STATE])
        w_ops = sb("w_ops", [P, 2 * P])
        w_ofd = sb("w_ofd", [P, 2, 2, DIM])
        nrm_q = sb("nrm_q", [P, 3, DIM])
        nrm_s = sb("nrm_s", [P, 3])
        nrm_l = sb("nrm_l", [P, 3])
        nrm_r = sb("nrm_r", [P, 3])
        nrm_g = sb("nrm_g", [P, 3])
        a_neg = sb("a_neg", [P, SSM_H])
        a_exp = sb("a_exp", [P, SSM_H])
        d_half = sb("d_half", [P, SSM_H])

        att = ExitStack()
        xn_t = sb("xn_t", [P, TILES, 2, GRID], att)
        q_bd = sb("q_bd", [P, 2, CT, 2, GRID], att)
        k_bd = sb("k_bd", [P, 2, HEADS, CW], att)
        v_bd = sb("v_bd", [P, 2, CT, P], att)
        s_max = sb("s_max", [P, 2, 8], att)
        s_cen = sb("s_cen", [P, 2, 8, GRID], att)
        prob = sb("prob", [P, 2, 4, P], att)
        prob_t = sb("prob_t", [P, 2, 4, P], att)
        z_log = sb("z_log", [P, 2, P], att)
        z_inv = sb("z_inv", [P, 2, P], att)
        o_t = sb("o_t", [P, 2, CT, GRID], att)
        wo_b = sb("wo_b", [P, CW], att)
        wo_e = sb("wo_e", [P, CW], att)
        rot = sb("rot", [P, 4, CW], att)
        k_rot = sb("k_rot", [P, CW], att)
        v_dup = sb("v_dup", [P, CT, 2, GRID], att)
        y_tok = sb("y_tok", [P, CHUNKS, CW], att)
        att.close()

        ssm = ExitStack()
        ut_a = sb("ut_a", [P, TILES, 2, GRID], ssm)
        b_c = sb("b_c", [P, 2, CW], ssm)
        b_s = sb("b_s", [2 * STATE, 2, CW], ssm)
        c_s = sb("c_s", [2 * STATE, 2, CW], ssm)
        z_s = sb("z_s", [P, 2, 2, CT, GRID], ssm)
        a_msk = sb("a_msk", [P, 2, SSM_H, GRID], ssm)
        dec = sb("dec", [P, 2, SSM_H, GRID], ssm)
        mix = sb("mix", [P, 2, SSM_H, GRID], ssm)
        g_m = sb("g_m", [P, 2, 4, GRID], ssm)
        dtx = sb("dtx", [P, 2, 4, SSM_H, 2, SSM_P], ssm)
        d_x = sb("d_x", [P, 2, 4, SSM_H, 2, SSM_P], ssm)
        y_g = sb("y_g", [P, CHUNKS, 2, CT, GRID], ssm)
        u2 = sb("u2", [P, CHUNKS, CW], ssm)
        ut_b = sb("ut_b", [P, TILES, 2, GRID], ssm)
        xv = sb("xv", [P, TILES, INNER], ssm)
        dt_fin = sb("dt_fin", [P, 2, TILES * SSM_H], ssm)
        ssm.close()
        dt_tmp = y_t[:, 0, 0:3, :].rearrange("p a n -> p (a n)")[:, 0:5 * TILES * SSM_H].rearrange("p (k n) -> p k n", k=5)
        xth = [ap.rearrange("p (t n) -> p t n", t=4) for ap in (y_t[:, 1, 0, :], y_t[:, 0, 3, :])]
        y_sq = y_t[:, 0, 0:2, :].rearrange("p h (t j) -> p h t j", j=GRID)
        y_n, y_o = y_t[:, 0, 2, :], y_t[:, 0, 3, :]
        flat_back = [back[:, 4 * k:4 * k + 4, :].rearrange("p u n -> p (u n)") for k in range(4)]
        h_t, f_1 = flat_back[0:2], flat_back[2:4]
        rms_r, z_th, f_2, rms_l = y_t[:, 1, 0, :], y_t[:, 1, 1:3, :], y_t[:, 1, 1:3, :], y_t[:, 1, 3, :]

        consts_in = sem("consts_in")
        params_in = sem("params_in")
        cols_in = sem("cols_in")
        turned_out = sem("turned_out")
        out_done = sem("out_done")
        eps_set = sem("eps_set")
        q_zeroed = sem("q_zeroed")
        sin_signed = sem("sin_signed")
        late_in = sem("late_in")
        w_scaled = sem("w_scaled")
        bias_row = sem("bias_row")
        w_ready = sem("w_ready")
        taps_ready = sem("taps_ready")
        out_scaled = sem("out_scaled")
        out_folded = sem("out_folded")
        w_out_ready = sem("w_out_ready")
        nrm_sq = sem("nrm_sq")
        nrm_sum = sem("nrm_sum")
        nrm_log = sem("nrm_log")
        nrm_rs = sem("nrm_rs")
        nrm_ready = sem("nrm_ready")
        a_exped = sem("a_exped")
        a_ready = sem("a_ready")
        d_ready = sem("d_ready")
        xn_ones = sem("xn_ones")
        xn_ready = sem("xn_ready")
        ln_sum = sem("ln_sum")
        ln_negmean = sem("ln_negmean")
        ln_centred = sem("ln_centred")
        ln_squared = sem("ln_squared")
        ln_var = sem("ln_var")
        ln_log = sem("ln_log")
        ln_rstd = sem("ln_rstd")
        ln_done = sem("ln_done")
        ln_turned = sem("ln_turned")
        ring_filled = sem("ring_filled")
        rotated = sem("rotated")
        q_ready = sem("q_ready")
        k_added = sem("k_added")
        k_ready = sem("k_ready")
        v_duped = sem("v_duped")
        v_ready = sem("v_ready")
        scored = sem("scored")
        s_maxed = sem("s_maxed")
        s_centred = sem("s_centred")
        exped = sem("exped")
        p_turned = sem("p_turned")
        p_copied = sem("p_copied")
        av_done = sem("av_done")
        z_logged = sem("z_logged")
        z_inverted = sem("z_inverted")
        o_ready = sem("o_ready")
        wo_biased = sem("wo_biased")
        wo_exped = sem("wo_exped")
        y_ready = sem("y_ready")
        y_turned = sem("y_turned")
        halved = sem("halved")
        x_halved = sem("x_halved")
        u_starts = sem("u_starts")
        x1_ready = sem("x1_ready")
        u2_ready = sem("u2_ready")
        ut_here = sem("ut_here")
        ssm_zeroed = sem("ssm_zeroed")
        xv_ready = sem("xv_ready")
        dtv_ready = sem("dtv_ready")
        dt_chain = sem("dt_chain")
        dt_act = sem("dt_act")
        dt_ready = sem("dt_ready")
        xth_ready = sem("xth_ready")
        xs_ready = sem("xs_ready")
        x_scaled = sem("x_scaled")
        bc_biased = sem("bc_biased")
        bc_tanh = sem("bc_tanh")
        b_ready = sem("b_ready")
        c_ready = sem("c_ready")
        z_tanh = sem("z_tanh")
        z_ready = sem("z_ready")
        a_masked = sem("a_masked")
        decayed = sem("decayed")
        dec_exped = sem("dec_exped")
        g_scored = sem("g_scored")
        g_masked = sem("g_masked")
        mixed = sem("mixed")
        y_summed = sem("y_summed")
        gated = sem("gated")
        y_squared = sem("y_squared")
        squares_added = sem("squares_added")
        rms_logged = sem("rms_logged")
        rms_ready = sem("rms_ready")
        y_normed = sem("y_normed")
        yo_ready = sem("yo_ready")
        z1_ready = sem("z1_ready")
        h_ready = sem("h_ready")
        f1_ready = sem("f1_ready")
        f2_ready = sem("f2_ready")
        o_added = sem("o_added")
        x_in = [sem(f"x_in{q}") for q in range(CHUNKS)]
        back_in = [sem(f"back_in{q}") for q in range(CHUNKS)]
        ut_in = [sem(f"ut_in{q}") for q in range(CHUNKS)]
        block = ctx.enter_context(nc.Block())

        def filled(eng, use):
            r = ring_at[use]
            eng.wait_ge(ring_filled, r + 1)
            return RING[r % 2]

        def drained(eng, use):
            kind, g = use
            signal, count = {
                "v": (v_duped, g + 1), "kA": (rotated, 4 * g + 1), "kB": (rotated, 4 * g + 2),
                "qA": (rotated, 4 * g + 3), "qB": (rotated, 4 * g + 4), "vt0": (v_ready, 2 * g + 1),
                "vt1": (v_ready, 2 * g + 2), "wo": (wo_biased, g + 1), "yt": (y_turned, g + 1),
                "xt": (x1_ready, g + 1), "ut": (u2_ready, g + 1), "bc": (bc_biased, g + 1),
                "z0": (z_ready, 2 * g + 1), "z1": (z_ready, 2 * g + 2), "xp": (dtv_ready, g + 1),
                "ms": (rms_logged, g + 1), "op": (y_normed, g + 1), "yo": (z1_ready, g + 1),
                "ht": (h_ready, g + 1), "f1": (f1_ready, g + 1), "f2": (f2_ready, g + 1),
                "fo": (o_added, g + 1), "fold": (w_out_ready, 1)}[kind]
            eng.wait_ge(signal, count)

        def x_of(layer, q):
            return x_tok[:, 4 * q:4 * q + 4, :].rearrange("p u n -> p (u n)")

        def groups(ap):
            return ap.rearrange("p (a c) -> p a c", c=DIM)

        def xn_cols(d, c, sp):
            if d == 0:
                flat = xn_t[:, :, :, :].rearrange("p t s (k r) -> p (t s) k r", r=2)
                return flat[:, :, CT * c:CT * c + CT, sp].rearrange("p i k -> p k i")
            return xn_t[:, CT * c:CT * c + CT, sp, :]

        def wide(ap, n=CT):
            return ap.unsqueeze(1).broadcast_to([ap.shape[0], n, ap.shape[1]])

        def deep(ap, n):
            return ap.unsqueeze(2).broadcast_to([ap.shape[0], ap.shape[1], n])

        HALVES = [(tau, ip) for tau in range(2) for ip in range(2)]

        def part_of(tile, q, tau, ip):
            return tile[64 * tau:64 * tau + 64, 4 * q:4 * q + 4, DIM * ip:DIM * ip + DIM]

        @block.sync
        def _(sp):
            for q in range(CHUNKS):
                for tau, ip in HALVES:
                    sp.dma_start(part_of(x_tok, q, tau, ip), x_v[tau, ip, :, 4 * q:4 * q + 4]).then_inc(x_in[q], 16)
                if q == 1:
                    sp.dma_start(c_sb[:, :], consts).then_inc(consts_in, 16)
            sp.dma_start(l_sb[:, :], cols).then_inc(cols_in, 16)
            late = po["w_xbc"][0]
            sp.dma_start(p_sb[:, :late], params[:, :late]).then_inc(params_in, 16)
            sp.dma_start(p_sb[:, late:], params[:, late:]).then_inc(late_in, 16)
            for g in range(CHUNKS):
                sp.wait_ge(y_turned, g + 1)
                for tau in range(2):
                    sp.dma_start(turned_w[tau, :, 4 * g:4 * g + 4],
                                 y_tok[64 * tau:64 * tau + 64, g, :].rearrange("p (u n) -> p u n", u=4)).then_inc(turned_out, 16)
            sp.wait_ge(turned_out, 32 * CHUNKS)
            for q in range(CHUNKS):
                for tau, ip in HALVES:
                    sp.dma_start(part_of(back, q, tau, ip), turned_r[tau, ip, :, 4 * q:4 * q + 4]).then_inc(back_in[q], 16)
            sp.wait_ge(u_starts, 3)
            for q in range(CHUNKS):
                sp.wait_ge(u2_ready, q + 1)
                for dst, half, shift in ((ut_a, 1, 1), (ut_b, 0, 2), (ut_b, 1, 3)):
                    for m in range(2):
                        src = u2[64 * m:64 * m + 64, q, :].rearrange("p (t j) -> p t j", j=GRID)
                        sp.dma_start(dst[64 * half:64 * half + 64, CT * q:CT * q + CT, m, shift:GRID],
                                     src[:, :, 0:GRID - shift]).then_inc(ut_in[q], 16)
            for q in range(CHUNKS):
                sp.wait_ge(o_added, q + 1)
                for tau, ip in HALVES:
                    sp.dma_start(out_v[tau, ip, :, 4 * q:4 * q + 4], part_of(x_tok, q, tau, ip)).then_inc(out_done, 16)
            sp.wait_ge(out_done, 64 * CHUNKS)

        @block.tensor
        def _(pe):
            def mm(dst, lhsT, rhs, start=True, stop=True):
                return pe.matmul(dst, lhsT, rhs, start=start, stop=stop, skip_group_check=True)

            pe.wait_ge(consts_in, 16)

            def turn(dst, src, last_sem=None):
                for k in range(4):
                    last = pe.transpose(dst[:, P * k:P * k + P], src[:, P * k:P * k + P], cst("ident"))
                return last

            for q in range(CHUNKS):
                pe.wait_ge(ln_done, q + 1)
                turn(bank[4 + q], xhat[:, q % 2, :]).then_inc(ln_turned, 1)

            pe.wait_ge(cols_in, 16)
            pe.wait_ge(params_in, 16)
            for d, n in enumerate("ji"):
                mm(RING[d][64:65, 0:128], col(f"ba_{n}"), par(f"wqkv_{n}")[:, 0:128])
                mm(RING[d][64:65, 128:320], col(f"bb_{n}"), par(f"wqkv_{n}")[:, 128:320]).then_inc(bias_row, 1)

            def take(use):
                r = ring_at[use]
                if r >= 2:
                    drained(pe, order[r - 2])
                return RING[r % 2]

            Q, RQ, K, V, RK = (slice(DIM * k, DIM * k + DIM) for k in range(5))

            def att_use(use):
                kind, g = use
                if kind in ("xt", "ut", "xp"):
                    ssm_use(use)
                    return
                dst = take(use)
                d, c = divmod(g, CHUNKS)
                if kind in ("v", "qA", "qB", "kA", "kB"):
                    part = {"v": V, "qA": Q, "qB": RQ, "kA": K, "kB": RK}[kind]
                    for m in range(2):
                        last = mm(dst[64 * m:64 * m + 64, :], w_att[d][:, part], xn_cols(d, c, m))
                elif kind in ("vt0", "vt1"):
                    if kind == "vt0":
                        pe.wait_ge(v_duped, g + 1)
                    half = int(kind[2])
                    last = turn(dst, v_dup[:, 4 * half:4 * half + 4, :, :].rearrange("p t r j -> p (t r j)"))
                elif kind == "wo":
                    pe.wait_ge(o_ready, 4 * g + 4)
                    last = mm(dst[:, :], par("wo_j" if d == 0 else "wo_i"),
                              o_t[:, g % 2, :, :].rearrange("p t j -> p (t j)"))
                elif kind == "yt":
                    pe.wait_ge(y_ready, g + 1)
                    last = turn(dst, y_t[:, 0, g, :])
                elif kind == "fold":
                    pe.wait_ge(out_scaled, 1)
                    for hh in range(2):
                        last = mm(dst[:, DIM * hh:DIM * hh + DIM], w_ops[:, P * hh:P * hh + P], par("ff_vt"))
                last.then_inc(ring_filled, 1)

            def ssm_use(use):
                kind, c = use
                dst = take(use)
                if kind == "xt":
                    pe.wait_ge(y_ready, CHUNKS + c + 1)
                    last = turn(dst, y_t[:, 1, c, :])
                elif kind == "ut":
                    pe.wait_ge(ln_done, CHUNKS + c + 1)
                    last = turn(dst, xhat[:, c % 2, :])
                elif kind == "bc":
                    pe.wait_ge(ut_in[c], 96)
                    pe.wait_ge(ut_here, 2 * c + 2)
                    for half, (w, u) in enumerate(((w_bca, ut_a), (w_bcb, ut_b))):
                        for part in range(2):
                            for m in range(2):
                                row = 64 * part + 32 * m
                                last = mm(dst[row:row + 32, :], w[:, STATE * part:STATE * part + STATE],
                                          u[:, CT * c:CT * c + CT, m, :], start=half == 0, stop=half == 1)
                elif kind in ("z0", "z1"):
                    hh = int(kind[1])
                    last = mm(dst[:, :], par("w_z")[:, P * hh:P * hh + P], u2[:, c, :])
                elif kind == "xp":
                    pe.wait_ge(ut_in[2 * c // CT], 96)
                    pe.wait_ge(ut_here, 2 * (2 * c // CT) + 2)
                    pe.wait_ge(taps_ready, 5)
                    for k in range(2):
                        t, w = 2 * c + k, INNER + SSM_H
                        mm(dst[:, w * k:w * k + INNER], ut_b[:, t, :, :].rearrange("p s j -> p (s j)"), w_xb[:, :],
                           start=True, stop=False)
                        last = mm(dst[:, w * k:w * k + w], ut_a[:, t, :, :].rearrange("p s j -> p (s j)"), w_xdt[:, :],
                                  start=False, stop=True)
                elif kind == "ms":
                    pe.wait_ge(squares_added, c + 1)
                    last = mm(dst[:, :], cst("mean_bd"), y_sq[:, 0, :, :].rearrange("p t j -> p (t j)"))
                elif kind == "op":
                    for hh in range(2):
                        last = mm(dst[:, :], w_ofd[:, hh, :, :].rearrange("p s c -> p (s c)"),
                                  y_g[:, c, hh, :, :].rearrange("p t j -> p (t j)"), start=hh == 0, stop=hh == 1)
                elif kind == "yo":
                    pe.wait_ge(yo_ready, c + 1)
                    last = turn(dst, y_o)
                elif kind == "ht":
                    pe.wait_ge(ln_done, 2 * CHUNKS + c + 1)
                    last = turn(dst, xhat[:, c % 2, :])
                elif kind == "f1":
                    pe.wait_ge(h_ready, c + 1)
                    last = mm(dst[:, :], par("fc1_vt"), h_t[c % 2])
                elif kind == "f2":
                    pe.wait_ge(f1_ready, c + 1)
                    last = mm(dst[:, :], par("fc2_vt"), f_1[c % 2])
                elif kind == "fo":
                    pe.wait_ge(f2_ready, c + 1)
                    last = turn(dst, f_2[:, c % 2, :])
                last.then_inc(ring_filled, 1)

            pe.wait_ge(w_ready, 2)
            pe.wait_ge(xn_ones, 2)
            pe.wait_ge(xn_ready, 2 * CHUNKS)
            for use in att_steps[-1]:
                att_use(use)
            for n in range(ATT_STEPS):
                if n < PAIRS:
                    g, slot = divmod(n, 4)
                    if slot == 0:
                        pe.wait_ge(q_ready, 2 * g + 2)
                        pe.wait_ge(k_ready, 4 * g + 4)
                    if n >= 2:
                        pe.wait_ge(s_centred, n - 1)
                    for k in range(2):
                        t = 2 * slot + k
                        last = mm(SCORE[n % 2][:, 256 * k:256 * k + 256],
                                  q_bd[:, g % 2, t, :, :].rearrange("p s i -> p (s i)"),
                                  k_bd[:, g % 2, :, GRID * t:GRID * t + GRID])
                    last.then_inc(scored, 1)
                for use in att_steps[n][:1]:
                    att_use(use)
                if 1 <= n <= PAIRS:
                    e = n - 1
                    pe.wait_ge(exped, e + 1)
                    if e >= 2:
                        pe.wait_ge(p_copied, e - 1)
                    turn(PT[e % 2], prob[:, e % 2, :, :].rearrange("p k n -> p (k n)")).then_inc(p_turned, 1)
                for use in att_steps[n][1:2]:
                    att_use(use)
                if 2 <= n <= PAIRS + 1:
                    e = n - 2
                    g, slot = divmod(e, 4)
                    pe.wait_ge(p_copied, e + 1)
                    if slot == 0:
                        pe.wait_ge(v_ready, 2 * g + 2)
                    if e >= 2:
                        pe.wait_ge(o_ready, e - 1)
                    pts = prob_t[:, e % 2, :, :].rearrange("p (t r) n -> p t r n", t=2)
                    for k in range(2):
                        for m in range(2):
                            for hp in range(2):
                                row = 64 * m + 32 * hp
                                mm(OZ[e % 2][row:row + 32, 64 * k:64 * k + 64],
                                   v_bd[:, g % 2, 2 * slot + k, row:row + 32], pts[:, k, hp, 64 * m:64 * m + 64])
                    for m in range(2):
                        for hp in range(2):
                            row = 64 * m + 32 * hp
                            last = mm(OZ[e % 2][row:row + 32, 128:256], cst("v_mask")[:, 0:32],
                                      pts[:, :, hp, 64 * m:64 * m + 64])
                    last.then_inc(av_done, 1)
                for use in att_steps[n][2:]:
                    att_use(use)

            for use in ssm_before:
                ssm_use(use)
            for m in range(SSM_STEPS):
                for use in ssm_steps[m]:
                    ssm_use(use)
                if m < TILES and m % 4 == 0:
                    k, c = m // 4, m // CT
                    if m % CT == 0:
                        pe.wait_ge(b_ready, c + 1)
                        pe.wait_ge(c_ready, c + 1)
                    if k >= 2:
                        pe.wait_ge(g_masked, k - 1)
                    for t in range(4):
                        at = GRID * ((m + t) % CT)
                        for s in range(2):
                            rows = slice(STATE * s, STATE * s + STATE)
                            last = mm(GB[k % 2][64 * s:64 * s + 64, GRID * t:GRID * t + GRID],
                                      b_s[rows, c % 2, at:at + GRID], c_s[rows, c % 2, at:at + GRID])
                    last.then_inc(g_scored, 1)
                if m < TILES:
                    pe.wait_ge(a_masked, m + 1)
                    if m >= 2:
                        pe.wait_ge(dec_exped, m - 1)
                    mm(DEC[m % 2][:, :], cst("later"), a_msk[:, m % 2, :, :].rearrange("p h t -> p (h t)"))\
                        .then_inc(decayed, 1)
                e = m - 2
                if 0 <= e < TILES:
                    k = e // 4
                    pe.wait_ge(mixed, e + 1)
                    if e % 4 == 0:
                        pe.wait_ge(x_scaled, 4 * k + 4)
                        if k >= 2:
                            pe.wait_ge(gated, k - 1)
                    for hh in range(2):
                        at = P * (e % 4) + GRID * hh
                        for term in range(2):
                            for h4 in range(4):
                                h = 4 * hh + h4
                                xs = (dtx, d_x)[term][:, k % 2, e % 4, h, :, :].rearrange("p s n -> p (s n)")
                                rhs = cst("ident2") if term else mix[:, e % 2, h, :]
                                last = mm(YT[k % 2][32 * h4:32 * h4 + 32, at:at + GRID], xs, rhs,
                                          start=term == 0, stop=term == 1)
                    last.then_inc(y_summed, 1)

        def wait_ln_turned(eng, m):
            if m < CHUNKS:
                eng.wait_ge(ln_turned, m + 1)
            else:
                filled(eng, ("ut" if m < 2 * CHUNKS else "ht", m % CHUNKS))

        def ln_vector_a(v, m):
            src = x_of(m // CHUNKS, m % CHUNKS)
            v.tensor_reduce(ln_s[:, m, :], groups(src), AX, ALU.add).then_inc(ln_sum, 1)
            v.wait_ge(ln_sum, m + 1)
            v.tensor_scalar(ln_n[:, m, :], ln_s[:, m, :], -1.0 / DIM, None, ALU.mult).then_inc(ln_negmean, 1)
            v.wait_ge(ln_negmean, m + 1)
            v.tensor_tensor(groups(cen[:, m % 2, :]), groups(src), deep(ln_n[:, m, :], DIM), ALU.add).then_inc(ln_centred, 1)

        def ln_scalar_a(a, m):
            a.wait_ge(ln_centred, m + 1)
            if m >= 2:
                a.wait_ge(ln_var, m - 1)
            a.activation(sqr[:, m % 2, :], cen[:, m % 2, :], ACT.Square).then_inc(ln_squared, 1)

        def ln_vector_b(v, m):
            v.wait_ge(ln_squared, m + 1)
            v.tensor_reduce(ln_v[:, m, :], groups(sqr[:, m % 2, :]), AX, ALU.add).then_inc(ln_var, 1)

        def ln_scalar_b(a, m):
            a.wait_ge(ln_var, m + 1)
            a.activation(ln_l[:, m, :], ln_v[:, m, :], ACT.Ln, bias=eps_col[:, 0:1], scale=1.0 / DIM).then_inc(ln_log, 1)
            a.wait_ge(ln_log, m + 1)
            a.activation(ln_r[:, m, :], ln_l[:, m, :], ACT.Exp, scale=-0.5).then_inc(ln_rstd, 1)

        def ln_vector_c(v, m):
            v.wait_ge(ln_rstd, m + 1)
            if m >= 2:
                wait_ln_turned(v, m - 2)
            v.tensor_tensor(groups(xhat[:, m % 2, :]), groups(cen[:, m % 2, :]), deep(ln_r[:, m, :], DIM), ALU.mult)\
                .then_inc(ln_done, 1)

        @block.vector
        def _(v):
            v.memset(eps_col[:, 0:1], LN_EPS)
            v.memset(eps_col[:, 1:2], 4 * LN_EPS)
            v.memset(eps_col[:, 2:3], 0.0).then_inc(eps_set, 1)
            for q in range(CHUNKS + 2):
                if q >= 2:
                    ln_vector_c(v, q - 2)
                if 1 <= q <= CHUNKS:
                    ln_vector_b(v, q - 1)
                if q < CHUNKS:
                    v.wait_ge(x_in[q], 64)
                    ln_vector_a(v, q)
            for d in range(2):
                v.wait_ge(bias_row, d + 1)
                v.wait_ge(w_scaled, 2 * d + 2)
                v.tensor_copy(w_att[d][64:65, :], RING[d][64:65, 0:320]).then_inc(w_ready, 1)
            v.wait_ge(sin_signed, 2)

            def late_weights():
                v.wait_ge(late_in, 16)
                v.wait_ge(cols_in, 16)
                v.tensor_tensor(w_ops[:, :], par("w_out"), par("norm_w"), ALU.mult).then_inc(out_scaled, 1)
                for k, n in enumerate(("ff", "fc1", "fc2")):
                    v.tensor_tensor(nrm_q[:, k, :], par(f"{n}_v"), par(f"{n}_v"), ALU.mult).then_inc(nrm_sq, 1)
                v.wait_ge(nrm_sq, 3)
                v.tensor_reduce(nrm_s[:, :], nrm_q[:, :, :], AX, ALU.add).then_inc(nrm_sum, 1)
                v.tensor_scalar(d_half[:, :], par("d_par"), 0.5, None, ALU.mult).then_inc(d_ready, 1)
                v.tensor_tensor(w_xdt[:, 0:INNER], par("w_xbc")[:, 0:INNER], par("tap_a")[:, 0:INNER], ALU.mult).then_inc(taps_ready, 1)
                v.tensor_copy(w_xdt[:, INNER:INNER + SSM_H], par("w_dt")).then_inc(taps_ready, 1)
                v.tensor_tensor(w_xb[:, :], par("w_xbc")[:, 0:INNER], par("tap_b")[:, 0:INNER], ALU.mult).then_inc(taps_ready, 1)
                v.tensor_tensor(w_bca[:, :], par("w_xbc")[:, INNER:], par("tap_a")[:, INNER:], ALU.mult).then_inc(taps_ready, 1)
                v.tensor_tensor(w_bcb[:, :], par("w_xbc")[:, INNER:], par("tap_b")[:, INNER:], ALU.mult).then_inc(taps_ready, 1)

            def late_scales():
                v.wait_ge(nrm_rs, 1)
                for k, n in enumerate(("ff", "fc1", "fc2")):
                    v.tensor_tensor(nrm_g[:, k:k + 1], nrm_r[:, k:k + 1], col(f"{n}_g"), ALU.mult).then_inc(nrm_ready, 1)
                v.wait_ge(a_exped, 1)
                v.tensor_scalar(a_neg[:, :], a_exp[:, :], -1.0, None, ALU.mult).then_inc(a_ready, 1)

            def softplus(part):
                first, end = DT_PARTS[part]
                cols_of = slice(SSM_H * first, SSM_H * end)
                T = [dt_tmp[:, k, cols_of] for k in range(5)]
                F = [dt_fin[:, k, cols_of] for k in range(2)]
                v.wait_ge(dtv_ready, end // 2)
                v.scalar_tensor_tensor(T[1], T[0], -1.0, T[0], ALU.mult, ALU.max).then_inc(dt_chain, 1)
                v.wait_ge(dt_act, 3 * part + 1)
                v.tensor_scalar(F[1], F[0], 1.0, None, ALU.add).then_inc(dt_chain, 1)
                v.wait_ge(dt_chain, 6 * part + 2)
                v.scalar_tensor_tensor(T[3], F[1], -1.0, F[0], ALU.add, ALU.subtract).then_inc(dt_chain, 1)
                v.wait_ge(dt_chain, 6 * part + 3)
                v.wait_ge(dt_act, 3 * part + 3)
                v.tensor_tensor(T[3], T[3], T[4], ALU.mult).then_inc(dt_chain, 1)
                v.wait_ge(dt_chain, 6 * part + 4)
                v.tensor_tensor(T[2], T[2], T[3], ALU.subtract).then_inc(dt_chain, 1)
                v.wait_ge(dt_chain, 6 * part + 5)
                v.scalar_tensor_tensor(T[1], T[0], 0.0, T[2], ALU.max, ALU.add).then_inc(dt_chain, 1)
                v.wait_ge(dt_chain, 6 * part + 6)
                v.wait_ge(a_ready, 1)
                v.tensor_tensor(F[0].rearrange("p (t h) -> p t h", h=SSM_H), T[1].rearrange("p (t h) -> p t h", h=SSM_H),
                                wide(a_neg[:, :], end - first), ALU.mult).then_inc(dt_ready, 1)
                v.tensor_scalar(F[1], T[1], 0.5, None, ALU.mult).then_inc(dt_ready, 1)

            def xp_use(n):
                src = filled(v, ("xp", n))[:, 0:2 * (INNER + SSM_H)].rearrange("p (t w) -> p t w", t=2)
                v.wait_ge(y_turned, CHUNKS)
                v.tensor_tensor(xv[:, 2 * n:2 * n + 2, :], src[:, :, 0:INNER], wide(par("conv_bx"), 2), ALU.add).then_inc(xv_ready, 1)
                v.tensor_tensor(dt_tmp[:, 0, 2 * SSM_H * n:2 * SSM_H * (n + 1)].rearrange("p (t h) -> p t h", t=2),
                                src[:, :, INNER:INNER + SSM_H], wide(par("dt_bias"), 2), ALU.add).then_inc(dtv_ready, 1)

            def att_use(use):
                kind, g = use
                if kind in ("qA", "qB", "kA", "kB"):
                    slot = ("kA", "kB", "qA", "qB").index(kind)
                    table = sin_s[g // CHUNKS][:, :] if slot % 2 else par("cos_" + "ji"[g // CHUNKS])
                    src = filled(v, use)
                    if g >= 1:
                        if slot < 2:
                            v.wait_ge(k_added, g)
                        else:
                            v.wait_ge(q_ready, 2 * g)
                    v.tensor_tensor(rot[:, slot, :].rearrange("p (t j) -> p t j", j=GRID),
                                    src[:, :].rearrange("p (t j) -> p t j", j=GRID), wide(table), ALU.mult)\
                        .then_inc(rotated, 1)
                elif kind in ("vt0", "vt1"):
                    half = int(kind[2])
                    src = filled(v, use)
                    if half == 0 and g >= 2:
                        v.wait_ge(av_done, 4 * (g - 2) + 4)
                    v.tensor_tensor(v_bd[:, g % 2, 4 * half:4 * half + 4, :],
                                    src[:, :].rearrange("p (t n) -> p t n", n=P), wide(cst("v_mask"), 4), ALU.mult)\
                        .then_inc(v_ready, 1)
                elif kind == "xt":
                    src = filled(v, use)
                    v.wait_ge(x_halved, g + 1)
                    v.scalar_tensor_tensor(x_of(0, g), src[:, :], 0.5, flat_back[g], ALU.mult, ALU.add).then_inc(x1_ready, 1)
                    v.wait_ge(x1_ready, g + 1)
                    ln_vector_a(v, CHUNKS + g)
                elif kind == "xp":
                    xp_use(g)
                elif kind == "fold":
                    src = filled(v, use)
                    for hh in range(2):
                        for s in range(2):
                            last = v.tensor_scalar(w_ofd[:, hh, s, :], src[:, DIM * hh:DIM * hh + DIM],
                                                   cst("sp_mask")[:, s:s + 1], None, ALU.mult)
                    last.then_inc(w_out_ready, 1)

            for use in att_steps[-1]:
                att_use(use)
            for n in range(ATT_STEPS):
                if n == FOLD_STEP - 1:
                    late_weights()
                if n == FOLD_STEP + 1:
                    late_scales()
                g = (n - 8) // 4
                if (n % 4 == 0 and 0 <= g < ATT_CHUNKS - 1) or n == PAIRS + 3:
                    g = min(g, ATT_CHUNKS - 1) if n < PAIRS else ATT_CHUNKS - 1 - (n == PAIRS)
                    v.wait_ge(wo_biased, g + 1)
                    v.scalar_tensor_tensor(y_t[:, g // CHUNKS, g % CHUNKS, :], wo_e[:, :], 1.0, wo_b[:, :], ALU.min, ALU.add)\
                        .then_inc(y_ready, 1)
                if n < PAIRS:
                    v.wait_ge(scored, n + 1)
                    sc = SCORE[n % 2][:, :].rearrange("p (h j) -> p h j", j=GRID)
                    v.tensor_reduce(s_max[:, n % 2, :], sc, AX, ALU.max).then_inc(s_maxed, 1)
                    v.wait_ge(s_maxed, n + 1)
                    if n >= 2:
                        v.wait_ge(exped, n - 1)
                    v.tensor_tensor(s_cen[:, n % 2, :, :], sc, deep(s_max[:, n % 2, :], GRID), ALU.subtract)\
                        .then_inc(s_centred, 1)
                for use in att_steps[n][:1]:
                    att_use(use)
                e = n - 3
                if 0 <= e < PAIRS:
                    g, slot = divmod(e, 4)
                    v.wait_ge(z_inverted, e + 1)
                    if slot == 0 and g >= 2:
                        filled(v, ("wo", g - 2))
                    v.tensor_tensor(o_t[:, g % 2, 2 * slot:2 * slot + 2, :].rearrange("p t j -> p (t j)"),
                                    OZ[e % 2][:, 0:128], z_inv[:, e % 2, :], ALU.mult).then_inc(o_ready, 1)
                for use in att_steps[n][1:]:
                    att_use(use)
                for q in range(CHUNKS):
                    if n == XT_STEP[q] + 1:
                        ln_vector_b(v, CHUNKS + q)
                    if n == UT_STEP[q] - 1:
                        ln_vector_c(v, CHUNKS + q)
                if n == XT_STEP[0] + 1:
                    filled(v, ("vt1", ATT_CHUNKS - 1))
                    v.wait_ge(turned_out, 32 * CHUNKS)
                    v.memset(ut_a[64:128, :, :, 0:1], 0.0).then_inc(u_starts, 1)
                    v.memset(ut_b[0:64, :, :, 0:2], 0.0).then_inc(u_starts, 1)
                    v.memset(ut_b[64:128, :, :, 0:3], 0.0).then_inc(u_starts, 1)
            softplus(0)

            def z_use(use):
                hh, c = int(use[0][1]), use[1]
                src = filled(v, use)
                v.wait_ge(z_tanh, 2 * c + hh + 1)
                if c >= 2:
                    v.wait_ge(gated, 2 * (c - 2) + 2)
                v.scalar_tensor_tensor(z_s[:, c % 2, hh, :, :].rearrange("p t j -> p (t j)"), z_th[:, hh, :], 1.0, src[:, :],
                                       ALU.add, ALU.mult).then_inc(z_ready, 1)

            def bc_silu(c):
                v.wait_ge(bc_tanh, c + 1)
                if c >= 2:
                    v.wait_ge(g_scored, 2 * (c - 2) + 2)
                for dst, rows, ready in ((b_s, slice(0, 64), b_ready), (c_s, slice(64, 128), c_ready)):
                    v.scalar_tensor_tensor(dst[:, c % 2, :], b_c[rows, 1, :], 1.0, b_c[rows, 0, :], ALU.add, ALU.mult)\
                        .then_inc(ready, 1)

            def x_silu(k):
                v.wait_ge(xth_ready, k + 1)
                at = xv[:, 4 * k:4 * k + 4, :].rearrange("p t n -> p (t n)")
                v.scalar_tensor_tensor(at, xth[k % 2].rearrange("p t n -> p (t n)"), 1.0, at, ALU.add, ALU.mult)\
                    .then_inc(xs_ready, 1)

            x_silu(0)
            bc_silu(0)
            z_use(("z0", 0))
            z_use(("z1", 0))
            x_silu(1)

            for m in range(SSM_STEPS):
                for use in ssm_steps[m]:
                    kind, c = use
                    if kind in ("z0", "z1"):
                        z_use(use)
                    elif kind == "xp":
                        xp_use(c)
                    elif kind == "op":
                        src = filled(v, use)
                        v.wait_ge(rms_ready, c + 1)
                        v.tensor_tensor(y_n, src[:, :], rms_r, ALU.mult).then_inc(y_normed, 1)
                        v.wait_ge(y_normed, c + 1)
                        v.tensor_scalar(y_o, y_n, nrm_g[:, 0:1], col("ff_b"), ALU.mult, ALU.add).then_inc(yo_ready, 1)
                    elif kind == "yo":
                        src = filled(v, use)
                        v.tensor_tensor(x_of(0, c), x_of(0, c), src[:, :], ALU.add).then_inc(z1_ready, 1)
                        v.wait_ge(z1_ready, c + 1)
                        ln_vector_a(v, 2 * CHUNKS + c)
                    elif kind == "f2":
                        src = filled(v, use)
                        v.tensor_scalar(f_2[:, c % 2, :], src[:, :], nrm_g[:, 2:3], col("fc2_b"), ALU.mult, ALU.add).then_inc(f2_ready, 1)
                    elif kind == "fo":
                        src = filled(v, use)
                        v.tensor_tensor(x_of(0, c), x_of(0, c), src[:, :], ALU.add).then_inc(o_added, 1)
                if m == SOFTPLUS_STEP:
                    softplus(1)
                if m % CT == 3 and m // CT + 1 < CHUNKS:
                    bc_silu(m // CT + 1)
                if m % 2 == 1 and m // 2 + 2 < TILES // 4:
                    x_silu(m // 2 + 2)
                if m < TILES and m % 4 == 0:
                    k = m // 4
                    v.wait_ge(g_scored, k + 1)
                    if k >= 2:
                        v.wait_ge(mixed, 4 * (k - 2) + 4)
                    v.tensor_tensor(g_m[:, k % 2, :, :], GB[k % 2][:, 0:4 * GRID].rearrange("p (t j) -> p t j", j=GRID),
                                    wide(cst("tri_quarter"), 4), ALU.mult).then_inc(g_masked, 1)
                e = m - 1
                if 0 <= e < TILES:
                    v.wait_ge(dec_exped, e + 1)
                    if e % 4 == 0:
                        v.wait_ge(g_masked, e // 4 + 1)
                    if e >= 2:
                        v.wait_ge(y_summed, e - 1)
                    v.tensor_tensor(mix[:, e % 2, :, :], dec[:, e % 2, :, :], wide(g_m[:, e // 4 % 2, e % 4, :], SSM_H), ALU.mult)\
                        .then_inc(mixed, 1)
                k, rest = divmod(m - 6, 4)
                if rest == 0 and 0 <= k < TILES // 4:
                    c = k // 2
                    v.wait_ge(y_summed, 4 * k + 4)
                    v.wait_ge(z_ready, 2 * c + 2)
                    half = 4 * (k % 2)
                    v.tensor_tensor(y_g[:, c, :, half:half + 4, :], YT[k % 2][:, :].rearrange("p (t h j) -> p h t j", t=4, h=2),
                                    z_s[:, c % 2, :, half:half + 4, :], ALU.mult).then_inc(gated, 1)
                for c in range(CHUNKS):
                    if m == NORM_STEP[c] - 1:
                        ln_vector_b(v, 2 * CHUNKS + c)
                        ln_vector_c(v, 2 * CHUNKS + c)

        @block.scalar
        def _(a):
            a.preload_act_table_set("natural_log_exp_and_others")
            a.wait_ge(eps_set, 1)
            for q in range(CHUNKS + 2):
                if 1 <= q <= CHUNKS:
                    ln_scalar_b(a, q - 1)
                if q >= 2:
                    a.wait_ge(ln_turned, q - 1)
                    for m in range(2):
                        a.activation(xn_t[0:64, CT * (q - 2):CT * (q - 1), m, :],
                                     bank[2 + q][64 * m:64 * m + 64, :].rearrange("p (t j) -> p t j", j=GRID),
                                     ACT.Identity).then_inc(xn_ready, 1)
                if q < CHUNKS:
                    ln_scalar_a(a, q)
            a.wait_ge(cols_in, 16)

            def late_weights():
                a.wait_ge(late_in, 16)
                a.activation(a_exp[:, :], par("a_log"), ACT.Exp).then_inc(a_exped, 1)
                a.wait_ge(nrm_sum, 1)
                a.activation(nrm_l[:, :], nrm_s[:, :], ACT.Ln).then_inc(nrm_log, 1)
                a.wait_ge(nrm_log, 1)
                a.activation(nrm_r[:, :], nrm_l[:, :], ACT.Exp, scale=-0.5).then_inc(nrm_rs, 1)

            def att_use(use):
                kind, g = use
                if kind == "v":
                    src = filled(a, use)
                    if g >= 1:
                        filled(a, ("vt1", g - 1))
                    a.activation(v_dup[:, :, :, :], src[:, :].rearrange("p (t j) -> p t j", j=GRID).unsqueeze(2)
                                 .broadcast_to([P, CT, 2, GRID]), ACT.Identity).then_inc(v_duped, 1)
                elif kind == "wo":
                    src = filled(a, use)
                    if g >= 1:
                        a.wait_ge(y_ready, g)
                    bias = col("bo_" + "ji"[g // CHUNKS])
                    a.activation(wo_e[:, :], src[:, :], ACT.Exp, bias=bias).then_inc(wo_exped, 1)
                    a.wait_ge(wo_exped, g + 1)
                    a.activation(wo_b[:, :], src[:, :], ACT.Relu, bias=bias).then_inc(wo_biased, 1)
                elif kind == "ut":
                    src = filled(a, use)
                    a.wait_ge(turned_out, 32 * CHUNKS)
                    a.activation(u2[:, g, :], src[:, :], ACT.Identity, bias=col("ln1_b"), scale=col("ln1_w")).then_inc(u2_ready, 1)
                    a.wait_ge(u2_ready, g + 1)
                    for m in range(2):
                        a.activation(ut_a[0:64, CT * g:CT * g + CT, m, :],
                                     u2[64 * m:64 * m + 64, g, :].rearrange("p (t j) -> p t j", j=GRID), ACT.Identity)\
                            .then_inc(ut_here, 1)
                elif kind == "yt":
                    src = filled(a, use)
                    a.activation(y_tok[:, g, :], src[:, :], ACT.Identity).then_inc(y_turned, 1)

            def expand_k(g):
                a.wait_ge(k_added, g + 1)
                if g >= 2:
                    a.wait_ge(scored, 4 * (g - 2) + 4)
                for h in range(HEADS):
                    a.activation(k_bd[:, g % 2, h, :], k_rot[:, :], ACT.Identity, scale=cst("head_mask")[:, h:h + 1])\
                        .then_inc(k_ready, 1)

            a.wait_ge(consts_in, 16)
            expand_k(0)
            for use in att_steps[-1]:
                att_use(use)
            for n in range(ATT_STEPS):
                for use in att_steps[n][:1]:
                    att_use(use)
                e = n - 1
                if 0 <= e < PAIRS:
                    a.wait_ge(p_turned, e + 1)
                    if e >= 2:
                        a.wait_ge(av_done, e - 1)
                    a.activation(prob_t[:, e % 2, :, :].rearrange("p k n -> p (k n)"), PT[e % 2][:, :], ACT.Identity)\
                        .then_inc(p_copied, 1)
                if n < PAIRS:
                    a.wait_ge(s_centred, n + 1)
                    if n >= 2:
                        a.wait_ge(p_turned, n - 1)
                    a.activation(prob[:, n % 2, :, :].rearrange("p k n -> p (k n)"),
                                 s_cen[:, n % 2, :, :].rearrange("p h j -> p (h j)"), ACT.Exp).then_inc(exped, 1)
                for use in att_steps[n][1:]:
                    att_use(use)
                e = n - 2
                if 0 <= e < PAIRS:
                    a.wait_ge(av_done, e + 1)
                    a.activation(z_log[:, e % 2, :], OZ[e % 2][:, 128:256], ACT.Ln).then_inc(z_logged, 1)
                    a.wait_ge(z_logged, e + 1)
                    if e >= 2:
                        a.wait_ge(o_ready, e - 1)
                    a.activation(z_inv[:, e % 2, :], z_log[:, e % 2, :], ACT.Exp, scale=-1.0).then_inc(z_inverted, 1)
                g = (n - 1) // 4 + 1
                if n % 4 == 1 and g < ATT_CHUNKS:
                    expand_k(g)
                if n == FOLD_STEP:
                    late_weights()
                for q in range(CHUNKS):
                    if n == XT_STEP[q]:
                        ln_scalar_a(a, CHUNKS + q)
                    if n == XT_STEP[q] + 1:
                        ln_scalar_b(a, CHUNKS + q)

            def bc_use(c):
                src = filled(a, ("bc", c))
                if c >= 1:
                    a.wait_ge(c_ready, c)
                a.activation(b_c[:, 0, :], src[:, :], ACT.Identity, bias=col("conv_bbc")).then_inc(bc_biased, 1)
                a.wait_ge(bc_biased, c + 1)
                a.activation(b_c[:, 1, :], b_c[:, 0, :], ACT.Tanh, scale=0.5).then_inc(bc_tanh, 1)

            def z_use(use):
                hh, c = int(use[0][1]), use[1]
                src = filled(a, use)
                if c >= 1:
                    a.wait_ge(z_ready, 2 * (c - 1) + hh + 1)
                a.activation(z_th[:, hh, :], src[:, :], ACT.Tanh, scale=0.5).then_inc(z_tanh, 1)

            def x_tanh(k):
                a.wait_ge(xv_ready, 2 * k + 2)
                if k >= 2:
                    a.wait_ge(xs_ready, k - 1)
                a.activation(xth[k % 2], xv[:, 4 * k:4 * k + 4, :], ACT.Tanh, scale=0.5).then_inc(xth_ready, 1)

            def softplus(part):
                first, end = DT_PARTS[part]
                w, u, v_abs, ln_u, inv_u = (t[:, SSM_H * first:SSM_H * end] for t in (
                    dt_fin[:, 0, :], dt_fin[:, 1, :], dt_tmp[:, 1, :], dt_tmp[:, 2, :], dt_tmp[:, 4, :]))
                a.preload_act_table_set("natural_log_exp_and_others")
                a.wait_ge(dt_chain, 6 * part + 1)
                a.activation(w, v_abs, ACT.Exp, scale=-1.0).then_inc(dt_act, 1)
                a.wait_ge(dt_chain, 6 * part + 2)
                a.activation(ln_u, u, ACT.Ln).then_inc(dt_act, 1)
                a.wait_ge(dt_act, 3 * part + 2)
                a.activation(inv_u, ln_u, ACT.Exp, scale=-1.0).then_inc(dt_act, 1)

            softplus(0)
            x_tanh(0)
            bc_use(0)
            z_use(("z0", 0))
            z_use(("z1", 0))
            x_tanh(1)

            for m in range(SSM_STEPS):
                for use in ssm_steps[m]:
                    kind, c = use
                    if kind == "bc":
                        bc_use(c)
                    elif kind in ("z0", "z1"):
                        z_use(use)
                    elif kind == "ms":
                        if c == 0:
                            a.preload_act_table_set("natural_log_exp_and_others")
                        src = filled(a, use)
                        if c >= 1:
                            a.wait_ge(rms_ready, c)
                        a.activation(rms_l, src[:, :], ACT.Ln, bias=eps_col[:, 1:2]).then_inc(rms_logged, 1)
                        a.wait_ge(rms_logged, c + 1)
                        if c >= 1:
                            a.wait_ge(y_normed, c)
                        a.activation(rms_r, rms_l, ACT.Exp, scale=-0.5).then_inc(rms_ready, 1)
                    elif kind == "ht":
                        src = filled(a, use)
                        a.activation(h_t[c % 2], src[:, :], ACT.Identity, bias=col("ln2_b"), scale=col("ln2_w")).then_inc(h_ready, 1)
                    elif kind == "f1":
                        src = filled(a, use)
                        a.wait_ge(nrm_ready, 3)
                        a.activation(f_1[c % 2], src[:, :], ACT.Gelu, bias=col("fc1_b"), scale=nrm_g[:, 1:2]).then_inc(f1_ready, 1)
                        if c == 1:
                            a.preload_act_table_set("natural_log_exp_and_others")
                    elif kind == "yo":
                        ln_scalar_a(a, 2 * CHUNKS + c)
                if m < TILES:
                    a.wait_ge(decayed, m + 1)
                    if m >= 2:
                        a.wait_ge(mixed, m - 1)
                    a.activation(dec[:, m % 2, :, :].rearrange("p h t -> p (h t)"), DEC[m % 2][:, :], ACT.Exp).then_inc(dec_exped, 1)
                if m == SOFTPLUS_STEP:
                    softplus(1)
                if m % 2 == 0 and m // 2 + 2 < TILES // 4:
                    x_tanh(m // 2 + 2)
                for c in range(CHUNKS):
                    if m == SQUARE_STEP[c]:
                        a.wait_ge(gated, 2 * c + 2)
                        if c >= 1:
                            filled(a, ("ms", c - 1))
                        a.activation(y_sq.rearrange("p h t j -> p (h t j)"),
                                     y_g[:, c, :, :, :].rearrange("p h t j -> p (h t j)"), ACT.Square).then_inc(y_squared, 1)
                    if m == NORM_STEP[c] - 1:
                        ln_scalar_b(a, 2 * CHUNKS + c)

        @block.gpsimd
        def _(gp):
            gp.memset(q_bd[:, :, :, :, :], 0.0).then_inc(q_zeroed, 1)
            gp.wait_ge(q_zeroed, 1)
            gp.memset(xn_t[64:128, :, :, :], 0.0).then_inc(xn_ones, 1)
            gp.wait_ge(xn_ones, 1)
            gp.memset(xn_t[64:65, :, :, :], 1.0).then_inc(xn_ones, 1)
            gp.wait_ge(xn_ones, 2)
            gp.wait_ge(consts_in, 16)
            gp.wait_ge(params_in, 16)
            gp.wait_ge(cols_in, 16)
            for d, n in enumerate("ji"):
                gp.tensor_scalar(w_att[d][:, 0:128], par(f"wqkv_{n}")[:, 0:128], col(f"ga_{n}"), None, ALU.mult).then_inc(w_scaled, 1)
                gp.tensor_scalar(w_att[d][:, 128:320], par(f"wqkv_{n}")[:, 128:320], col(f"gb_{n}"), None, ALU.mult)\
                    .then_inc(w_scaled, 1)
            for d, n in enumerate("ji"):
                gp.tensor_scalar(sin_s[d][:, :], par(f"sin_{n}"), cst("swap_sign"), None, ALU.mult).then_inc(sin_signed, 1)

            def rotary(g):
                gp.wait_ge(rotated, 4 * g + 2)
                if g >= 1:
                    gp.wait_ge(q_ready, 2 * g)
                    gp.wait_ge(k_ready, 4 * g)
                gp.tensor_tensor(k_rot[:, :], rot[:, 0, :], rot[:, 1, :], ALU.add).then_inc(k_added, 1)
                gp.wait_ge(rotated, 4 * g + 4)
                if g >= 2:
                    gp.wait_ge(scored, 4 * (g - 2) + 4)
                gp.wait_ge(k_added, g + 1)
                for m in range(2):
                    rows = slice(64 * m, 64 * m + 64)
                    if m:
                        gp.wait_ge(q_ready, 2 * g + m)
                    gp.tensor_tensor(q_bd[rows, g % 2, :, m, :], rot[rows, 2, :].rearrange("p (t j) -> p t j", j=GRID),
                                     rot[rows, 3, :].rearrange("p (t j) -> p t j", j=GRID), ALU.add).then_inc(q_ready, 1)

            for g in range(ATT_CHUNKS):
                rotary(g)
            gp.wait_ge(q_ready, 2 * ATT_CHUNKS)
            for q in range(CHUNKS):
                quarter = back[:, 4 * q:4 * q + 4, :].rearrange("p u n -> p (u n)")
                gp.wait_ge(back_in[q], 64)
                gp.tensor_scalar(quarter, quarter, 0.5, -1.0, ALU.mult, ALU.add).then_inc(halved, 1)
                gp.wait_ge(halved, q + 1)
                gp.wait_ge(x_in[q], 64)
                gp.tensor_tensor(quarter, quarter, x_of(0, q), ALU.add).then_inc(x_halved, 1)

            gp.wait_ge(y_ready, ATT_CHUNKS)
            gp.memset(dtx[:, :, :, :, :, :], 0.0).then_inc(ssm_zeroed, 1)
            gp.memset(d_x[:, :, :, :, :, :], 0.0).then_inc(ssm_zeroed, 1)
            gp.wait_ge(ssm_zeroed, 2)
            gp.wait_ge(dt_ready, 2)
            gp.wait_ge(d_ready, 1)

            def scale_x(k, part):
                if part == 0:
                    gp.wait_ge(xs_ready, k + 1)
                    if k >= 2:
                        gp.wait_ge(y_summed, 4 * (k - 2) + 4)
                if k or part:
                    gp.wait_ge(x_scaled, 4 * k + part)
                s, which = part % 2, part // 2
                rows = slice(64 * s, 64 * s + 64)
                xs = xv[rows, 4 * k:4 * k + 4, :].rearrange("p t (h n) -> p t h n", h=SSM_H)
                if which == 0:
                    by = dt_fin[rows, 1, 4 * SSM_H * k:4 * SSM_H * (k + 1)].rearrange("p (t h) -> p t h", t=4)\
                        .unsqueeze(3).broadcast_to([64, 4, SSM_H, SSM_P])
                else:
                    by = d_half[rows, :].unsqueeze(1).unsqueeze(3).broadcast_to([64, 4, SSM_H, SSM_P])
                gp.tensor_tensor((dtx, d_x)[which][rows, k % 2, :, :, s, :], xs, by, ALU.mult).then_inc(x_scaled, 1)

            for m in range(SSM_STEPS):
                scaled = min(2 * m if m < 2 else m + 2, TILES)
                if m - 1 in SQUARE_STEP:
                    gp.wait_ge(x_scaled, scaled)
                    gp.wait_ge(y_squared, SQUARE_STEP.index(m - 1) + 1)
                    gp.tensor_tensor(y_sq[:, 0, :, :], y_sq[:, 0, :, :], y_sq[:, 1, :, :], ALU.add).then_inc(squares_added, 1)
                if m >= TILES:
                    continue
                if m >= 2:
                    gp.wait_ge(decayed, m - 1)
                if m:
                    gp.wait_ge(x_scaled, scaled)
                gp.tensor_tensor(a_msk[:, m % 2, :, :], deep(dt_fin[:, 0, SSM_H * m:SSM_H * (m + 1)], GRID), wide(cst("tri"), SSM_H),
                                 ALU.mult).then_inc(a_masked, 1)
                if m == 2 * len(XP_STEP) - 3:
                    gp.wait_ge(dt_ready, 4)
                k, part = divmod(m + 2, 4)
                if k < TILES // 4:
                    gp.wait_ge(a_masked, m + 1)
                    for part in (part,) if k else (2 * m, 2 * m + 1):
                        scale_x(k, part)


def constants():
    co, width = offsets(CONSTS)
    c = np.zeros((P, width), np.float32)
    row = np.arange(P)
    half, pos = row // 64, row % 64

    def put(name, value):
        c[:, co[name][0]:co[name][1]] = value

    put("ident", np.eye(P))
    put("swap_sign", np.where(row % 2 == 0, -1.0, 1.0)[:, None])
    put("head_mask", (pos[:, None] // HD) == np.arange(HEADS)[None, :])
    m = np.arange(P)
    put("v_mask", half[:, None] == (m[None, :] // HD % 2))
    t = np.arange(GRID)
    put("tri", pos[:, None] <= t[None, :])
    put("tri_quarter", 0.25 * (pos[:, None] <= t[None, :]))
    put("later", (half[:, None] == half[None, :]) & (pos[:, None] > pos[None, :]))
    put("ident2", pos[:, None] == t[None, :])
    sp = row // SSM_P % 2
    put("mean_bd", (sp[:, None] == half[None, :]) / INNER)
    put("sp_mask", sp[:, None] == np.arange(2)[None, :])
    return c


def stack(*rows):
    a = np.concatenate(rows, axis=0)
    return np.concatenate([a, np.zeros((P - a.shape[0], a.shape[1]), a.dtype)], axis=0)


def two(w):
    z = np.zeros_like(w)
    return np.concatenate([np.concatenate([w, z], 1), np.concatenate([z, w], 1)], 0)


def pack(inp):
    po, n_params = offsets(PARAMS)
    lo, n_cols = offsets(COLS)
    p = np.zeros((P, n_params), np.float32)
    c = np.zeros((P, n_cols), np.float32)
    l0 = lambda n: inp["L0_conv_" + n]
    l1 = lambda n: inp["L1_conv_" + n]

    def put(name, value):
        p[:, po[name][0]:po[name][1]] = value

    def put_col(name, value):
        c[:value.shape[0], lo[name][0]] = value

    pair = np.arange(DIM) ^ 1
    for d in "ji":
        wq, wkv = l0(f"Wq_{d}"), l0(f"Wkv_{d}")
        wk, wv = wkv[:, :DIM], wkv[:, DIM:]
        put(f"wqkv_{d}", stack(np.concatenate([wq, wq[:, pair], wk, wv, wk[:, pair]], 1)))
        wo = l0(f"Wo_{d}").reshape(HD, HEADS, DIM).transpose(1, 0, 2).reshape(DIM, DIM)
        put(f"wo_{d}", two(wo))
        for t in ("cos", "sin"):
            put(f"{t}_{d}", np.tile(l0(f"{t}_{d}")[0].T, (2 * HEADS, 1)))
        for k in ("ga", "ba", "gb", "bb"):
            put_col(f"{k}_{d}", l0(k[0] + d + k[1]))
        put_col(f"bo_{d}", np.tile(l0(f"bo_{d}"), 2))
    w = l1("in_proj_w").T
    xbc = w[:, INNER:2 * INNER + 2 * STATE]
    put("w_xbc", np.concatenate([xbc, xbc], 0))
    taps = l1("conv_w")
    put("tap_a", np.repeat(np.stack([taps[:, 3], taps[:, 2]]), DIM, axis=0))
    put("tap_b", np.repeat(np.stack([taps[:, 1], taps[:, 0]]), DIM, axis=0))
    put("w_dt", stack(w[:, 2 * INNER + 2 * STATE:]))
    wz = w[:, :INNER].reshape(DIM, 2, 4, SSM_P)
    z = np.zeros((2, DIM, 2, 4, 2, SSM_P), np.float32)
    z[0, :, :, :, 0], z[1, :, :, :, 1] = wz, wz
    put("w_z", z.reshape(P, 2 * P))
    spread = lambda a: np.repeat(a.reshape(a.shape[0], 2, 4, 1, SSM_P), 2, axis=3).reshape(a.shape[0], 2 * P)
    put("w_out", stack(spread(l1("out_proj_w"))))
    put("norm_w", np.repeat(spread(l1("ssm_norm_w")[None, :]), P, axis=0))
    put("ff_vt", stack(l1("ff_v").T))
    for n in ("fc1", "fc2"):
        put(f"{n}_vt", two(l1(f"{n}_v").T))
    for n in ("ff", "fc1", "fc2"):
        put(f"{n}_v", np.concatenate([l1(f"{n}_v")] * 2, 0))
        put_col(f"{n}_g", np.tile(l1(f"{n}_g"), 2))
        put_col(f"{n}_b", np.tile(l1(f"{n}_b"), 2))
    put("conv_bx", np.repeat(l1("conv_b")[None, :INNER], P, axis=0))
    put("dt_bias", np.repeat(l1("dt_bias")[None, :], P, axis=0))
    put("a_log", np.repeat(l1("A_log")[None, :], P, axis=0))
    put("d_par", np.repeat(l1("D_param")[None, :], P, axis=0))
    for n in ("ln1_w", "ln1_b", "ln2_w", "ln2_b"):
        put_col(n, np.tile(l1(n), 2))
    bc = l1("conv_b")[INNER:]
    put_col("conv_bbc", np.concatenate([bc[:STATE], bc[:STATE], bc[STATE:], bc[STATE:]]))
    return p, c


def kernel(**inputs):
    import concourse.bacc as bacc
    from concourse.bass_utils import run_bass_kernel_spmd

    inp = {k: np.asarray(v) for k, v in inputs.items()}
    params, cols = pack(inp)
    arrays = {"x": np.ascontiguousarray(inp["x"]), "consts": constants(), "params": params, "cols": cols}
    nc = bacc.Bacc("TRN2", target_bir_lowering=False, num_devices=1)
    aps = {n: nc.dram_tensor(n, a.shape, mybir.dt.from_np(a.dtype), kind="ExternalInput").ap() for n, a in arrays.items()}
    out = nc.dram_tensor("out", (1, GRID, GRID, DIM), F32, kind="ExternalOutput").ap()
    build(nc, out=out, **aps)
    r = run_bass_kernel_spmd(nc, [arrays], core_ids=[0])
    return r.results[0]["out"]
```

```python
from contextlib import ExitStack

import numpy as np

import concourse.bass as bass
from concourse import mybir

F32 = mybir.dt.float32
ALU = mybir.AluOpType
ACT = mybir.ActivationFunctionType
AX = mybir.AxisListType.X

P = 128
GRID = 64
DIM = 64
HEADS, HD = 4, 16
SSM_H, SSM_P, STATE = 8, 16, 32
INNER = SSM_H * SSM_P
LN_EPS = 1e-5
TILES = GRID // 2
CT = 8
CHUNKS = TILES // CT
CW = CT * GRID
ATT_CHUNKS = 2 * CHUNKS
PAIRS = ATT_CHUNKS * CT // 2
ATT_STEPS = 40

CONSTS = dict(ident=P, swap_sign=1, head_mask=HEADS, v_mask=P, tri=GRID, tri_quarter=GRID,
              later=P, ident2=GRID, mean_bd=P, sp_mask=2)
PARAMS = dict(wqkv_j=3 * DIM, wqkv_i=3 * DIM, cos_j=GRID, sin_j=GRID, cos_i=GRID,
              sin_i=GRID, wo_j=P, wo_i=P, w_xbc=INNER + 2 * STATE, tap_a=INNER + 2 * STATE, tap_b=INNER + 2 * STATE,
              w_dt=SSM_H, w_z=2 * P, w_out=2 * P, norm_w=2 * P, ff_vt=DIM, fc1_vt=P, fc2_vt=P,
              ff_v=DIM, fc1_v=DIM, fc2_v=DIM, conv_bx=INNER, dt_bias=SSM_H, a_log=SSM_H, d_par=SSM_H)
COLS = dict(ga_j=1, ba_j=1, gb_j=1, bb_j=1, ga_i=1, ba_i=1, gb_i=1, bb_i=1, bo_j=1, bo_i=1, ln1_w=1,
            ln1_b=1, ln2_w=1, ln2_b=1, ff_g=1, ff_b=1, fc1_g=1, fc1_b=1, fc2_g=1, fc2_b=1, conv_bbc=1)


def offsets(widths):
    at, out = 0, {}
    for name, w in widths.items():
        out[name] = (at, at + w)
        at += w
    return out, at


FOLD_STEP = 6
XT_STEP = (26, 29, 32, 35)
UT_STEP = (29, 32, 35, 38)
XP_STEP = (31, 32, 33, 34, 35, 35, 36, 36)


def attention_uses():
    steps = {-1: [("k", 0), ("q", 0), ("v", 0), ("vt0", 0), ("vt1", 0), ("k", 1), ("q", 1)]}
    for n in range(PAIRS):
        g, slot = divmod(n, 4)
        uses = []
        if g + 1 < ATT_CHUNKS:
            uses += [(k, g + 1) for k in (("v",), ("vt0", "vt1"), (), ())[slot]]
        if slot >= 2 and g + 2 < ATT_CHUNKS:
            uses.append(("kq"[slot - 2], g + 2))
        if slot == 2 and 2 <= g < 2 + CHUNKS:
            uses.append(("yt", g - 2))
        if slot == 3 and g >= 1:
            uses.append(("wo", g - 1))
        if n == FOLD_STEP:
            uses.append(("fold", 0))
        steps[n] = uses
    for n in range(PAIRS, ATT_STEPS):
        steps[n] = []
    for n in range(ATT_STEPS):
        steps[n] += [("ut", q) for q in range(CHUNKS) if UT_STEP[q] == n]
        steps[n] += [("xt", q) for q in range(CHUNKS) if XT_STEP[q] == n]
        steps[n] += [("xp", k) for k, at in enumerate(XP_STEP) if at == n]
    steps[PAIRS + 2].append(("wo", ATT_CHUNKS - 1))
    return steps


GROUPS = ((0, 8), (8, 16), (16, 24), (24, 28), (28, 32))
SQUARE_STEP = (20, 22, 27, 31, 33)
PROJ_STEP = (22, 24, 29, 32, 34)
NORM_STEP = (25, 27, 32, 35, 37)
MLP_STEPS = ((28, 29, 30), (28, 30, 31), (36, 37, 38), (37, 38, 39), (38, 39, 40))
TAIL_STEP = 33
SSM_STEPS = 41
LAPS = 3
SOFTPLUS_STEP = 8
DT_STEP = 36
DT_PARTS = ((0, 2 * len(XP_STEP)), (2 * len(XP_STEP), TILES))


def ssm_uses():
    before = [("bc", 0), ("z0", 0), ("z1", 0)]
    steps = {m: [] for m in range(SSM_STEPS)}
    for m in range(TILES // 2 - len(XP_STEP)):
        steps[m].append(("xp", len(XP_STEP) + m))
    for c in range(1, CHUNKS):
        steps[CT * (c - 1) + 2].append(("bc", c))
        steps[CT * (c - 1) + 4].append(("z0", c))
        steps[CT * (c - 1) + 5].append(("z1", c))
    for o in range(len(GROUPS)):
        steps[PROJ_STEP[o]] += [("ms", o), ("op", o)]
        steps[PROJ_STEP[o] + 1].append(("yo", o))
    for o in range(len(GROUPS)):
        for kind, at in zip(("f1", "f2", "fo"), MLP_STEPS[o]):
            steps[at].append((kind, o))
        steps[NORM_STEP[o]].append(("ht", o))
    return before, steps


def build(nc, x, consts, params, cols, out):
    co, n_consts = offsets(CONSTS)
    po, n_params = offsets(PARAMS)
    lo, n_cols = offsets(COLS)
    att_steps = attention_uses()
    ssm_before, ssm_steps = ssm_uses()
    order = [u for n in sorted(att_steps) for u in att_steps[n]] + ssm_before \
        + [u for m in range(SSM_STEPS) for u in ssm_steps[m]]
    ring_at = {use: r for r, use in enumerate(order)}
    tail_at = ring_at[next(u for m in range(TAIL_STEP, SSM_STEPS) for u in ssm_steps[m])]

    x_v = x.rearrange("o (u t i) j c -> t i j (o u) c", t=2, i=2)
    out_v = out.rearrange("o (u t i) j c -> t i j (o u) c", t=2, i=2)
    turned = nc.dram_tensor("attention_j_turned", (GRID, GRID, DIM), F32, kind="Internal").ap()
    turned_w = turned.rearrange("i (u t j) c -> t i u (j c)", t=2, j=2)
    turned_r = turned.rearrange("(u t i) j c -> t i j u c", t=2, i=2)

    with ExitStack() as ctx:
        def sb(name, shape, where=ctx):
            return where.enter_context(nc.sbuf_tensor(name, shape, F32))

        def sem(name):
            return ctx.enter_context(nc.semaphore(name))

        bank = [ctx.enter_context(nc.psum_tensor(f"bank{b}", [P, CW], F32)) for b in range(8)]
        RING, SCORE, PT, OZ = bank[0:2], bank[2:4], bank[4:6], bank[6:8]
        DEC, YT = (bank[2], bank[3], bank[7]), bank[4:6]
        GB = (bank[6][:, 0:4 * GRID], bank[6][:, 4 * GRID:8 * GRID])

        def bank_of(r):
            tail = (RING[tail_at % 2], RING[(tail_at + 1) % 2]) + DEC
            return RING[r % 2] if r < tail_at else tail[(r - tail_at) % len(tail)]

        c_sb = sb("c_sb", [P, n_consts])
        p_sb = sb("p_sb", [P, n_params])
        l_sb = sb("l_sb", [P, n_cols])

        def cst(name):
            return c_sb[:, co[name][0]:co[name][1]]

        def par(name):
            return p_sb[:, po[name][0]:po[name][1]]

        def col(name, a=0, b=P):
            return l_sb[a:b, lo[name][0]:lo[name][1]]

        eps_col = sb("eps_col", [P, 3])
        x_tok = sb("x_tok", [P, 16, 2 * DIM])
        back = sb("back", [P, 16, 2 * DIM])
        cen = sb("cen", [P, 2, CW])
        sqr = sb("sqr", [P, 2, CW])
        xhat = sb("xhat", [P, 2, CW])
        ln_s = sb("ln_s", [P, 2 * CHUNKS + len(GROUPS), CT])
        ln_n = sb("ln_n", [P, 2 * CHUNKS + len(GROUPS), CT])
        ln_v = sb("ln_v", [P, 2 * CHUNKS + len(GROUPS), CT])
        ln_l = sb("ln_l", [P, 2 * CHUNKS + len(GROUPS), CT])
        ln_r = sb("ln_r", [P, 2 * CHUNKS + len(GROUPS), CT])
        y_t = sb("y_t", [P, 2, CHUNKS, CW])
        sin_s = [sb(f"sin_s{d}", [P, GRID]) for d in range(2)]
        w_att = [sb(f"w_att{d}", [P, 3 * DIM]) for d in range(2)]
        w_xdt = sb("w_xdt", [P, INNER + SSM_H])
        w_xb = sb("w_xb", [P, INNER])
        w_bca = sb("w_bca", [P, 2 * STATE])
        w_bcb = sb("w_bcb", [P, 2 * STATE])
        w_ops = sb("w_ops", [P, 2 * P])
        w_ofd = sb("w_ofd", [P, 2, 2, DIM])
        nrm_q = sb("nrm_q", [P, 3, DIM])
        nrm_s = sb("nrm_s", [P, 3])
        nrm_l = sb("nrm_l", [P, 3])
        nrm_r = sb("nrm_r", [P, 3])
        nrm_g = sb("nrm_g", [P, 3])
        a_neg = sb("a_neg", [P, SSM_H])
        a_exp = sb("a_exp", [P, SSM_H])
        d_half = sb("d_half", [P, SSM_H])
        d_ident = sb("d_ident", [P, SSM_H, GRID])

        att = ExitStack()
        xn_t = sb("xn_t", [P, TILES, 2, GRID], att)
        q_bd = sb("q_bd", [P, 2, CT, 2, GRID], att)
        k_bd = sb("k_bd", [P, 2, HEADS, CW], att)
        v_bd = sb("v_bd", [P, 2, CT, P], att)
        s_max = sb("s_max", [P, 2, 8], att)
        s_cen = sb("s_cen", [P, 2, 8, GRID], att)
        prob = sb("prob", [P, 2, 4, P], att)
        prob_t = sb("prob_t", [P, 2, 4, P], att)
        z_log = sb("z_log", [P, 2, P], att)
        z_inv = sb("z_inv", [P, 2, P], att)
        o_t = sb("o_t", [P, 2, CT, GRID], att)
        wo_b = sb("wo_b", [P, CW], att)
        wo_e = sb("wo_e", [P, CW], att)
        rot_cos = sb("rot_cos", [P, 2, CW], att)
        rot_sin = sb("rot_sin", [P, 2, CW], att)
        rot_swap = sb("rot_swap", [P, 2, CW], att)
        k_rot = sb("k_rot", [P, CW], att)
        v_dup = sb("v_dup", [P, CT, 2, GRID], att)
        y_tok = sb("y_tok", [P, CHUNKS, CW], att)
        att.close()

        ssm = ExitStack()
        ut_a = sb("ut_a", [P, TILES, 2, GRID], ssm)
        b_c = sb("b_c", [P, 2, CW], ssm)
        b_s = sb("b_s", [2 * STATE, 2, CW], ssm)
        c_s = sb("c_s", [2 * STATE, 2, CW], ssm)
        z_s = sb("z_s", [P, 2, 2, CT, GRID], ssm)
        a_msk = sb("a_msk", [P, LAPS, SSM_H, GRID], ssm)
        dec = sb("dec", [P, LAPS, SSM_H, GRID], ssm)
        mix = sb("mix", [P, LAPS, SSM_H, GRID], ssm)
        g_m = sb("g_m", [P, 2, 4, GRID], ssm)
        dtx = sb("dtx", [P, 2, 4, SSM_H, 2, SSM_P], ssm)
        x_bd = sb("x_bd", [P, 2, 4, SSM_H, 2, SSM_P], ssm)
        y_g = sb("y_g", [P, CHUNKS, 2, CT, GRID], ssm)
        u2 = sb("u2", [P, CHUNKS, CW], ssm)
        ut_b = sb("ut_b", [P, TILES, 2, GRID], ssm)
        xv = sb("xv", [P, TILES, INNER], ssm)
        dt_fin = sb("dt_fin", [P, 2, TILES * SSM_H], ssm)
        ssm.close()
        dt_tmp = y_t[:, 0, 0:3, :].rearrange("p a n -> p (a n)")[:, 0:5 * TILES * SSM_H].rearrange("p (k n) -> p k n", k=5)
        xth = [ap.rearrange("p (t n) -> p t n", t=4) for ap in (y_t[:, 1, 0, :], y_t[:, 0, 3, :])]
        y_sq = y_t[:, 0, 0:2, :]
        y_n, y_o = y_t[:, 0, 2, :], y_t[:, 0, 3, :]
        flat_back = [back[:, 4 * k:4 * k + 4, :].rearrange("p u n -> p (u n)") for k in range(4)]
        h_t, f_1 = flat_back[0:2], flat_back[2:4]
        rms_r, z_th, f_2, rms_l = y_t[:, 1, 0, :], y_t[:, 1, 1:3, :], y_t[:, 1, 1:3, :], y_t[:, 1, 3, :]

        ident_in = sem("ident_in")
        consts_in = sem("consts_in")
        params_in = sem("params_in")
        cols_in = sem("cols_in")
        turned_out = sem("turned_out")
        out_done = sem("out_done")
        eps_set = sem("eps_set")
        q_zeroed = sem("q_zeroed")
        sin_signed = sem("sin_signed")
        late_in = sem("late_in")
        w_scaled = sem("w_scaled")
        bias_row = sem("bias_row")
        w_ready = sem("w_ready")
        taps_ready = sem("taps_ready")
        out_scaled = sem("out_scaled")
        w_out_ready = sem("w_out_ready")
        nrm_sq = sem("nrm_sq")
        nrm_sum = sem("nrm_sum")
        nrm_log = sem("nrm_log")
        nrm_rs = sem("nrm_rs")
        nrm_ready = sem("nrm_ready")
        a_exped = sem("a_exped")
        a_ready = sem("a_ready")
        d_ready = sem("d_ready")
        xn_ones = sem("xn_ones")
        xn_ready = sem("xn_ready")
        ln_sum = sem("ln_sum")
        ln_negmean = sem("ln_negmean")
        ln_centred = sem("ln_centred")
        ln_squared = sem("ln_squared")
        ln_var = sem("ln_var")
        ln_log = sem("ln_log")
        ln_rstd = sem("ln_rstd")
        ln_done = sem("ln_done")
        ln_turned = sem("ln_turned")
        ring_filled = sem("ring_filled")
        rotated = sem("rotated")
        swapped = sem("swapped")
        q_ready = sem("q_ready")
        k_added = sem("k_added")
        k_ready = sem("k_ready")
        v_duped = sem("v_duped")
        v_ready = sem("v_ready")
        scored = sem("scored")
        s_maxed = sem("s_maxed")
        s_centred = sem("s_centred")
        exped = sem("exped")
        p_turned = sem("p_turned")
        p_copied = sem("p_copied")
        av_done = sem("av_done")
        z_logged = sem("z_logged")
        z_inverted = sem("z_inverted")
        o_ready = sem("o_ready")
        wo_biased = sem("wo_biased")
        wo_exped = sem("wo_exped")
        y_ready = sem("y_ready")
        y_turned = sem("y_turned")
        halved = sem("halved")
        x_halved = sem("x_halved")
        u_starts = sem("u_starts")
        x1_ready = sem("x1_ready")
        u2_ready = sem("u2_ready")
        ut_here = sem("ut_here")
        ssm_zeroed = sem("ssm_zeroed")
        xv_ready = sem("xv_ready")
        dtv_ready = sem("dtv_ready")
        dt_chain = sem("dt_chain")
        dt_act = sem("dt_act")
        dt_ready = sem("dt_ready")
        xth_ready = sem("xth_ready")
        xs_ready = sem("xs_ready")
        dtx_ready = sem("dtx_ready")
        x_bd_ready = sem("x_bd_ready")
        d_ident_ready = sem("d_ident_ready")
        bc_biased = sem("bc_biased")
        bc_tanh = sem("bc_tanh")
        b_ready = sem("b_ready")
        c_ready = sem("c_ready")
        z_tanh = sem("z_tanh")
        z_ready = sem("z_ready")
        a_masked = sem("a_masked")
        decayed = sem("decayed")
        dec_exped = sem("dec_exped")
        g_scored = sem("g_scored")
        g_masked = sem("g_masked")
        mixed = sem("mixed")
        y_summed = sem("y_summed")
        gated = sem("gated")
        y_squared = sem("y_squared")
        squares_added = sem("squares_added")
        rms_logged = sem("rms_logged")
        rms_ready = sem("rms_ready")
        y_normed = sem("y_normed")
        yo_ready = sem("yo_ready")
        z1_ready = sem("z1_ready")
        h_ready = sem("h_ready")
        f1_ready = sem("f1_ready")
        f2_ready = sem("f2_ready")
        o_added = sem("o_added")
        x_in = [sem("x_in0"), sem("x_in1"), sem("x_in23")]
        x_in.append(x_in[2])
        back_in = [sem(f"back_in{q}") for q in range(CHUNKS)]
        ut_in = [sem(f"ut_in{q}") for q in range(CHUNKS)]
        block = ctx.enter_context(nc.Block())

        def filled(eng, use):
            r = ring_at[use]
            eng.wait_ge(ring_filled, r + 1)
            return bank_of(r)

        def drained(eng, use):
            kind, g = use
            signal, count = {
                "v": (v_duped, g + 1), "k": (rotated, 4 * g + 2), "q": (rotated, 4 * g + 4), "vt0": (v_ready, 2 * g + 1),
                "vt1": (v_ready, 2 * g + 2), "wo": (wo_biased, g + 1), "yt": (y_turned, g + 1),
                "xt": (x1_ready, g + 1), "ut": (u2_ready, g + 1), "bc": (bc_biased, g + 1),
                "z0": (z_ready, 2 * g + 1), "z1": (z_ready, 2 * g + 2), "xp": (dtv_ready, g + 1),
                "ms": (rms_logged, g + 1), "op": (y_normed, g + 1), "yo": (z1_ready, g + 1),
                "ht": (h_ready, g + 1), "f1": (f1_ready, g + 1), "f2": (f2_ready, g + 1),
                "fo": (o_added, g + 1), "fold": (w_out_ready, 1)}[kind]
            eng.wait_ge(signal, count)

        def ln_tiles(m):
            if m >= 2 * CHUNKS:
                return GROUPS[m - 2 * CHUNKS]
            return CT * (m % CHUNKS), CT * (m % CHUNKS) + CT

        def x_tiles(first, end):
            return x_tok[:, first // 2:end // 2, :].rearrange("p u n -> p (u n)")

        def in_chunk(o):
            return slice(GRID * (GROUPS[o][0] % CT), GRID * (GROUPS[o][0] % CT + GROUPS[o][1] - GROUPS[o][0]))

        def side(o):
            return min(o, 1) if o != 2 else 0

        def x_of(layer, q):
            return x_tok[:, 4 * q:4 * q + 4, :].rearrange("p u n -> p (u n)")

        def groups(ap):
            return ap.rearrange("p (a c) -> p a c", c=DIM)

        def xn_cols(d, c, sp):
            if d == 0:
                flat = xn_t[:, :, :, :].rearrange("p t s (k r) -> p (t s) k r", r=2)
                return flat[:, :, CT * c:CT * c + CT, sp].rearrange("p i k -> p k i")
            return xn_t[:, CT * c:CT * c + CT, sp, :]

        def wide(ap, n=CT):
            return ap.unsqueeze(1).broadcast_to([ap.shape[0], n, ap.shape[1]])

        def deep(ap, n):
            return ap.unsqueeze(2).broadcast_to([ap.shape[0], ap.shape[1], n])

        HALVES = [(tau, ip) for tau in range(2) for ip in range(2)]

        def part_of(tile, q, tau, ip):
            return tile[64 * tau:64 * tau + 64, 4 * q:4 * q + 4, DIM * ip:DIM * ip + DIM]

        def store(eng, o, tau):
            first, end = GROUPS[o]
            for ip in range(2):
                eng.dma_start(out_v[tau, ip, :, first // 2:end // 2],
                              x_tok[64 * tau:64 * tau + 64, first // 2:end // 2, DIM * ip:DIM * ip + DIM]).then_inc(out_done, 16)

        @block.sync
        def _(sp):
            for q in range(2):
                for tau, ip in HALVES:
                    sp.dma_start(part_of(x_tok, q, tau, ip), x_v[tau, ip, :, 4 * q:4 * q + 4]).then_inc(x_in[q], 16)
                if q == 0:
                    sp.dma_start(c_sb[:, :P], consts[:, :P]).then_inc(ident_in, 16)
            for tau, ip in HALVES:
                sp.dma_start(x_tok[64 * tau:64 * tau + 64, 8:16, DIM * ip:DIM * ip + DIM], x_v[tau, ip, :, 8:16]).then_inc(x_in[2], 16)
            sp.dma_start(c_sb[:, P:], consts[:, P:]).then_inc(consts_in, 16)
            sp.dma_start(l_sb[:, :], cols).then_inc(cols_in, 16)
            late = po["w_xbc"][0]
            sp.dma_start(p_sb[:, :late], params[:, :late]).then_inc(params_in, 16)
            sp.dma_start(p_sb[:, late:], params[:, late:]).then_inc(late_in, 16)

            def swap(g):
                sp.wait_ge(rotated, 4 * g + 4)
                if g >= 1:
                    sp.wait_ge(k_added, g)
                    sp.wait_ge(q_ready, 2 * g)
                for odd in range(2):
                    sp.dma_start(rot_swap[odd:P:2, :, :], rot_sin[1 - odd:P:2, :, :]).then_inc(swapped, 16)

            for g in range(CHUNKS):
                swap(g)
            for g in range(CHUNKS):
                sp.wait_ge(y_turned, g + 1)
                for tau in range(2):
                    sp.dma_start(turned_w[tau, :, 4 * g:4 * g + 4],
                                 y_tok[64 * tau:64 * tau + 64, g, :].rearrange("p (u n) -> p u n", u=4)).then_inc(turned_out, 16)
                swap(CHUNKS + g)
            sp.wait_ge(turned_out, 32 * CHUNKS)
            for q in range(CHUNKS):
                for tau, ip in HALVES:
                    sp.dma_start(part_of(back, q, tau, ip), turned_r[tau, ip, :, 4 * q:4 * q + 4]).then_inc(back_in[q], 16)
            sp.wait_ge(u_starts, 3)
            for q in range(CHUNKS):
                sp.wait_ge(u2_ready, q + 1)
                for dst, half, shift in ((ut_a, 1, 1), (ut_b, 0, 2), (ut_b, 1, 3)):
                    for m in range(2):
                        src = u2[64 * m:64 * m + 64, q, :].rearrange("p (t j) -> p t j", j=GRID)
                        sp.dma_start(dst[64 * half:64 * half + 64, CT * q:CT * q + CT, m, shift:GRID],
                                     src[:, :, 0:GRID - shift]).then_inc(ut_in[q], 16)
            for o in range(len(GROUPS)):
                sp.wait_ge(o_added, o + 1)
                store(sp, o, 0)
                if o < CHUNKS - 2:
                    store(sp, o, 1)
            sp.wait_ge(out_done, 64 * len(GROUPS))

        @block.tensor
        def _(pe):
            def mm(dst, lhsT, rhs, start=True, stop=True):
                return pe.matmul(dst, lhsT, rhs, start=start, stop=stop, skip_group_check=True)

            pe.wait_ge(ident_in, 16)

            def turn(dst, src, n=4):
                for k in range(n):
                    last = pe.transpose(dst[:, P * k:P * k + P], src[:, P * k:P * k + P], cst("ident"))
                return last

            for q in range(CHUNKS):
                pe.wait_ge(ln_done, q + 1)
                turn(bank[4 + q], xhat[:, q % 2, :]).then_inc(ln_turned, 1)

            pe.wait_ge(consts_in, 16)
            pe.wait_ge(cols_in, 16)
            pe.wait_ge(params_in, 16)
            for d, n in enumerate("ji"):
                mm(RING[d][64:65, 0:DIM], col(f"ba_{n}"), par(f"wqkv_{n}")[:, 0:DIM])
                mm(RING[d][64:65, DIM:3 * DIM], col(f"bb_{n}"), par(f"wqkv_{n}")[:, DIM:3 * DIM]).then_inc(bias_row, 1)

            def take(use):
                r = ring_at[use]
                tail = 2 + len(DEC)
                if r >= tail_at + tail:
                    drained(pe, order[r - tail])
                elif r >= tail_at + 2:
                    pe.wait_ge(dec_exped, TILES)
                elif r >= 2:
                    drained(pe, order[r - 2])
                return bank_of(r)

            def att_use(use):
                kind, g = use
                if kind in ("xt", "ut", "xp"):
                    ssm_use(use)
                    return
                dst = take(use)
                d, c = divmod(g, CHUNKS)
                if kind in ("q", "k", "v"):
                    at = DIM * ("q", "k", "v").index(kind)
                    for m in range(2):
                        last = mm(dst[64 * m:64 * m + 64, :], w_att[d][:, at:at + DIM], xn_cols(d, c, m))
                elif kind in ("vt0", "vt1"):
                    if kind == "vt0":
                        pe.wait_ge(v_duped, g + 1)
                    half = int(kind[2])
                    last = turn(dst, v_dup[:, 4 * half:4 * half + 4, :, :].rearrange("p t r j -> p (t r j)"))
                elif kind == "wo":
                    pe.wait_ge(o_ready, 4 * g + 4)
                    last = mm(dst[:, :], par("wo_j" if d == 0 else "wo_i"),
                              o_t[:, g % 2, :, :].rearrange("p t j -> p (t j)"))
                elif kind == "yt":
                    pe.wait_ge(y_ready, g + 1)
                    last = turn(dst, y_t[:, 0, g, :])
                elif kind == "fold":
                    pe.wait_ge(out_scaled, 1)
                    for hh in range(2):
                        last = mm(dst[:, DIM * hh:DIM * hh + DIM], w_ops[:, P * hh:P * hh + P], par("ff_vt"))
                last.then_inc(ring_filled, 1)

            def ssm_use(use):
                kind, c = use
                dst = take(use)
                if kind == "xt":
                    pe.wait_ge(y_ready, CHUNKS + c + 1)
                    last = turn(dst, y_t[:, 1, c, :])
                elif kind == "ut":
                    pe.wait_ge(ln_done, CHUNKS + c + 1)
                    last = turn(dst, xhat[:, c % 2, :])
                elif kind == "bc":
                    pe.wait_ge(ut_in[c], 96)
                    pe.wait_ge(ut_here, 2 * c + 2)
                    for half, (w, u) in enumerate(((w_bca, ut_a), (w_bcb, ut_b))):
                        for part in range(2):
                            for m in range(2):
                                row = 64 * part + 32 * m
                                last = mm(dst[row:row + 32, :], w[:, STATE * part:STATE * part + STATE],
                                          u[:, CT * c:CT * c + CT, m, :], start=half == 0, stop=half == 1)
                elif kind in ("z0", "z1"):
                    hh = int(kind[1])
                    last = mm(dst[:, :], par("w_z")[:, P * hh:P * hh + P], u2[:, c, :])
                elif kind == "xp":
                    pe.wait_ge(ut_in[2 * c // CT], 96)
                    pe.wait_ge(ut_here, 2 * (2 * c // CT) + 2)
                    pe.wait_ge(taps_ready, 5)
                    for k in range(2):
                        t, w = 2 * c + k, INNER + SSM_H
                        mm(dst[:, w * k:w * k + INNER], ut_b[:, t, :, :].rearrange("p s j -> p (s j)"), w_xb[:, :],
                           start=True, stop=False)
                        last = mm(dst[:, w * k:w * k + w], ut_a[:, t, :, :].rearrange("p s j -> p (s j)"), w_xdt[:, :],
                                  start=False, stop=True)
                elif kind == "ms":
                    w = in_chunk(c)
                    if c < CHUNKS - 1:
                        pe.wait_ge(squares_added, c + 1)
                    else:
                        pe.wait_ge(y_squared, c + 1)
                    for hh in range(1 if c < CHUNKS - 1 else 2):
                        last = mm(dst[:, 0:w.stop - w.start], cst("mean_bd"), y_sq[:, hh, w], start=hh == 0,
                                  stop=c < CHUNKS - 1 or hh == 1)
                elif kind == "op":
                    w = in_chunk(c)
                    pe.wait_ge(gated, GROUPS[c][1] // 4)
                    for hh in range(2):
                        last = mm(dst[:, 0:w.stop - w.start], w_ofd[:, hh, :, :].rearrange("p s c -> p (s c)"),
                                  y_g[:, GROUPS[c][0] // CT, hh, :, :].rearrange("p t j -> p (t j)")[:, w], start=hh == 0, stop=hh == 1)
                elif kind == "yo":
                    pe.wait_ge(yo_ready, c + 1)
                    last = turn(dst, y_o[:, in_chunk(c)], (GROUPS[c][1] - GROUPS[c][0]) // 2)
                elif kind == "ht":
                    pe.wait_ge(ln_done, 2 * CHUNKS + c + 1)
                    last = turn(dst, xhat[:, c % 2, :], (GROUPS[c][1] - GROUPS[c][0]) // 2)
                elif kind == "f1":
                    w = in_chunk(c)
                    pe.wait_ge(h_ready, c + 1)
                    last = mm(dst[:, 0:w.stop - w.start], par("fc1_vt"), h_t[side(c)][:, w])
                elif kind == "f2":
                    w = in_chunk(c)
                    pe.wait_ge(f1_ready, c + 1)
                    last = mm(dst[:, 0:w.stop - w.start], par("fc2_vt"), f_1[side(c)][:, w])
                elif kind == "fo":
                    pe.wait_ge(f2_ready, c + 1)
                    last = turn(dst, f_2[:, side(c), in_chunk(c)], (GROUPS[c][1] - GROUPS[c][0]) // 2)
                last.then_inc(ring_filled, 1)

            pe.wait_ge(w_ready, 2)
            pe.wait_ge(xn_ones, 2)
            pe.wait_ge(xn_ready, 2 * CHUNKS)
            for use in att_steps[-1]:
                att_use(use)
            for n in range(ATT_STEPS):
                if n < PAIRS:
                    g, slot = divmod(n, 4)
                    if slot == 0:
                        pe.wait_ge(q_ready, 2 * g + 2)
                        pe.wait_ge(k_ready, 4 * g + 4)
                    if n >= 2:
                        pe.wait_ge(s_centred, n - 1)
                    for k in range(2):
                        t = 2 * slot + k
                        last = mm(SCORE[n % 2][:, 256 * k:256 * k + 256],
                                  q_bd[:, g % 2, t, :, :].rearrange("p s i -> p (s i)"),
                                  k_bd[:, g % 2, :, GRID * t:GRID * t + GRID])
                    last.then_inc(scored, 1)
                for use in att_steps[n][:1]:
                    att_use(use)
                if 1 <= n <= PAIRS:
                    e = n - 1
                    pe.wait_ge(exped, e + 1)
                    if e >= 2:
                        pe.wait_ge(p_copied, e - 1)
                    turn(PT[e % 2], prob[:, e % 2, :, :].rearrange("p k n -> p (k n)")).then_inc(p_turned, 1)
                for use in att_steps[n][1:2]:
                    att_use(use)
                if 2 <= n <= PAIRS + 1:
                    e = n - 2
                    g, slot = divmod(e, 4)
                    pe.wait_ge(p_copied, e + 1)
                    if slot == 0:
                        pe.wait_ge(v_ready, 2 * g + 2)
                    if e >= 2:
                        pe.wait_ge(o_ready, e - 1)
                    pts = prob_t[:, e % 2, :, :].rearrange("p (t r) n -> p t r n", t=2)
                    for k in range(2):
                        for m in range(2):
                            for hp in range(2):
                                row = 64 * m + 32 * hp
                                mm(OZ[e % 2][row:row + 32, 64 * k:64 * k + 64],
                                   v_bd[:, g % 2, 2 * slot + k, row:row + 32], pts[:, k, hp, 64 * m:64 * m + 64])
                    for m in range(2):
                        for hp in range(2):
                            row = 64 * m + 32 * hp
                            last = mm(OZ[e % 2][row:row + 32, 128:256], cst("v_mask")[:, 0:32],
                                      pts[:, :, hp, 64 * m:64 * m + 64])
                    last.then_inc(av_done, 1)
                for use in att_steps[n][2:]:
                    att_use(use)

            for use in ssm_before:
                ssm_use(use)
            for m in range(SSM_STEPS):
                if m < TILES:
                    pe.wait_ge(a_masked, m + 1)
                    if m >= LAPS:
                        pe.wait_ge(dec_exped, m - LAPS + 1)
                    mm(DEC[m % LAPS][:, :], cst("later"), a_msk[:, m % LAPS, :, :].rearrange("p h t -> p (h t)"))\
                        .then_inc(decayed, 1)
                e = m - 2
                if 0 <= e < TILES:
                    k = e // 4
                    pe.wait_ge(mixed, e + 1)
                    if e % 4 == 0:
                        pe.wait_ge(dtx_ready, 2 * k + 2)
                        pe.wait_ge(x_bd_ready, 2 * k + 2)
                        pe.wait_ge(d_ident_ready, 1)
                        if k >= 2:
                            pe.wait_ge(gated, k - 1)
                    for hh in range(2):
                        at = P * (e % 4) + GRID * hh
                        for term in range(2):
                            for h4 in range(4):
                                h = 4 * hh + h4
                                xs = (dtx, x_bd)[term][:, k % 2, e % 4, h, :, :].rearrange("p s n -> p (s n)")
                                rhs = d_ident[:, h, :] if term else mix[:, e % LAPS, h, :]
                                last = mm(YT[k % 2][32 * h4:32 * h4 + 32, at:at + GRID], xs, rhs,
                                          start=term == 0, stop=term == 1)
                    last.then_inc(y_summed, 1)
                if m < TILES and m % 4 == 0:
                    k, c = m // 4, m // CT
                    if m % CT == 0:
                        pe.wait_ge(b_ready, c + 1)
                        pe.wait_ge(c_ready, c + 1)
                    if k >= 2:
                        pe.wait_ge(g_masked, k - 1)
                    for t in range(4):
                        at = GRID * ((m + t) % CT)
                        for s in range(2):
                            rows = slice(STATE * s, STATE * s + STATE)
                            last = mm(GB[k % 2][64 * s:64 * s + 64, GRID * t:GRID * t + GRID],
                                      b_s[rows, c % 2, at:at + GRID], c_s[rows, c % 2, at:at + GRID])
                    last.then_inc(g_scored, 1)
                for use in ssm_steps[m]:
                    ssm_use(use)

        def wait_ln_turned(eng, m):
            if m < CHUNKS:
                eng.wait_ge(ln_turned, m + 1)
            elif m < 2 * CHUNKS:
                filled(eng, ("ut", m - CHUNKS))
            else:
                filled(eng, ("ht", m - 2 * CHUNKS))

        def ln_shape(m):
            n = ln_tiles(m)[1] - ln_tiles(m)[0]
            return n, GRID * n

        def ln_vector_a(v, m):
            src = x_tiles(*ln_tiles(m))
            n, w = ln_shape(m)
            v.tensor_reduce(ln_s[:, m, 0:n], groups(src), AX, ALU.add).then_inc(ln_sum, 1)
            v.wait_ge(ln_sum, m + 1)
            v.tensor_scalar(ln_n[:, m, 0:n], ln_s[:, m, 0:n], -1.0 / DIM, None, ALU.mult).then_inc(ln_negmean, 1)
            v.wait_ge(ln_negmean, m + 1)
            v.tensor_tensor(groups(cen[:, m % 2, 0:w]), groups(src), deep(ln_n[:, m, 0:n], DIM), ALU.add).then_inc(ln_centred, 1)

        def ln_scalar_a(a, m):
            n, w = ln_shape(m)
            a.wait_ge(ln_centred, m + 1)
            if m >= 2:
                a.wait_ge(ln_var, m - 1)
            a.activation(sqr[:, m % 2, 0:w], cen[:, m % 2, 0:w], ACT.Square).then_inc(ln_squared, 1)

        def ln_vector_b(v, m):
            n, w = ln_shape(m)
            v.wait_ge(ln_squared, m + 1)
            v.tensor_reduce(ln_v[:, m, 0:n], groups(sqr[:, m % 2, 0:w]), AX, ALU.add).then_inc(ln_var, 1)

        def ln_scalar_b(a, m):
            n, w = ln_shape(m)
            a.wait_ge(ln_var, m + 1)
            a.activation(ln_l[:, m, 0:n], ln_v[:, m, 0:n], ACT.Ln, bias=eps_col[:, 0:1], scale=1.0 / DIM).then_inc(ln_log, 1)
            a.wait_ge(ln_log, m + 1)
            a.activation(ln_r[:, m, 0:n], ln_l[:, m, 0:n], ACT.Exp, scale=-0.5).then_inc(ln_rstd, 1)

        def ln_vector_c(v, m):
            n, w = ln_shape(m)
            v.wait_ge(ln_rstd, m + 1)
            if m >= 2:
                wait_ln_turned(v, m - 2)
            v.tensor_tensor(groups(xhat[:, m % 2, 0:w]), groups(cen[:, m % 2, 0:w]), deep(ln_r[:, m, 0:n], DIM), ALU.mult)\
                .then_inc(ln_done, 1)

        def q_sum(engine, g, m):
            rows = slice(64 * m, 64 * m + 64)
            engine.tensor_tensor(q_bd[rows, g % 2, :, m, :], rot_cos[rows, 1, :].rearrange("p (t j) -> p t j", j=GRID),
                                 rot_swap[rows, 1, :].rearrange("p (t j) -> p t j", j=GRID), ALU.add).then_inc(q_ready, 1)

        @block.vector
        def _(v):
            v.memset(eps_col[:, 0:1], LN_EPS)
            v.memset(eps_col[:, 1:2], 4 * LN_EPS)
            v.memset(eps_col[:, 2:3], 0.0).then_inc(eps_set, 1)
            for q in range(CHUNKS + 2):
                if q >= 2:
                    ln_vector_c(v, q - 2)
                if 1 <= q <= CHUNKS:
                    ln_vector_b(v, q - 1)
                if q < CHUNKS:
                    v.wait_ge(x_in[q], 64)
                    ln_vector_a(v, q)
            for d in range(2):
                v.wait_ge(bias_row, d + 1)
                v.wait_ge(w_scaled, 2 * d + 2)
                v.tensor_copy(w_att[d][64:65, :], RING[d][64:65, 0:3 * DIM]).then_inc(w_ready, 1)
            v.wait_ge(sin_signed, 2)
            v.wait_ge(consts_in, 16)
            v.wait_ge(params_in, 16)

            def late_weights():
                v.wait_ge(late_in, 16)
                v.wait_ge(cols_in, 16)
                v.tensor_tensor(w_ops[:, :], par("w_out"), par("norm_w"), ALU.mult).then_inc(out_scaled, 1)
                for k, n in enumerate(("ff", "fc1", "fc2")):
                    v.tensor_tensor(nrm_q[:, k, :], par(f"{n}_v"), par(f"{n}_v"), ALU.mult).then_inc(nrm_sq, 1)
                v.wait_ge(nrm_sq, 3)
                v.tensor_reduce(nrm_s[:, :], nrm_q[:, :, :], AX, ALU.add).then_inc(nrm_sum, 1)
                v.tensor_scalar(d_half[:, :], par("d_par"), 0.5, None, ALU.mult).then_inc(d_ready, 1)
                v.tensor_tensor(w_xdt[:, 0:INNER], par("w_xbc")[:, 0:INNER], par("tap_a")[:, 0:INNER], ALU.mult).then_inc(taps_ready, 1)
                v.tensor_copy(w_xdt[:, INNER:INNER + SSM_H], par("w_dt")).then_inc(taps_ready, 1)
                v.tensor_tensor(w_xb[:, :], par("w_xbc")[:, 0:INNER], par("tap_b")[:, 0:INNER], ALU.mult).then_inc(taps_ready, 1)
                v.tensor_tensor(w_bca[:, :], par("w_xbc")[:, INNER:], par("tap_a")[:, INNER:], ALU.mult).then_inc(taps_ready, 1)
                v.tensor_tensor(w_bcb[:, :], par("w_xbc")[:, INNER:], par("tap_b")[:, INNER:], ALU.mult).then_inc(taps_ready, 1)

            def late_scales():
                v.wait_ge(nrm_rs, 1)
                for k, n in enumerate(("ff", "fc1", "fc2")):
                    v.tensor_tensor(nrm_g[:, k:k + 1], nrm_r[:, k:k + 1], col(f"{n}_g"), ALU.mult).then_inc(nrm_ready, 1)
                v.wait_ge(a_exped, 1)
                v.tensor_scalar(a_neg[:, :], a_exp[:, :], -1.0, None, ALU.mult).then_inc(a_ready, 1)
                v.wait_ge(d_ready, 1)
                v.tensor_tensor(d_ident[:, :, :], wide(cst("ident2"), SSM_H), deep(d_half[:, :], GRID), ALU.mult)\
                    .then_inc(d_ident_ready, 1)

            def dt_slices(part):
                cols_of = slice(SSM_H * DT_PARTS[part][0], SSM_H * DT_PARTS[part][1])
                return [dt_tmp[:, k, cols_of] for k in range(5)], [dt_fin[:, k, cols_of] for k in range(2)]

            def softplus_a(part):
                T, F = dt_slices(part)
                v.wait_ge(dtv_ready, DT_PARTS[part][1] // 2)
                v.scalar_tensor_tensor(T[1], T[0], -1.0, T[0], ALU.mult, ALU.max).then_inc(dt_chain, 1)

            def softplus_b(part):
                T, F = dt_slices(part)
                v.wait_ge(dt_act, 3 * part + 1)
                v.tensor_scalar(F[1], F[0], 1.0, None, ALU.add).then_inc(dt_chain, 1)
                v.wait_ge(dt_chain, 6 * part + 2)
                v.scalar_tensor_tensor(T[3], F[1], -1.0, F[0], ALU.add, ALU.subtract).then_inc(dt_chain, 1)

            def softplus_c(part):
                T, F = dt_slices(part)
                v.wait_ge(dt_chain, 6 * part + 3)
                v.wait_ge(dt_act, 3 * part + 3)
                v.tensor_tensor(T[3], T[3], T[4], ALU.mult).then_inc(dt_chain, 1)
                v.wait_ge(dt_chain, 6 * part + 4)
                v.tensor_tensor(T[2], T[2], T[3], ALU.subtract).then_inc(dt_chain, 1)
                v.wait_ge(dt_chain, 6 * part + 5)
                v.scalar_tensor_tensor(T[1], T[0], 0.0, T[2], ALU.max, ALU.add).then_inc(dt_chain, 1)
                v.wait_ge(dt_chain, 6 * part + 6)
                v.wait_ge(a_ready, 1)
                v.tensor_tensor(F[0].rearrange("p (t h) -> p t h", h=SSM_H), T[1].rearrange("p (t h) -> p t h", h=SSM_H),
                                wide(a_neg[:, :], DT_PARTS[part][1] - DT_PARTS[part][0]), ALU.mult).then_inc(dt_ready, 1)
                v.tensor_scalar(F[1], T[1], 0.5, None, ALU.mult).then_inc(dt_ready, 1)

            def xp_use(n):
                src = filled(v, ("xp", n))[:, 0:2 * (INNER + SSM_H)].rearrange("p (t w) -> p t w", t=2)
                v.wait_ge(y_turned, CHUNKS)
                v.tensor_tensor(xv[:, 2 * n:2 * n + 2, :], src[:, :, 0:INNER], wide(par("conv_bx"), 2), ALU.add).then_inc(xv_ready, 1)
                v.tensor_tensor(dt_tmp[:, 0, 2 * SSM_H * n:2 * SSM_H * (n + 1)].rearrange("p (t h) -> p t h", t=2),
                                src[:, :, INNER:INNER + SSM_H], wide(par("dt_bias"), 2), ALU.add).then_inc(dtv_ready, 1)

            def first_sums():
                v.wait_ge(swapped, 32)
                v.wait_ge(rotated, 4)
                v.tensor_tensor(k_rot[:, :], rot_cos[:, 0, :], rot_swap[:, 0, :], ALU.add).then_inc(k_added, 1)
                v.wait_ge(q_zeroed, 1)
                q_sum(v, 0, 1)
                v.wait_ge(k_added, 1)
                h = HEADS - 1
                v.tensor_scalar(k_bd[:, 0, h, :], k_rot[:, :], cst("head_mask")[:, h:h + 1], None, ALU.mult).then_inc(k_ready, 1)

            def att_use(use):
                kind, g = use
                if kind in ("k", "q"):
                    slot = ("k", "q").index(kind)
                    src = filled(v, use)
                    if g >= 1:
                        if slot == 0:
                            v.wait_ge(k_added, g)
                            v.wait_ge(swapped, 32 * g)
                        else:
                            v.wait_ge(q_ready, 2 * g)
                    for dst, table in ((rot_cos, par("cos_" + "ji"[g // CHUNKS])), (rot_sin, sin_s[g // CHUNKS][:, :])):
                        v.tensor_tensor(dst[:, slot, :].rearrange("p (t j) -> p t j", j=GRID),
                                        src[:, :].rearrange("p (t j) -> p t j", j=GRID), wide(table), ALU.mult)\
                            .then_inc(rotated, 1)
                elif kind in ("vt0", "vt1"):
                    half = int(kind[2])
                    src = filled(v, use)
                    if half == 0 and g >= 2:
                        v.wait_ge(av_done, 4 * (g - 2) + 4)
                    v.tensor_tensor(v_bd[:, g % 2, 4 * half:4 * half + 4, :],
                                    src[:, :].rearrange("p (t n) -> p t n", n=P), wide(cst("v_mask"), 4), ALU.mult)\
                        .then_inc(v_ready, 1)
                elif kind == "xt":
                    src = filled(v, use)
                    v.wait_ge(x_halved, g + 1)
                    v.scalar_tensor_tensor(x_of(0, g), src[:, :], 0.5, flat_back[g], ALU.mult, ALU.add).then_inc(x1_ready, 1)
                    v.wait_ge(x1_ready, g + 1)
                    ln_vector_a(v, CHUNKS + g)
                elif kind == "xp":
                    xp_use(g)
                elif kind == "fold":
                    src = filled(v, use)
                    for hh in range(2):
                        for s in range(2):
                            last = v.tensor_scalar(w_ofd[:, hh, s, :], src[:, DIM * hh:DIM * hh + DIM],
                                                   cst("sp_mask")[:, s:s + 1], None, ALU.mult)
                    last.then_inc(w_out_ready, 1)

            for use in att_steps[-1]:
                if use == ("k", 1):
                    first_sums()
                att_use(use)
            for n in range(ATT_STEPS):
                if n == FOLD_STEP - 1:
                    late_weights()
                if n == FOLD_STEP + 1:
                    late_scales()
                g = (n - 8) // 4
                if (n % 4 == 0 and 0 <= g < ATT_CHUNKS - 1) or n == PAIRS + 3:
                    g = min(g, ATT_CHUNKS - 1) if n < PAIRS else ATT_CHUNKS - 1 - (n == PAIRS)
                    v.wait_ge(wo_biased, g + 1)
                    v.scalar_tensor_tensor(y_t[:, g // CHUNKS, g % CHUNKS, :], wo_e[:, :], 1.0, wo_b[:, :], ALU.min, ALU.add)\
                        .then_inc(y_ready, 1)
                if n < PAIRS:
                    v.wait_ge(scored, n + 1)
                    sc = SCORE[n % 2][:, :].rearrange("p (h j) -> p h j", j=GRID)
                    v.tensor_reduce(s_max[:, n % 2, :], sc, AX, ALU.max).then_inc(s_maxed, 1)
                    v.wait_ge(s_maxed, n + 1)
                    if n >= 2:
                        v.wait_ge(exped, n - 1)
                    v.tensor_tensor(s_cen[:, n % 2, :, :], sc, deep(s_max[:, n % 2, :], GRID), ALU.subtract)\
                        .then_inc(s_centred, 1)
                early = 1 if att_steps[n] and att_steps[n][0][0] in ("k", "q", "v") else 0
                for use in att_steps[n][:early]:
                    att_use(use)
                e = n - 3
                if 0 <= e < PAIRS:
                    g, slot = divmod(e, 4)
                    v.wait_ge(z_inverted, e + 1)
                    if slot == 0 and g >= 2:
                        filled(v, ("wo", g - 2))
                    v.tensor_tensor(o_t[:, g % 2, 2 * slot:2 * slot + 2, :].rearrange("p t j -> p (t j)"),
                                    OZ[e % 2][:, 0:128], z_inv[:, e % 2, :], ALU.mult).then_inc(o_ready, 1)
                for use in att_steps[n][early:]:
                    att_use(use)
                for q in range(CHUNKS):
                    if n == XT_STEP[q] + 1:
                        ln_vector_b(v, CHUNKS + q)
                    if n == UT_STEP[q] - 1:
                        ln_vector_c(v, CHUNKS + q)
                if n == XT_STEP[0] + 1:
                    filled(v, ("vt1", ATT_CHUNKS - 1))
                    v.wait_ge(turned_out, 32 * CHUNKS)
                    v.memset(ut_a[64:128, :, :, 0:1], 0.0).then_inc(u_starts, 1)
                    v.memset(ut_b[0:64, :, :, 0:2], 0.0).then_inc(u_starts, 1)
                    v.memset(ut_b[64:128, :, :, 0:3], 0.0).then_inc(u_starts, 1)
                if n == DT_STEP:
                    softplus_a(0)
                if n == DT_STEP + 1:
                    softplus_b(0)
                if n == DT_STEP + 2:
                    softplus_c(0)

            def z_use(use):
                hh, c = int(use[0][1]), use[1]
                src = filled(v, use)
                v.wait_ge(z_tanh, 2 * c + hh + 1)
                if c >= 2:
                    v.wait_ge(gated, 2 * (c - 2) + 2)
                v.scalar_tensor_tensor(z_s[:, c % 2, hh, :, :].rearrange("p t j -> p (t j)"), z_th[:, hh, :], 1.0, src[:, :],
                                       ALU.add, ALU.mult).then_inc(z_ready, 1)

            def bc_silu(c):
                v.wait_ge(bc_tanh, c + 1)
                if c >= 2:
                    v.wait_ge(g_scored, 2 * (c - 2) + 2)
                for dst, rows, ready in ((b_s, slice(0, 64), b_ready), (c_s, slice(64, 128), c_ready)):
                    v.scalar_tensor_tensor(dst[:, c % 2, :], b_c[rows, 1, :], 1.0, b_c[rows, 0, :], ALU.add, ALU.mult)\
                        .then_inc(ready, 1)

            def x_silu(k):
                v.wait_ge(xth_ready, k + 1)
                at = xv[:, 4 * k:4 * k + 4, :].rearrange("p t n -> p (t n)")
                v.scalar_tensor_tensor(at, xth[k % 2].rearrange("p t n -> p (t n)"), 1.0, at, ALU.add, ALU.mult)\
                    .then_inc(xs_ready, 1)

            x_silu(0)
            bc_silu(0)
            z_use(("z0", 0))
            z_use(("z1", 0))
            x_silu(1)

            for m in range(SSM_STEPS):
                e = m - 1
                if 0 <= e < TILES:
                    v.wait_ge(dec_exped, e + 1)
                    if e % 4 == 0:
                        v.wait_ge(g_masked, e // 4 + 1)
                    if e >= LAPS:
                        v.wait_ge(y_summed, e - LAPS + 1)
                    v.tensor_tensor(mix[:, e % LAPS, :, :], dec[:, e % LAPS, :, :], wide(g_m[:, e // 4 % 2, e % 4, :], SSM_H), ALU.mult)\
                        .then_inc(mixed, 1)
                k, rest = divmod(m - 6, 4)
                if m == TILES + 1 or (rest == 0 and 0 <= k < TILES // 4 - 1):
                    k = TILES // 4 - 1 if m == TILES + 1 else k
                    c = k // 2
                    v.wait_ge(y_summed, 4 * k + 4)
                    v.wait_ge(z_ready, 2 * c + 2)
                    half = 4 * (k % 2)
                    v.tensor_tensor(y_g[:, c, :, half:half + 4, :], YT[k % 2][:, :].rearrange("p (t h j) -> p h t j", t=4, h=2),
                                    z_s[:, c % 2, :, half:half + 4, :], ALU.mult).then_inc(gated, 1)
                for use in ssm_steps[m]:
                    kind, c = use
                    if kind in ("z0", "z1"):
                        z_use(use)
                    elif kind == "xp":
                        xp_use(c)
                    elif kind == "op":
                        w = in_chunk(c)
                        src = filled(v, use)[:, 0:w.stop - w.start]
                        v.wait_ge(rms_ready, c + 1)
                        v.tensor_tensor(y_n[:, w], src, rms_r[:, w], ALU.mult).then_inc(y_normed, 1)
                        v.wait_ge(y_normed, c + 1)
                        v.tensor_scalar(y_o[:, w], y_n[:, w], nrm_g[:, 0:1], col("ff_b"), ALU.mult, ALU.add).then_inc(yo_ready, 1)
                    elif kind == "yo":
                        x = x_tiles(*GROUPS[c])
                        v.tensor_tensor(x, x, filled(v, use)[:, 0:x.shape[1]], ALU.add).then_inc(z1_ready, 1)
                        v.wait_ge(z1_ready, c + 1)
                        ln_vector_a(v, 2 * CHUNKS + c)
                    elif kind == "f2":
                        w = in_chunk(c)
                        v.tensor_scalar(f_2[:, side(c), w], filled(v, use)[:, 0:w.stop - w.start], nrm_g[:, 2:3], col("fc2_b"),
                                        ALU.mult, ALU.add).then_inc(f2_ready, 1)
                    elif kind == "fo":
                        x = x_tiles(*GROUPS[c])
                        v.tensor_tensor(x, x, filled(v, use)[:, 0:x.shape[1]], ALU.add).then_inc(o_added, 1)
                if m == SOFTPLUS_STEP:
                    softplus_a(1)
                if m == SOFTPLUS_STEP + 1:
                    softplus_b(1)
                if m == SOFTPLUS_STEP + 2:
                    softplus_c(1)
                if m % CT == 3 and m // CT + 1 < CHUNKS:
                    bc_silu(m // CT + 1)
                if m % 2 == 1 and m // 2 + 2 < TILES // 4:
                    x_silu(m // 2 + 2)
                if m < TILES and m % 4 == 0:
                    k = m // 4
                    v.wait_ge(g_scored, k + 1)
                    if k >= 2:
                        v.wait_ge(mixed, 4 * (k - 2) + 4)
                    v.tensor_tensor(g_m[:, k % 2, :, :], GB[k % 2].rearrange("p (t j) -> p t j", j=GRID),
                                    wide(cst("tri_quarter"), 4), ALU.mult).then_inc(g_masked, 1)
                for o in range(len(GROUPS)):
                    if m == NORM_STEP[o] - 1:
                        ln_vector_b(v, 2 * CHUNKS + o)
                        ln_vector_c(v, 2 * CHUNKS + o)

        @block.scalar
        def _(a):
            a.preload_act_table_set("natural_log_exp_and_others")
            a.wait_ge(eps_set, 1)
            for q in range(CHUNKS + 2):
                if 1 <= q <= CHUNKS:
                    ln_scalar_b(a, q - 1)
                if q >= 2:
                    a.wait_ge(ln_turned, q - 1)
                    for m in range(2):
                        a.activation(xn_t[0:64, CT * (q - 2):CT * (q - 1), m, :],
                                     bank[2 + q][64 * m:64 * m + 64, :].rearrange("p (t j) -> p t j", j=GRID),
                                     ACT.Identity).then_inc(xn_ready, 1)
                if q < CHUNKS:
                    ln_scalar_a(a, q)
            a.wait_ge(cols_in, 16)

            def late_weights():
                a.wait_ge(late_in, 16)
                a.activation(a_exp[:, :], par("a_log"), ACT.Exp).then_inc(a_exped, 1)
                a.wait_ge(nrm_sum, 1)
                a.activation(nrm_l[:, :], nrm_s[:, :], ACT.Ln).then_inc(nrm_log, 1)
                a.wait_ge(nrm_log, 1)
                a.activation(nrm_r[:, :], nrm_l[:, :], ACT.Exp, scale=-0.5).then_inc(nrm_rs, 1)

            def att_use(use):
                kind, g = use
                if kind == "v":
                    src = filled(a, use)
                    if g >= 1:
                        filled(a, ("vt1", g - 1))
                    a.activation(v_dup[:, :, :, :], src[:, :].rearrange("p (t j) -> p t j", j=GRID).unsqueeze(2)
                                 .broadcast_to([P, CT, 2, GRID]), ACT.Identity).then_inc(v_duped, 1)
                elif kind == "wo":
                    src = filled(a, use)
                    if g >= 1:
                        a.wait_ge(y_ready, g)
                    bias = col("bo_" + "ji"[g // CHUNKS])
                    a.activation(wo_e[:, :], src[:, :], ACT.Exp, bias=bias).then_inc(wo_exped, 1)
                    a.wait_ge(wo_exped, g + 1)
                    a.activation(wo_b[:, :], src[:, :], ACT.Relu, bias=bias).then_inc(wo_biased, 1)
                elif kind == "ut":
                    src = filled(a, use)
                    a.wait_ge(turned_out, 32 * CHUNKS)
                    a.activation(u2[:, g, :], src[:, :], ACT.Identity, bias=col("ln1_b"), scale=col("ln1_w")).then_inc(u2_ready, 1)
                    a.wait_ge(u2_ready, g + 1)
                    for m in range(2):
                        a.activation(ut_a[0:64, CT * g:CT * g + CT, m, :],
                                     u2[64 * m:64 * m + 64, g, :].rearrange("p (t j) -> p t j", j=GRID), ACT.Identity)\
                            .then_inc(ut_here, 1)
                elif kind == "yt":
                    src = filled(a, use)
                    a.activation(y_tok[:, g, :], src[:, :], ACT.Identity).then_inc(y_turned, 1)

            def softplus_a(part):
                cols_of = slice(SSM_H * DT_PARTS[part][0], SSM_H * DT_PARTS[part][1])
                a.preload_act_table_set("natural_log_exp_and_others")
                a.wait_ge(dt_chain, 6 * part + 1)
                a.activation(dt_fin[:, 0, cols_of], dt_tmp[:, 1, cols_of], ACT.Exp, scale=-1.0).then_inc(dt_act, 1)

            def softplus_b(part):
                cols_of = slice(SSM_H * DT_PARTS[part][0], SSM_H * DT_PARTS[part][1])
                a.wait_ge(dt_chain, 6 * part + 2)
                a.activation(dt_tmp[:, 2, cols_of], dt_fin[:, 1, cols_of], ACT.Ln).then_inc(dt_act, 1)
                a.wait_ge(dt_act, 3 * part + 2)
                a.activation(dt_tmp[:, 4, cols_of], dt_tmp[:, 2, cols_of], ACT.Exp, scale=-1.0).then_inc(dt_act, 1)

            def expand_k(g, heads=range(HEADS)):
                a.wait_ge(k_added, g + 1)
                if g >= 2:
                    a.wait_ge(scored, 4 * (g - 2) + 4)
                for h in heads:
                    a.activation(k_bd[:, g % 2, h, :], k_rot[:, :], ACT.Identity, scale=cst("head_mask")[:, h:h + 1])\
                        .then_inc(k_ready, 1)

            a.wait_ge(consts_in, 16)
            for use in att_steps[-1]:
                att_use(use)
            expand_k(0, range(HEADS - 1))
            for n in range(ATT_STEPS):
                for use in att_steps[n][:1]:
                    att_use(use)
                e = n - 1
                if 0 <= e < PAIRS:
                    a.wait_ge(p_turned, e + 1)
                    if e >= 2:
                        a.wait_ge(av_done, e - 1)
                    a.activation(prob_t[:, e % 2, :, :].rearrange("p k n -> p (k n)"), PT[e % 2][:, :], ACT.Identity)\
                        .then_inc(p_copied, 1)
                if n < PAIRS:
                    a.wait_ge(s_centred, n + 1)
                    if n >= 2:
                        a.wait_ge(p_turned, n - 1)
                    a.activation(prob[:, n % 2, :, :].rearrange("p k n -> p (k n)"),
                                 s_cen[:, n % 2, :, :].rearrange("p h j -> p (h j)"), ACT.Exp).then_inc(exped, 1)
                for use in att_steps[n][1:]:
                    att_use(use)
                e = n - 2
                if 0 <= e < PAIRS:
                    a.wait_ge(av_done, e + 1)
                    a.activation(z_log[:, e % 2, :], OZ[e % 2][:, 128:256], ACT.Ln).then_inc(z_logged, 1)
                    a.wait_ge(z_logged, e + 1)
                    if e >= 2:
                        a.wait_ge(o_ready, e - 1)
                    a.activation(z_inv[:, e % 2, :], z_log[:, e % 2, :], ACT.Exp, scale=-1.0).then_inc(z_inverted, 1)
                g, first = n // 4 + 1, n % 4 - 1
                if 0 <= first < 2 and g < ATT_CHUNKS:
                    expand_k(g, range(2 * first, 2 * first + 2))
                if n == FOLD_STEP:
                    late_weights()
                if n == DT_STEP:
                    softplus_a(0)
                if n == DT_STEP + 1:
                    softplus_b(0)
                for q in range(CHUNKS):
                    if n == XT_STEP[q]:
                        ln_scalar_a(a, CHUNKS + q)
                    if n == XT_STEP[q] + 1:
                        ln_scalar_b(a, CHUNKS + q)

            def bc_use(c):
                src = filled(a, ("bc", c))
                if c >= 1:
                    a.wait_ge(c_ready, c)
                a.activation(b_c[:, 0, :], src[:, :], ACT.Identity, bias=col("conv_bbc")).then_inc(bc_biased, 1)
                a.wait_ge(bc_biased, c + 1)
                a.activation(b_c[:, 1, :], b_c[:, 0, :], ACT.Tanh, scale=0.5).then_inc(bc_tanh, 1)

            def z_use(use):
                hh, c = int(use[0][1]), use[1]
                src = filled(a, use)
                if c >= 1:
                    a.wait_ge(z_ready, 2 * (c - 1) + hh + 1)
                a.activation(z_th[:, hh, :], src[:, :], ACT.Tanh, scale=0.5).then_inc(z_tanh, 1)

            def x_tanh(k):
                a.wait_ge(xv_ready, 2 * k + 2)
                if k >= 2:
                    a.wait_ge(xs_ready, k - 1)
                a.activation(xth[k % 2], xv[:, 4 * k:4 * k + 4, :], ACT.Tanh, scale=0.5).then_inc(xth_ready, 1)

            def spread_x(k):
                a.wait_ge(xs_ready, k + 1)
                if k >= 2:
                    a.wait_ge(y_summed, 4 * (k - 2) + 4)
                for s in range(2):
                    rows = slice(64 * s, 64 * s + 64)
                    a.activation(x_bd[rows, k % 2, :, :, s, :].rearrange("p t h n -> p (t h) n"),
                                 xv[rows, 4 * k:4 * k + 4, :].rearrange("p t (h n) -> p (t h) n", h=SSM_H), ACT.Identity)\
                        .then_inc(x_bd_ready, 1)

            x_tanh(0)
            bc_use(0)
            z_use(("z0", 0))
            z_use(("z1", 0))
            x_tanh(1)
            a.wait_ge(ssm_zeroed, 2)
            spread_x(0)

            for m in range(SSM_STEPS):
                if m < TILES:
                    a.wait_ge(decayed, m + 1)
                    if m >= LAPS:
                        a.wait_ge(mixed, m - LAPS + 1)
                    a.activation(dec[:, m % LAPS, :, :].rearrange("p h t -> p (h t)"), DEC[m % LAPS][:, :], ACT.Exp).then_inc(dec_exped, 1)
                for use in ssm_steps[m]:
                    kind, c = use
                    if kind == "bc":
                        bc_use(c)
                    elif kind in ("z0", "z1"):
                        z_use(use)
                    elif kind == "ms":
                        if c == 0:
                            a.preload_act_table_set("natural_log_exp_and_others")
                        w = in_chunk(c)
                        src = filled(a, use)[:, 0:w.stop - w.start]
                        if c >= 1:
                            a.wait_ge(rms_ready, c)
                        a.activation(rms_l[:, w], src, ACT.Ln, bias=eps_col[:, 1:2]).then_inc(rms_logged, 1)
                        a.wait_ge(rms_logged, c + 1)
                        if c >= 1:
                            a.wait_ge(y_normed, c)
                        a.activation(rms_r[:, w], rms_l[:, w], ACT.Exp, scale=-0.5).then_inc(rms_ready, 1)
                    elif kind == "ht":
                        w = in_chunk(c)
                        a.activation(h_t[side(c)][:, w], filled(a, use)[:, 0:w.stop - w.start], ACT.Identity,
                                     bias=col("ln2_b"), scale=col("ln2_w")).then_inc(h_ready, 1)
                    elif kind == "f1":
                        w = in_chunk(c)
                        src = filled(a, use)[:, 0:w.stop - w.start]
                        a.wait_ge(nrm_ready, 3)
                        a.activation(f_1[side(c)][:, w], src, ACT.Gelu, bias=col("fc1_b"), scale=nrm_g[:, 1:2]).then_inc(f1_ready, 1)
                        if c == 1:
                            a.preload_act_table_set("natural_log_exp_and_others")
                    elif kind == "yo":
                        ln_scalar_a(a, 2 * CHUNKS + c)
                if m == 0:
                    spread_x(1)
                if m % 4 == 3 and 2 <= (m + 1) // 4 < TILES // 4:
                    spread_x((m + 1) // 4)
                if m % 2 == 0 and m // 2 + 2 < TILES // 4:
                    x_tanh(m // 2 + 2)
                if m == SOFTPLUS_STEP:
                    softplus_a(1)
                if m == SOFTPLUS_STEP + 1:
                    softplus_b(1)
                for o, (first, end) in enumerate(GROUPS):
                    if m == SQUARE_STEP[o]:
                        a.wait_ge(gated, end // 4)
                        if o >= 1:
                            filled(a, ("ms", o - 1))
                        a.activation(y_sq[:, :, in_chunk(o)],
                                     y_g[:, first // CT, :, :, :].rearrange("p h t j -> p h (t j)")[:, :, in_chunk(o)],
                                     ACT.Square).then_inc(y_squared, 1)
                    if m == NORM_STEP[o] - 1:
                        ln_scalar_b(a, 2 * CHUNKS + o)
            for o in range(CHUNKS - 2, len(GROUPS)):
                a.wait_ge(o_added, o + 1)
                store(a, o, 1)

        @block.gpsimd
        def _(gp):
            gp.memset(q_bd[:, :, :, :, :], 0.0).then_inc(q_zeroed, 1)
            gp.wait_ge(q_zeroed, 1)
            gp.memset(xn_t[64:128, :, :, :], 0.0).then_inc(xn_ones, 1)
            gp.wait_ge(xn_ones, 1)
            gp.memset(xn_t[64:65, :, :, :], 1.0).then_inc(xn_ones, 1)
            gp.wait_ge(xn_ones, 2)
            gp.wait_ge(consts_in, 16)
            gp.wait_ge(params_in, 16)
            gp.wait_ge(cols_in, 16)
            for d, n in enumerate("ji"):
                gp.tensor_scalar(w_att[d][:, 0:DIM], par(f"wqkv_{n}")[:, 0:DIM], col(f"ga_{n}"), None, ALU.mult).then_inc(w_scaled, 1)
                gp.tensor_scalar(w_att[d][:, DIM:3 * DIM], par(f"wqkv_{n}")[:, DIM:3 * DIM], col(f"gb_{n}"), None, ALU.mult)\
                    .then_inc(w_scaled, 1)
            for d, n in enumerate("ji"):
                gp.tensor_scalar(sin_s[d][:, :], par(f"sin_{n}"), cst("swap_sign"), None, ALU.mult).then_inc(sin_signed, 1)

            def rotary(g):
                gp.wait_ge(swapped, 32 * g + 32)
                gp.wait_ge(rotated, 4 * g + 4)
                if g >= 1:
                    gp.wait_ge(q_ready, 2 * g)
                    gp.wait_ge(k_ready, 4 * g)
                if g == 0:
                    q_sum(gp, 0, 0)
                    return
                gp.tensor_tensor(k_rot[:, :], rot_cos[:, 0, :], rot_swap[:, 0, :], ALU.add).then_inc(k_added, 1)
                if g >= 2:
                    gp.wait_ge(scored, 4 * (g - 2) + 4)
                gp.wait_ge(k_added, g + 1)
                q_sum(gp, g, 0)
                gp.wait_ge(q_ready, 2 * g + 1)
                q_sum(gp, g, 1)

            for g in range(ATT_CHUNKS):
                rotary(g)

            gp.wait_ge(q_ready, 2 * ATT_CHUNKS)
            for q in range(CHUNKS):
                quarter = back[:, 4 * q:4 * q + 4, :].rearrange("p u n -> p (u n)")
                gp.wait_ge(back_in[q], 64)
                gp.tensor_scalar(quarter, quarter, 0.5, -1.0, ALU.mult, ALU.add).then_inc(halved, 1)
                gp.wait_ge(halved, q + 1)
                gp.wait_ge(x_in[q], 64)
                gp.tensor_tensor(quarter, quarter, x_of(0, q), ALU.add).then_inc(x_halved, 1)

            gp.wait_ge(y_ready, ATT_CHUNKS)
            gp.memset(dtx[:, :, :, :, :, :], 0.0).then_inc(ssm_zeroed, 1)
            gp.memset(x_bd[:, :, :, :, :, :], 0.0).then_inc(ssm_zeroed, 1)
            gp.wait_ge(ssm_zeroed, 2)
            gp.wait_ge(dt_ready, 2)
            def scale_x(k, s):
                gp.wait_ge(xs_ready, k + 1)
                if k >= 2:
                    gp.wait_ge(y_summed, 4 * (k - 2) + 4)
                rows = slice(64 * s, 64 * s + 64)
                gp.tensor_tensor(dtx[rows, k % 2, :, :, s, :].rearrange("p t h n -> p (t h) n"),
                                 xv[rows, 4 * k:4 * k + 4, :].rearrange("p t (h n) -> p (t h) n", h=SSM_H),
                                 dt_fin[rows, 1, 4 * SSM_H * k:4 * SSM_H * (k + 1)].unsqueeze(2).broadcast_to([64, 4 * SSM_H, SSM_P]),
                                 ALU.mult).then_inc(dtx_ready, 1)

            before, count = ssm_zeroed, 2
            for m in range(SSM_STEPS):
                if m < TILES:
                    gp.wait_ge(before, count)
                    if m >= LAPS:
                        gp.wait_ge(decayed, m - LAPS + 1)
                    if m == DT_PARTS[1][0] - 1:
                        gp.wait_ge(dt_ready, 4)
                    gp.tensor_tensor(a_msk[:, m % LAPS, :, :], deep(dt_fin[:, 0, SSM_H * m:SSM_H * (m + 1)], GRID),
                                     wide(cst("tri"), SSM_H), ALU.mult).then_inc(a_masked, 1)
                    before, count = a_masked, m + 1
                for k, sp in {1: ((0, 0), (0, 1))}.get(m, (((m + 1) // 4, (m + 1) % 4),) if m >= 3 and (m + 1) % 4 < 2 else ()):
                    if k < TILES // 4:
                        gp.wait_ge(before, count)
                        scale_x(k, sp)
                        before, count = dtx_ready, 2 * k + sp + 1
                if m - 2 in SQUARE_STEP[0:CHUNKS - 1]:
                    c = SQUARE_STEP.index(m - 2)
                    gp.wait_ge(before, count)
                    gp.wait_ge(y_squared, c + 1)
                    gp.tensor_tensor(y_sq[:, 0, :], y_sq[:, 0, :], y_sq[:, 1, :], ALU.add).then_inc(squares_added, 1)
                    before, count = squares_added, c + 1


def constants():
    co, width = offsets(CONSTS)
    c = np.zeros((P, width), np.float32)
    row = np.arange(P)
    half, pos = row // 64, row % 64

    def put(name, value):
        c[:, co[name][0]:co[name][1]] = value

    put("ident", np.eye(P))
    put("swap_sign", np.where(row % 2 == 1, -1.0, 1.0)[:, None])
    put("head_mask", (pos[:, None] // HD) == np.arange(HEADS)[None, :])
    m = np.arange(P)
    put("v_mask", half[:, None] == (m[None, :] // HD % 2))
    t = np.arange(GRID)
    put("tri", pos[:, None] <= t[None, :])
    put("tri_quarter", 0.25 * (pos[:, None] <= t[None, :]))
    put("later", (half[:, None] == half[None, :]) & (pos[:, None] > pos[None, :]))
    put("ident2", pos[:, None] == t[None, :])
    sp = row // SSM_P % 2
    put("mean_bd", (sp[:, None] == half[None, :]) / INNER)
    put("sp_mask", sp[:, None] == np.arange(2)[None, :])
    return c


def stack(*rows):
    a = np.concatenate(rows, axis=0)
    return np.concatenate([a, np.zeros((P - a.shape[0], a.shape[1]), a.dtype)], axis=0)


def two(w):
    z = np.zeros_like(w)
    return np.concatenate([np.concatenate([w, z], 1), np.concatenate([z, w], 1)], 0)


def pack(inp):
    po, n_params = offsets(PARAMS)
    lo, n_cols = offsets(COLS)
    p = np.zeros((P, n_params), np.float32)
    c = np.zeros((P, n_cols), np.float32)
    l0 = lambda n: inp["L0_conv_" + n]
    l1 = lambda n: inp["L1_conv_" + n]

    def put(name, value):
        p[:, po[name][0]:po[name][1]] = value

    def put_col(name, value):
        c[:value.shape[0], lo[name][0]] = value

    pair = np.arange(HD) ^ 1
    for d in "ji":
        wq, wkv = l0(f"Wq_{d}"), l0(f"Wkv_{d}")
        wk, wv = wkv[:, :DIM], wkv[:, DIM:]
        put(f"wqkv_{d}", stack(np.concatenate([wq, wk, wv], 1)))
        wo = l0(f"Wo_{d}").reshape(HD, HEADS, DIM).transpose(1, 0, 2).reshape(DIM, DIM)
        put(f"wo_{d}", two(wo))
        put(f"cos_{d}", np.tile(l0(f"cos_{d}")[0].T, (2 * HEADS, 1)))
        put(f"sin_{d}", np.tile(l0(f"sin_{d}")[0].T[pair], (2 * HEADS, 1)))
        for k in ("ga", "ba", "gb", "bb"):
            put_col(f"{k}_{d}", l0(k[0] + d + k[1]))
        put_col(f"bo_{d}", np.tile(l0(f"bo_{d}"), 2))
    w = l1("in_proj_w").T
    xbc = w[:, INNER:2 * INNER + 2 * STATE]
    put("w_xbc", np.concatenate([xbc, xbc], 0))
    taps = l1("conv_w")
    put("tap_a", np.repeat(np.stack([taps[:, 3], taps[:, 2]]), DIM, axis=0))
    put("tap_b", np.repeat(np.stack([taps[:, 1], taps[:, 0]]), DIM, axis=0))
    put("w_dt", stack(w[:, 2 * INNER + 2 * STATE:]))
    wz = w[:, :INNER].reshape(DIM, 2, 4, SSM_P)
    z = np.zeros((2, DIM, 2, 4, 2, SSM_P), np.float32)
    z[0, :, :, :, 0], z[1, :, :, :, 1] = wz, wz
    put("w_z", z.reshape(P, 2 * P))
    spread = lambda a: np.repeat(a.reshape(a.shape[0], 2, 4, 1, SSM_P), 2, axis=3).reshape(a.shape[0], 2 * P)
    put("w_out", stack(spread(l1("out_proj_w"))))
    put("norm_w", np.repeat(spread(l1("ssm_norm_w")[None, :]), P, axis=0))
    put("ff_vt", stack(l1("ff_v").T))
    for n in ("fc1", "fc2"):
        put(f"{n}_vt", two(l1(f"{n}_v").T))
    for n in ("ff", "fc1", "fc2"):
        put(f"{n}_v", np.concatenate([l1(f"{n}_v")] * 2, 0))
        put_col(f"{n}_g", np.tile(l1(f"{n}_g"), 2))
        put_col(f"{n}_b", np.tile(l1(f"{n}_b"), 2))
    put("conv_bx", np.repeat(l1("conv_b")[None, :INNER], P, axis=0))
    put("dt_bias", np.repeat(l1("dt_bias")[None, :], P, axis=0))
    put("a_log", np.repeat(l1("A_log")[None, :], P, axis=0))
    put("d_par", np.repeat(l1("D_param")[None, :], P, axis=0))
    for n in ("ln1_w", "ln1_b", "ln2_w", "ln2_b"):
        put_col(n, np.tile(l1(n), 2))
    bc = l1("conv_b")[INNER:]
    put_col("conv_bbc", np.concatenate([bc[:STATE], bc[:STATE], bc[STATE:], bc[STATE:]]))
    return p, c


def kernel(**inputs):
    import concourse.bacc as bacc
    from concourse.bass_utils import run_bass_kernel_spmd

    inp = {k: np.asarray(v) for k, v in inputs.items()}
    params, cols = pack(inp)
    arrays = {"x": np.ascontiguousarray(inp["x"]), "consts": constants(), "params": params, "cols": cols}
    nc = bacc.Bacc("TRN2", target_bir_lowering=False, num_devices=1)
    aps = {n: nc.dram_tensor(n, a.shape, mybir.dt.from_np(a.dtype), kind="ExternalInput").ap() for n, a in arrays.items()}
    out = nc.dram_tensor("out", (1, GRID, GRID, DIM), F32, kind="ExternalOutput").ap()
    build(nc, out=out, **aps)
    r = run_bass_kernel_spmd(nc, [arrays], core_ids=[0])
    return r.results[0]["out"]
```
